# Optimizing a Trainium2 kernel written in Bass

```python
import numpy as np
import jax
import jax.numpy as jnp

def _softmax(x, axis=-1):
    return jax.nn.softmax(x, axis=axis)

def _gelu(x):
    return jax.nn.gelu(x, approximate=True)

def _silu(x):
    return jax.nn.silu(x)

def _sigmoid(x):
    return jax.nn.sigmoid(x)

def _layernorm(x, axis=-1, eps=1e-05):
    m = jnp.mean(x, axis=axis, keepdims=True)
    v = jnp.var(x, axis=axis, keepdims=True)
    return (x - m) / jnp.sqrt(v + eps)

def _scatter_add(tgt, idx, src, axis=0):
    return tgt.at[idx].add(src)

def _segment_sum(src, seg, n):
    return jax.ops.segment_sum(src, seg, n)
kernel_name = 'mk_conv_preact_d2_conv_nhwc768_r2_3e757d'

def setup_inputs(seed: int=0):
    np.random.seed(seed)
    _w = jnp.asarray

    def _rec_inputs():
        import jax
        import jax.numpy as jnp
        _gk = jax.random.key(seed)
        x = -0.0004039 + 1 * jax.random.normal(jax.random.fold_in(_gk, 1), (4, 32, 32, 384), jnp.float32)
        return x
    x = _rec_inputs()

    def _L0_conv_setup():
        import jax, jax.numpy as jnp
        import numpy as np
        B_, H_, W_, DM = (4, 32, 32, 384)
        DI = int(0.5 * DM)
        N = 16
        R = -(-DM // 16)
        K = 4

        def selective_scan(xs, dts, As, Bs, Cs, Dsk):
            u = jnp.moveaxis(xs, -1, 0)
            d = jnp.moveaxis(dts, -1, 0)
            Bt = jnp.moveaxis(Bs, -1, 0)
            Ct = jnp.moveaxis(Cs, -1, 0)

            def step(h, inp):
                u_t, d_t, B_t, C_t = inp
                dA = jnp.exp(d_t[..., None] * As)
                h = h * dA + (d_t * u_t)[..., None] * B_t[:, :, None, :]
                y = jnp.einsum('bkcn,bkn->bkc', h, C_t)
                return (h, y)
            h0 = jnp.zeros(u.shape[1:] + (As.shape[-1],), u.dtype)
            _, ys = jax.lax.scan(step, h0, (u, d, Bt, Ct))
            ys = jnp.moveaxis(ys, 0, -1)
            return ys + Dsk[None, :, :, None] * xs
        key = jax.random.key(seed)
        ks = jax.random.split(key, 8)
        s = lambda i, shape, sc=0.02: jax.random.normal(ks[i], shape, jnp.float32) * sc
        return dict(x=jax.random.normal(ks[0], (B_, H_, W_, DM), jnp.float32), in_proj_w=s(1, (2 * DI, DM)), conv_w=s(2, (DI, 1, 3, 3)), conv_b=jnp.zeros((DI,), jnp.float32), x_proj_w=s(3, (K, R + 2 * N, DI)), dt_projs_w=s(4, (K, DI, R)), dt_projs_b=s(5, (K, DI)), A_logs=jnp.log(jnp.tile(jnp.arange(1, N + 1, dtype=jnp.float32)[None, :], (K * DI, 1))), Ds=jnp.ones((K * DI,), jnp.float32), out_norm_g=jnp.ones((DI,), jnp.float32), out_norm_b=jnp.zeros((DI,), jnp.float32), out_proj_w=s(6, (DM, DI)))
    _L0_conv_all = _L0_conv_setup()
    _L0_conv_in = {k: v for k, v in _L0_conv_all.items() if k in ('in_proj_w', 'conv_w', 'conv_b', 'x_proj_w', 'dt_projs_w', 'dt_projs_b', 'A_logs', 'Ds', 'out_norm_g', 'out_norm_b', 'out_proj_w')}
    del _L0_conv_all

    def _L1_conv_setup():
        import jax, jax.numpy as jnp
        import numpy as np
        B, H, W, C = (32, 32, 32, 384)
        E = 4
        TOPK = 2
        HD = int(C * 0.25)
        key = jax.random.key(seed)
        ks = jax.random.split(key, 7)
        x = jax.random.normal(ks[0], (B, H, W, C), dtype=jnp.float32)
        router_w = jax.random.normal(ks[1], (E, C), dtype=jnp.float32) * 0.02
        router_b = jnp.zeros((E,), dtype=jnp.float32)
        fc1_w = jax.random.normal(ks[2], (E, HD, C), dtype=jnp.float32) * (1.0 / np.sqrt(C))
        fc1_b = jax.random.normal(ks[3], (E, HD), dtype=jnp.float32) * 0.01
        fc2_w = jax.random.normal(ks[4], (E, C, HD), dtype=jnp.float32) * (1.0 / np.sqrt(HD))
        fc2_b = jax.random.normal(ks[5], (E, C), dtype=jnp.float32) * 0.01
        return {'x': x, 'router_w': router_w, 'router_b': router_b, 'fc1_w': fc1_w, 'fc1_b': fc1_b, 'fc2_w': fc2_w, 'fc2_b': fc2_b}
    _L1_conv_all = _L1_conv_setup()
    _L1_conv_in = {k: v for k, v in _L1_conv_all.items() if k in ('router_w', 'router_b', 'fc1_w', 'fc1_b', 'fc2_w', 'fc2_b')}
    del _L1_conv_all
    return {'x': x, 'L0_conv_in_proj_w': _L0_conv_in['in_proj_w'], 'L0_conv_conv_w': _L0_conv_in['conv_w'], 'L0_conv_conv_b': _L0_conv_in['conv_b'], 'L0_conv_x_proj_w': _L0_conv_in['x_proj_w'], 'L0_conv_dt_projs_w': _L0_conv_in['dt_projs_w'], 'L0_conv_dt_projs_b': _L0_conv_in['dt_projs_b'], 'L0_conv_A_logs': _L0_conv_in['A_logs'], 'L0_conv_Ds': _L0_conv_in['Ds'], 'L0_conv_out_norm_g': _L0_conv_in['out_norm_g'], 'L0_conv_out_norm_b': _L0_conv_in['out_norm_b'], 'L0_conv_out_proj_w': _L0_conv_in['out_proj_w'], 'L1_conv_router_w': _L1_conv_in['router_w'], 'L1_conv_router_b': _L1_conv_in['router_b'], 'L1_conv_fc1_w': _L1_conv_in['fc1_w'], 'L1_conv_fc1_b': _L1_conv_in['fc1_b'], 'L1_conv_fc2_w': _L1_conv_in['fc2_w'], 'L1_conv_fc2_b': _L1_conv_in['fc2_b']}

def reference(x, L0_conv_in_proj_w, L0_conv_conv_w, L0_conv_conv_b, L0_conv_x_proj_w, L0_conv_dt_projs_w, L0_conv_dt_projs_b, L0_conv_A_logs, L0_conv_Ds, L0_conv_out_norm_g, L0_conv_out_norm_b, L0_conv_out_proj_w, L1_conv_router_w, L1_conv_router_b, L1_conv_fc1_w, L1_conv_fc1_b, L1_conv_fc2_w, L1_conv_fc2_b):
    import jax
    import jax.numpy as jnp

    def _L0_conv_ref(x, in_proj_w, conv_w, conv_b, x_proj_w, dt_projs_w, dt_projs_b, A_logs, Ds, out_norm_g, out_norm_b, out_proj_w):
        import jax, jax.numpy as jnp
        import numpy as np
        B_, H_, W_, DM = (4, 32, 32, 384)
        DI = int(0.5 * DM)
        N = 16
        R = -(-DM // 16)
        K = 4

        def selective_scan(xs, dts, As, Bs, Cs, Dsk):
            u = jnp.moveaxis(xs, -1, 0)
            d = jnp.moveaxis(dts, -1, 0)
            Bt = jnp.moveaxis(Bs, -1, 0)
            Ct = jnp.moveaxis(Cs, -1, 0)

            def step(h, inp):
                u_t, d_t, B_t, C_t = inp
                dA = jnp.exp(d_t[..., None] * As)
                h = h * dA + (d_t * u_t)[..., None] * B_t[:, :, None, :]
                y = jnp.einsum('bkcn,bkn->bkc', h, C_t)
                return (h, y)
            h0 = jnp.zeros(u.shape[1:] + (As.shape[-1],), u.dtype)
            _, ys = jax.lax.scan(step, h0, (u, d, Bt, Ct))
            ys = jnp.moveaxis(ys, 0, -1)
            return ys + Dsk[None, :, :, None] * xs
        B, H, W, _ = x.shape
        L = H * W
        xz = x @ in_proj_w.T
        xh, z = jnp.split(xz, 2, axis=-1)
        xc = jnp.transpose(xh, (0, 3, 1, 2))
        xc = jax.lax.conv_general_dilated(xc, conv_w, (1, 1), 'SAME', feature_group_count=DI)
        xc = jax.nn.silu(xc + conv_b[None, :, None, None])
        x_flat = xc.reshape(B, DI, L)
        x_t = jnp.transpose(xc, (0, 1, 3, 2)).reshape(B, DI, L)
        x_hwwh = jnp.stack([x_flat, x_t], 1)
        xs = jnp.concatenate([x_hwwh, jnp.flip(x_hwwh, -1)], 1)
        x_dbl = jnp.einsum('bkdl,kcd->bkcl', xs, x_proj_w)
        dts, Bs, Cs = jnp.split(x_dbl, [R, R + N], axis=2)
        dts = jnp.einsum('bkrl,kdr->bkdl', dts, dt_projs_w)
        dts = jax.nn.softplus(dts + dt_projs_b[None, :, :, None])
        As = -jnp.exp(A_logs).reshape(K, DI, N)
        out_y = selective_scan(xs, dts, As, Bs, Cs, Ds.reshape(K, DI))
        inv_y = jnp.flip(out_y[:, 2:4], -1)
        wh_y = jnp.transpose(out_y[:, 1].reshape(B, DI, W, H), (0, 1, 3, 2)).reshape(B, DI, L)
        invwh_y = jnp.transpose(inv_y[:, 1].reshape(B, DI, W, H), (0, 1, 3, 2)).reshape(B, DI, L)
        y = out_y[:, 0] + inv_y[:, 0] + wh_y + invwh_y
        y = jnp.transpose(y, (0, 2, 1)).reshape(B, H, W, DI)
        mu = y.mean(-1, keepdims=True)
        var = y.var(-1, keepdims=True)
        y = (y - mu) / jnp.sqrt(var + 1e-05) * out_norm_g + out_norm_b
        y = y * jax.nn.silu(z)
        return y @ out_proj_w.T

    def _L1_conv_ref(x, router_w, router_b, fc1_w, fc1_b, fc2_w, fc2_b):
        import jax, jax.numpy as jnp
        import numpy as np
        B, H, W, C = (32, 32, 32, 384)
        E = 4
        TOPK = 2
        HD = int(C * 0.25)
        b, h, w, c = x.shape
        xt = x.reshape(b, h * w, c)
        logits = jnp.einsum('bsc,ec->bse', xt, router_w) + router_b
        probs = jax.nn.softmax(logits, axis=-1)
        topk_w, topk_idx = jax.lax.top_k(probs, TOPK)
        topk_w = topk_w / (jnp.sum(topk_w, axis=-1, keepdims=True) + 1e-08)
        combine = jnp.sum(jax.nn.one_hot(topk_idx, E, dtype=xt.dtype) * topk_w[..., None], axis=-2)
        hmid = jax.nn.gelu(jnp.einsum('bsc,ehc->bseh', xt, fc1_w) + fc1_b, approximate=False)
        hw = hmid * combine[..., None]
        out = jnp.einsum('bseh,ech->bsc', hw, fc2_w)
        out = out + jnp.einsum('bse,ec->bsc', combine, fc2_b)
        return out.reshape(b, h, w, c)

    def _gn(v, G=32, eps=1e-05):
        B_, H_, W_, C_ = v.shape
        g = v.reshape(B_, H_, W_, G, C_ // G)
        m = jnp.mean(g, axis=(1, 2, 4), keepdims=True)
        s = jnp.var(g, axis=(1, 2, 4), keepdims=True)
        return ((g - m) / jnp.sqrt(s + eps)).reshape(v.shape)

    def _ln_c(v, eps=1e-06):
        m = jnp.mean(v, axis=-1, keepdims=True)
        s = jnp.var(v, axis=-1, keepdims=True)
        return (v - m) / jnp.sqrt(s + eps)

    def _ln_t(v, eps=1e-05):
        m = jnp.mean(v, axis=-1, keepdims=True)
        s = jnp.var(v, axis=-1, keepdims=True)
        return (v - m) / jnp.sqrt(s + eps)

    def _to_tokens(v):
        B_, H_, W_, C_ = v.shape
        return v.reshape(B_, H_ * W_, C_)

    def _from_tokens(t, like):
        return t.reshape(like.shape)
    x = x + _L0_conv_ref(_gn(x), L0_conv_in_proj_w, L0_conv_conv_w, L0_conv_conv_b, L0_conv_x_proj_w, L0_conv_dt_projs_w, L0_conv_dt_projs_b, L0_conv_A_logs, L0_conv_Ds, L0_conv_out_norm_g, L0_conv_out_norm_b, L0_conv_out_proj_w)
    x = x + _L1_conv_ref(_gn(x), L1_conv_router_w, L1_conv_router_b, L1_conv_fc1_w, L1_conv_fc1_b, L1_conv_fc2_w, L1_conv_fc2_b)
    return x

_drawn_inputs = setup_inputs


def setup_inputs(seed=0):
    import zlib

    import numpy as np

    out = dict(_drawn_inputs(seed))
    spreads = {'L0_conv_conv_b': (0.0, 0.1),
     'L0_conv_Ds': (1.0, 0.6),
     'L0_conv_out_norm_g': (1.0, 0.2),
     'L0_conv_out_norm_b': (0.0, 0.314),
     'L1_conv_router_b': (0.0, 0.1)}
    factors = {'L0_conv_x_proj_w': 64.0,
     'L0_conv_dt_projs_w': 64.0,
     'L0_conv_dt_projs_b': 64.0,
     'L0_conv_A_logs': 64.0,
     'L1_conv_fc1_b': 8.0,
     'L1_conv_fc2_b': 8.0}
    for name, (base, spread) in spreads.items():
        noise = np.random.default_rng([zlib.crc32(name.encode()), seed]).standard_normal(out[name].shape)
        drawn = base * np.exp(spread * noise) if base else spread * noise
        out[name] = jnp.asarray(drawn.astype(out[name].dtype))
    for name, factor in factors.items():
        out[name] = (out[name] * factor).astype(out[name].dtype)
    return out
```

```python
from contextlib import ExitStack

import concourse.bass as bass
from concourse import mybir

F32 = mybir.dt.float32
BF16 = mybir.dt.bfloat16
ALU = mybir.AluOpType
ACT = mybir.ActivationFunctionType
AX_X = mybir.AxisListType.X

P = 128
BATCH = 4
HW = 32
L = HW * HW
C = 384
NC = C // P
DI = 192
HALF = DI - P
N = 16
R = 24
DIRS = 4
KIND = 3
PAIRS = BATCH // 2
TT = L // P
PAD = HW + 2
EXPERTS = 4
HID = 96
BANK = 512
PIECES = 3
PR = 32
UNIT = N
GROUP = 2 * UNIT
GROUPS = PAIRS * 2 * KIND
LN2 = 0.693147
LOG_MAX = 80.0


def need(eng, semaphore, value):
    if isinstance(value, int) and value <= 0:
        return
    eng.wait_ge(semaphore, value)


def halves():
    return [slice(q * BANK, (q + 1) * BANK) for q in range(L // BANK)]


def head(nc, d):
    with ExitStack() as ctx:
        def sb(name, shape, dt=F32):
            return ctx.enter_context(nc.sbuf_tensor("h_" + name, shape, dt))

        def sem(name):
            return ctx.enter_context(nc.semaphore("h_" + name))

        eye = sb("eye", [P, P])
        win = sb("win", [P, NC, C])
        wx = sb("wx", [P, DIRS * KIND, P])
        gavg = sb("gavg", [P, NC * NC, P])
        conv_p = sb("conv_p", [P, KIND, 10])
        xin = sb("xin", [P, 2, TT, C])
        xt = sb("xt", [P, 2, NC, L])
        xn = sb("xn", [P, 2, NC, L])
        xpad = sb("xpad", [P, KIND, PAD, PAD])
        acc = sb("acc", [P, KIND, L])
        xc = sb("xc", [P, KIND, L])
        xct = sb("xct", [P, KIND, L])
        zt = sb("zt", [P, TT, 2 * DI])
        hi = sb("hi", [2 * PR, 2, L], BF16)
        mid = sb("mid", [2 * PR, 2, L], BF16)
        lo = sb("lo", [2 * PR, 2, L], BF16)
        rest = sb("rest", [2 * PR, L])
        dts = sb("dts", [P, 2, L])
        st = sb("st", [P, NC, 2, 6])
        mv = sb("mv", [P, BATCH, NC, 2])
        gmean = sb("gmean", [P, BATCH, NC])
        dev = sb("dev", [P, BATCH, NC])
        chan_var = sb("chan_var", [P, BATCH, NC])
        rstd = sb("rstd", [P, BATCH, NC])
        std = sb("std", [P, BATCH, NC])
        eps = sb("eps", [P, 1])
        big = [ctx.enter_context(nc.psum_tensor(f"h_big{i}", [P, L], F32)) for i in range(2)]
        pz = [ctx.enter_context(nc.psum_tensor(f"h_pz{i}", [P, BANK], F32)) for i in range(2)]
        pst = ctx.enter_context(nc.psum_tensor("h_pst", [P, BANK], F32))

        weights_in = sem("weights_in")
        x_in = [sem(f"x_in{b}") for b in range(BATCH)]
        xt_out = [sem(f"xt_out{b}") for b in range(BATCH)]
        borders = sem("borders")
        turned = sem("turned")
        xt_ready = sem("xt_ready")
        stats = sem("stats")
        sums = sem("sums")
        std_ready = sem("std_ready")
        xn_ready = sem("xn_ready")
        xh_done = sem("xh_done")
        xpad_ready = sem("xpad_ready")
        z_done = sem("z_done")
        z_ready = sem("z_ready")
        z_out = sem("z_out")
        conv_step = sem("conv_step")
        xc_ready = sem("xc_ready")
        xct_ready = sem("xct_ready")
        u_out = sem("u_out")
        xd_done = sem("xd_done")
        hi_ready = sem("hi_ready")
        rest_ready = sem("rest_ready")
        mid_ready = sem("mid_ready")
        lo_ready = sem("lo_ready")
        bc_out = [sem(f"bc_out{i}") for i in range(2)]
        block = ctx.enter_context(nc.Block())

        def xd(pair, k):
            return pair * DIRS + k

        @block.sync
        def _(sp):
            for t, src in ((eye, d["eye"]), (win, d["win"]), (gavg, d["gavg"]), (wx, d["wx"]), (conv_p, d["conv_p"])):
                sp.dma_start(t[:], src).then_inc(weights_in, 16)
            for b in range(BATCH):
                if b >= 2:
                    sp.wait_ge(turned, NC * (b - 1))
                sp.dma_start(xin[:, b % 2], d["x"][b].rearrange("(t p) c -> p t c", p=P)).then_inc(x_in[b], 16)
            for pair in range(PAIRS):
                for b in (2 * pair, 2 * pair + 1):
                    sp.wait_ge(xt_ready, NC * (b + 1))
                    sp.dma_start(d["xt"][b].rearrange("c p l -> p c l"), xt[:, b % 2]).then_inc(xt_out[b], 16)
                sp.wait_ge(z_ready, TT * (pair + 1))
                sp.dma_start(d["sz"][pair], zt[:]).then_inc(z_out, 16)
                sp.wait_ge(xc_ready, KIND * (pair + 1))
                sp.dma_start(d["u"][pair, 0].rearrange("t p l -> p t l"), xc[:]).then_inc(u_out, 16)
                sp.wait_ge(xct_ready, KIND * (pair + 1))
                sp.dma_start(d["u"][pair, 1].rearrange("t p l -> p t l"), xct[:]).then_inc(u_out, 16)
                for k in range(DIRS):
                    i = xd(pair, k)
                    sp.wait_ge(lo_ready, i + 1)
                    for piece, t in enumerate((hi, mid, lo)):
                        for m in range(2):
                            sp.dma_start(d["bc"][pair, k, m, piece * PR:(piece + 1) * PR], t[m * PR:(m + 1) * PR, i % 2])\
                              .then_inc(bc_out[i % 2], 16)
                    sp.dma_start(d["dts"][pair, k], dts[2 * PR:P, i % 2]).then_inc(bc_out[i % 2], 16)
            for b in range(BATCH):
                sp.wait_ge(xt_out[b], 16)
            sp.wait_ge(z_out, 16 * PAIRS)
            sp.wait_ge(u_out, 32 * PAIRS)
            for i in range(2):
                sp.wait_ge(bc_out[i], 16 * 7 * PAIRS * DIRS // 2)

        @block.tensor
        def _(pe):
            pe.wait_ge(weights_in, 16 * 5)

            def transposes(pair):
                for b in (2 * pair, 2 * pair + 1):
                    pe.wait_ge(x_in[b], 16)
                    for c in range(NC):
                        i = b * NC + c
                        if b % 2 == 0 and c < 2:
                            if pair:
                                pe.wait_ge(xpad_ready, KIND * pair)
                        else:
                            pe.wait_ge(xt_ready, i - 1)
                        for t in range(TT):
                            mm = pe.transpose(big[i % 2][:, t * P:(t + 1) * P], xin[:, b % 2, t, c * P:(c + 1) * P], eye[:])
                        mm.then_inc(turned, 1)

            def group_stats(pair):
                for b in (2 * pair, 2 * pair + 1):
                    for step, src in ((0, mv), (1, chan_var)):
                        pe.wait_ge(stats, 2 * b + step + 1)
                        for co in range(NC):
                            for ci in range(NC):
                                rhs = mv[:, b, ci, 0:1] if step == 0 else chan_var[:, b, ci:ci + 1]
                                col = (b * 2 + step) * NC + co
                                mm = pe.matmul(pst[:, col:col + 1], gavg[:, ci * NC + co], rhs,
                                               start=(ci == 0), stop=(ci == NC - 1))
                        mm.then_inc(sums, 1)

            def in_proj(pair):
                pe.wait_ge(xn_ready, 2 * (pair + 1))
                pe.wait_ge(xt_ready, NC * 2 * (pair + 1))
                if pair:
                    pe.wait_ge(rest_ready, DIRS * pair)
                for kind in range(KIND):
                    i = pair * KIND + kind
                    buf = big[kind % 2]
                    if kind == 2:
                        pe.wait_ge(xpad_ready, i - 1)
                    for q in halves():
                        if kind < 2:
                            for c in range(NC):
                                mm = pe.matmul(buf[:, q], win[:, c, 0:P], xn[:, kind, c, q], start=(c == 0), stop=(c == NC - 1))
                        else:
                            for b in range(2):
                                for c in range(NC):
                                    mm = pe.matmul(buf[b * HALF:(b + 1) * HALF, q], win[:, c, P:DI], xn[:, b, c, q],
                                                   start=(c == 0), stop=(c == NC - 1))
                    mm.then_inc(xh_done, 1)
                for t in range(TT):
                    i = pair * TT + t
                    need(pe, z_ready, i - 1)
                    for b in range(2):
                        for c in range(NC):
                            mm = pe.matmul(pz[i % 2][:, b * DI:(b + 1) * DI], xn[:, b, c, t * P:(t + 1) * P], win[:, c, DI:C],
                                           start=(c == 0), stop=(c == NC - 1))
                    mm.then_inc(z_done, 1)

            def x_proj(pair):
                for k in range(DIRS):
                    i = xd(pair, k)
                    src = xct if k % 2 else xc
                    need(pe, xct_ready if k % 2 else xc_ready, KIND * (pair + 1))
                    if k < 2:
                        pe.wait_ge(xt_ready, NC * 2 * min(pair + 2, PAIRS))
                        pe.wait_ge(xpad_ready, KIND * (pair + 1))
                    else:
                        pe.wait_ge(rest_ready, i - 1)
                    for q in halves():
                        for t in range(KIND):
                            mm = pe.matmul(big[k % 2][:, q], wx[:, k * KIND + t], src[:, t, q], start=(t == 0), stop=(t == KIND - 1))
                    mm.then_inc(xd_done, 1)

            transposes(0)
            group_stats(0)
            in_proj(0)
            transposes(1)
            group_stats(1)
            x_proj(0)
            in_proj(1)
            x_proj(1)

        @block.scalar
        def _(act):
            def copy_xt(pair):
                for b in (2 * pair, 2 * pair + 1):
                    for c in range(NC):
                        i = b * NC + c
                        act.wait_ge(turned, i + 1)
                        if b >= 2:
                            act.wait_ge(xt_out[b - 2], 16)
                            act.wait_ge(xn_ready, b - 1)
                        nc.scalar.copy(xt[:, b % 2, c], big[i % 2][:]).then_inc(xt_ready, 1)

            def root(pair):
                for b in (2 * pair, 2 * pair + 1):
                    act.wait_ge(sums, 2 * b + 2)
                    nc.scalar.activation(std[:, b], pst[:, (b * 2 + 1) * NC:(b * 2 + 2) * NC], ACT.Sqrt,
                                         bias=eps[:]).then_inc(std_ready, 1)

            def fill_xpad(pair):
                act.wait_ge(borders, 1)
                for kind in range(KIND):
                    act.wait_ge(xh_done, pair * KIND + kind + 1)
                    need(act, conv_step, pair * KIND * 9)
                    nc.scalar.copy(xpad[:, kind, 1:HW + 1, 1:HW + 1], big[kind % 2][:].rearrange("p (h w) -> p h w", h=HW))\
                      .then_inc(xpad_ready, 1)

            def silu_z(pair):
                for t in range(TT):
                    i = pair * TT + t
                    act.wait_ge(z_done, i + 1)
                    need(act, z_out, 16 * pair)
                    nc.scalar.activation(zt[:, t], pz[i % 2][:, 0:2 * DI], ACT.Silu).then_inc(z_ready, 1)

            def silu_conv(pair):
                for kind in range(KIND):
                    act.wait_ge(conv_step, (pair * KIND + kind + 1) * 9)
                    need(act, u_out, 32 * pair)
                    need(act, xct_ready, KIND * pair)
                    need(act, xd_done, DIRS * pair)
                    nc.scalar.activation(xc[:, kind], acc[:, kind], ACT.Silu, bias=conv_p[:, kind, 9:10]).then_inc(xc_ready, 1)

            def split(pair):
                for k in range(DIRS):
                    i = xd(pair, k)
                    src = big[k % 2]
                    act.wait_ge(xd_done, i + 1)
                    need(act, bc_out[i % 2], 16 * 7 * (i // 2))
                    nc.scalar.copy(dts[2 * PR:P, i % 2], src[2 * PR:P, :])
                    nc.scalar.copy(hi[:, i % 2], src[0:2 * PR, :]).then_inc(hi_ready, 1)
                    act.wait_ge(rest_ready, i + 1)
                    nc.scalar.copy(mid[:, i % 2], rest[:]).then_inc(mid_ready, 1)

            act.wait_ge(weights_in, 16 * 5)
            copy_xt(0)
            root(0)
            fill_xpad(0)
            silu_z(0)
            copy_xt(1)
            silu_conv(0)
            root(1)
            split(0)
            fill_xpad(1)
            silu_z(1)
            silu_conv(1)
            split(1)

        @block.vector
        def _(dve):
            chain = ctx.enter_context(nc.semaphore("h_chain"))
            links = [0]

            def link(ins):
                links[0] += 1
                ins.then_inc(chain, 1)
                dve.wait_ge(chain, links[0])

            link(nc.vector.memset(eps[:], 1e-5))

            def normalise(pair):
                for b in (2 * pair, 2 * pair + 1):
                    for c in range(NC):
                        dve.wait_ge(xt_ready, b * NC + c + 1)
                        for h, q in enumerate(halves()):
                            last = nc.vector.bn_stats(st[:, c, h], xt[:, b % 2, c, q])
                        link(last)
                        last = nc.vector.bn_aggr(mv[:, b, c], st[:, c].rearrange("p a s -> p (a s)"))
                    last.then_inc(stats, 1)
                    dve.wait_ge(stats, 2 * b + 1)
                    dve.wait_ge(sums, 2 * b + 1)
                    link(nc.vector.tensor_copy(gmean[:, b], pst[:, b * 2 * NC:(b * 2 + 1) * NC]))
                    link(nc.vector.tensor_tensor(dev[:, b], mv[:, b, :, 0], gmean[:, b], ALU.subtract))
                    link(nc.vector.tensor_tensor(dev[:, b], dev[:, b], dev[:, b], ALU.mult))
                    nc.vector.tensor_tensor(chan_var[:, b], mv[:, b, :, 1], dev[:, b], ALU.add).then_inc(stats, 1)
                    dve.wait_ge(std_ready, b + 1)
                    link(nc.vector.reciprocal(rstd[:, b], std[:, b]))
                    need(dve, z_done, TT * pair)
                    for c in range(NC):
                        last = nc.vector.tensor_scalar(xn[:, b % 2, c], xt[:, b % 2, c], gmean[:, b, c:c + 1],
                                                       rstd[:, b, c:c + 1], ALU.subtract, ALU.mult)
                    last.then_inc(xn_ready, 1)

            def convolve(pair):
                for kind in range(KIND):
                    dve.wait_ge(xpad_ready, pair * KIND + kind + 1)
                    need(dve, xc_ready, KIND * pair)
                    out = acc[:, kind].rearrange("p (h w) -> p h w", h=HW)
                    for tap in range(9):
                        view = xpad[:, kind, tap // 3:tap // 3 + HW, tap % 3:tap % 3 + HW]
                        w = conv_p[:, kind, tap:tap + 1]
                        at = (pair * KIND + kind) * 9 + tap
                        if tap == 0:
                            nc.vector.tensor_scalar(out, view, w, None, ALU.mult).then_inc(conv_step, 1)
                        else:
                            dve.wait_ge(conv_step, at)
                            nc.vector.scalar_tensor_tensor(out, view, w, out, ALU.mult, ALU.add).then_inc(conv_step, 1)

            def split(pair):
                for k in range(DIRS):
                    i = xd(pair, k)
                    dve.wait_ge(hi_ready, i + 1)
                    need(dve, lo_ready, i)
                    nc.vector.tensor_tensor(rest[:], big[k % 2][0:2 * PR, :], hi[:, i % 2], ALU.subtract).then_inc(rest_ready, 1)
                    dve.wait_ge(mid_ready, i + 1)
                    nc.vector.tensor_tensor(lo[:, i % 2], rest[:], mid[:, i % 2], ALU.subtract).then_inc(lo_ready, 1)

            dve.wait_ge(weights_in, 16 * 5)
            normalise(0)
            convolve(0)
            normalise(1)
            split(0)
            convolve(1)
            split(1)

        @block.gpsimd
        def _(pool):
            nc.gpsimd.memset(xpad[:], 0.0).then_inc(borders, 1)
            for pair in range(PAIRS):
                for kind in range(KIND):
                    pool.wait_ge(xc_ready, pair * KIND + kind + 1)
                    need(pool, u_out, 32 * pair)
                    need(pool, xd_done, DIRS * pair)
                    nc.gpsimd.tensor_copy(xct[:, kind].rearrange("p (w h) -> p h w", w=HW),
                                          xc[:, kind].rearrange("p (h w) -> p h w", h=HW)).then_inc(xct_ready, 1)


def scan(nc, d):
    with ExitStack() as ctx:
        def sb(name, shape, dt=F32):
            return ctx.enter_context(nc.sbuf_tensor("s_" + name, shape, dt))

        def sem(name):
            return ctx.enter_context(nc.semaphore("s_" + name))

        eye = sb("eye", [P, P])
        bc = sb("bc", [PIECES * PR, 2, 2, L], BF16)
        pick = sb("pick", [PIECES * PR, 2, N * P], BF16)
        dtr = sb("dtr", [2 * PR, 2, L])
        wdt = sb("wdt", [2 * PR, 2, P])
        par = sb("par", [P, 2, N + 3])
        u = sb("u", [P, 2, L])
        amin = sb("amin", [P, 2, N])
        aexp = sb("aexp", [P, 2, N])
        aneg = sb("aneg", [P, 2, N])
        dt_ = sb("dt", [P, 2, L])
        dtu = sb("dtu", [P, 2, L])
        ez = sb("ez", [P, L])
        rz = sb("rz", [P, L])
        lz = sb("lz", [P, L])
        qz = sb("qz", [P, L])
        a = sb("a", [P, 2, L])
        h = sb("h", [P, 2, L])
        hc = sb("hc", [P, 2, L])
        crow = sb("crow", [P, 2, L])
        dsum = sb("dsum", [P, 1])
        yout = sb("yout", [P, L])
        pb = ctx.enter_context(nc.psum_tensor("s_pb", [P, 2, L], F32))
        pc = ctx.enter_context(nc.psum_tensor("s_pc", [P, L], F32))
        py = ctx.enter_context(nc.psum_tensor("s_py", [P, L], F32))

        eye_in = sem("eye_in")
        loads = [sem(f"loads{i}") for i in range(2)]
        NLOADS = 6
        b_row = sem("b_row")
        c_row = sem("c_row")
        crow_ready = sem("crow_ready")
        a_ready = sem("a_ready")
        b_ready = sem("b_ready")
        h_ready = sem("h_ready")
        hc_ready = sem("hc_ready")
        y_added = sem("y_added")
        y_taken = sem("y_taken")
        y_stored = sem("y_stored")
        z_done = sem("z_done")
        z_taken = sem("z_taken")
        e_ready = sem("e_ready")
        l_ready = sem("l_ready")
        q_ready = sem("q_ready")
        s_ready = sem("s_ready")
        s2_ready = sem("s2_ready")
        s3_ready = sem("s3_ready")
        dt_ready = sem("dt_ready")
        dtu_ready = sem("dtu_ready")
        amin_ready = sem("amin_ready")
        aexp_ready = sem("aexp_ready")
        a_neg_ready = sem("a_neg_ready")
        dsum_ready = sem("dsum_ready")
        block = ctx.enter_context(nc.Block())

        def groups(eng, body):
            body(0, False)
            with eng.Fori(1, GROUPS - 1) as g:
                body(g, False)
            body(GROUPS - 1, True)

        def flow(s):
            return slice(None, None, -1) if s else slice(None)

        @block.sync
        def _(sp):
            sp.dma_start(eye[:], d["eye"]).then_inc(eye_in, 16)

            def load(unit, s, pair, orient, kind):
                k = orient + 2 * s
                for dst, src in (
                    (bc[:, s, 0], d["bc_flat"][bass.ds((pair * DIRS + k) * 2, 1)]),
                    (bc[:, s, 1], d["bc_flat"][bass.ds((pair * DIRS + k) * 2 + 1, 1)]),
                    (pick[:, s], d["pick"][bass.ds(kind, 1)]),
                    (dtr[:, s], d["dts_flat"][bass.ds(pair * DIRS + k, 1)]),
                    (wdt[:, s], d["wdt"][bass.ds(k * KIND + kind, 1)]),
                    (par[:, s], d["par"][bass.ds(k * KIND + kind, 1)]),
                    (u[:, s], d["u_flat"][bass.ds((pair * 2 + orient) * KIND + kind, 1)]),
                ):
                    sp.dma_start(dst, src.rearrange("a p l -> p (a l)")).then_inc(loads[s], 16)

            def both(pair, orient, kind, g):
                for s in range(2):
                    need(sp, h_ready, (g - 1) * GROUP + (s + 1) * UNIT)
                    need(sp, c_row, (g - 1) * GROUP + (s + 1) * UNIT)
                    if s == 1:
                        need(sp, y_taken, g)
                    load(None, s, pair, orient, kind)
                    if s == 0:
                        pass

            for s in range(2):
                load(None, s, 0, 0, 0)
            with sp.Fori(1, GROUPS) as g:
                for s in range(2):
                    sp.wait_ge(h_ready, g * GROUP - GROUP + (s + 1) * UNIT)
                    sp.wait_ge(c_row, g * GROUP - GROUP + (s + 1) * UNIT)
                    if s == 1:
                        sp.wait_ge(y_taken, g)
                        sp.dma_start(d["y_flat"][bass.ds(g - 1, 1)].rearrange("a p l -> p (a l)"), yout[:]).then_inc(y_stored, 16)
                    po = g // KIND
                    load(None, s, po // 2, po % 2, g % KIND)
            sp.wait_ge(y_taken, GROUPS)
            sp.dma_start(d["y_flat"][bass.ds(GROUPS - 1, 1)].rearrange("a p l -> p (a l)"), yout[:]).then_inc(y_stored, 16)
            sp.wait_ge(y_stored, 16 * GROUPS)

        LOADED = 16 * 7

        @block.tensor
        def _(pe):
            def dt_product(g, s, unit):
                pe.wait_ge(loads[s], (g + 1) * LOADED)
                for q in halves():
                    mm = pe.matmul(pc[:, q], wdt[:, s], dtr[:, s, q], start=True, stop=True)
                mm.then_inc(z_done, 1)

            def add_y(g, j):
                step = g * GROUP + j
                n = j % GROUP
                pe.wait_ge(hc_ready, step + 1)
                if n == 0:
                    need(pe, y_taken, g)
                for q in halves():
                    mm = pe.matmul(py[:, q], eye[:], hc[:, n % 2, q], start=(n == 0), stop=(n == GROUP - 1))
                mm.then_inc(y_added, 1)

            def body(g, last):
                for j in range(GROUP):
                    s, n = j // UNIT, j % UNIT
                    step = g * GROUP + j
                    if n == 0:
                        pe.wait_ge(loads[s], (g + 1) * LOADED)
                    need(pe, h_ready, step - 1)
                    for q in halves():
                        mm = pe.matmul(pb[:, j % 2, q], pick[:, s, n * P:(n + 1) * P], bc[:, s, 0, q], start=True, stop=True)
                    mm.then_inc(b_row, 1)
                    need(pe, crow_ready, step)
                    if n == 5 and not (last and s == 1):
                        pe.wait_ge(z_taken, g * 2 + s + 2)
                    for q in halves():
                        mm = pe.matmul(pc[:, q], pick[:, s, n * P:(n + 1) * P], bc[:, s, 1, q], start=True, stop=True)
                    mm.then_inc(c_row, 1)
                    if n == 4 and not (last and s == 1):
                        pe.wait_ge(crow_ready, step + 1)
                        dt_product(g + s, 1 - s, None)
                    if j >= 2 or not (isinstance(g, int) and g == 0):
                        add_y(g, j - 2)

            pe.wait_ge(eye_in, 16)
            dt_product(0, 0, None)
            pe.wait_ge(z_taken, 1)
            groups(pe, body)
            add_y(GROUPS - 1, GROUP - 2)
            add_y(GROUPS - 1, GROUP - 1)

        @block.scalar
        def _(act):
            def take_z(g, s, unit):
                act.wait_ge(z_done, unit + 1)
                act.wait_ge(loads[s], (g + 1) * LOADED)
                need(act, dt_ready, unit)
                nc.scalar.activation(ez[:], pc[:], ACT.Abs, bias=par[:, s, N:N + 1]).then_inc(e_ready, 1)
                nc.scalar.activation(rz[:], pc[:], ACT.Relu, bias=par[:, s, N:N + 1]).then_inc(z_taken, 1)

            def exp_z(unit, s):
                act.wait_ge(e_ready, 2 * unit + 1)
                nc.scalar.activation(ez[:], ez[:], ACT.Exp, scale=-1.0).then_inc(e_ready, 1)
                act.wait_ge(amin_ready, unit + 1)
                nc.scalar.activation(aexp[:, s], amin[:, s], ACT.Exp).then_inc(aexp_ready, 1)

            def ln_z(unit):
                act.wait_ge(e_ready, 2 * unit + 2)
                nc.scalar.activation(lz[:], ez[:], ACT.Ln, bias=1.0).then_inc(l_ready, 1)

            def body(g, last):
                for j in range(GROUP):
                    s, n = j // UNIT, j % UNIT
                    step = g * GROUP + j
                    if n == 0:
                        act.wait_ge(dt_ready, g * 2 + s + 1)
                        act.wait_ge(a_neg_ready, g * 2 + s + 1)
                    need(act, h_ready, step - 1)
                    nc.scalar.activation(a[:, j % 2], dt_[:, s], ACT.Exp, scale=aneg[:, s, n:n + 1]).then_inc(a_ready, 1)
                    need(act, hc_ready, step - 1)
                    act.wait_ge(c_row, step + 1)
                    nc.scalar.copy(crow[:, j % 2], pc[:]).then_inc(crow_ready, 1)
                    if last and s == 1:
                        continue
                    if n == 4:
                        take_z(g + s, 1 - s, g * 2 + s + 1)
                    if n == 5 and not (last and s == 1):
                        exp_z(g * 2 + s + 1, 1 - s)
                    if n == 6:
                        ln_z(g * 2 + s + 1)

            take_z(0, 0, 0)
            exp_z(0, 0)
            ln_z(0)
            groups(act, body)

        @block.vector
        def _(dve):
            def clamp_a(g, s, unit):
                dve.wait_ge(loads[s], (g + 1) * LOADED)
                nc.vector.tensor_scalar(amin[:, s], par[:, s, 0:N], LOG_MAX, None, ALU.min).then_inc(amin_ready, 1)

            def softplus_1(unit):
                dve.wait_ge(e_ready, 2 * unit + 2)
                nc.vector.tensor_scalar(qz[:], ez[:], 1.0, -1.0, ALU.add, ALU.add).then_inc(q_ready, 1)

            def softplus_2(unit, s):
                dve.wait_ge(q_ready, unit + 1)
                dve.wait_ge(l_ready, unit + 1)
                nc.vector.tensor_tensor(qz[:], lz[:], qz[:], ALU.subtract).then_inc(s_ready, 1)
                dve.wait_ge(aexp_ready, unit + 1)
                nc.vector.tensor_scalar(aneg[:, s], aexp[:, s], -1.0, None, ALU.mult).then_inc(a_neg_ready, 1)

            def softplus_3(unit, s):
                dve.wait_ge(s2_ready, unit + 1)
                nc.vector.scalar_tensor_tensor(lz[:], ez[:], LN2, qz[:], ALU.mult, ALU.max).then_inc(s3_ready, 1)
                dve.wait_ge(s3_ready, unit + 1)
                nc.vector.tensor_tensor(dt_[:, s], lz[:], rz[:], ALU.add).then_inc(dt_ready, 1)

            def take_y(g):
                dve.wait_ge(y_added, g * GROUP + GROUP)
                nc.vector.tensor_tensor(dsum[:], par[:, 1, N + 1:N + 2], par[:, 1, N + 2:N + 3], ALU.add).then_inc(dsum_ready, 1)
                dve.wait_ge(dsum_ready, g + 1)
                need(dve, y_stored, g * 16)
                nc.vector.scalar_tensor_tensor(yout[:], u[:, 1], dsum[:], py[:], ALU.mult, ALU.add).then_inc(y_taken, 1)

            def body(g, last):
                for j in range(GROUP):
                    s, n = j // UNIT, j % UNIT
                    step = g * GROUP + j
                    if n == 0:
                        dve.wait_ge(dtu_ready, g * 2 + s + 1)
                    dve.wait_ge(b_row, step + 1)
                    nc.vector.tensor_tensor(pb[:, j % 2], dtu[:, s], pb[:, j % 2], ALU.mult).then_inc(b_ready, 1)
                    dve.wait_ge(b_ready, step + 1)
                    dve.wait_ge(a_ready, step + 1)
                    need(dve, hc_ready, step - 1)
                    f = flow(s)
                    nc.vector.tensor_tensor_scan(h[:, j % 2, f], a[:, j % 2, f], pb[:, j % 2, f], 0.0, ALU.mult, ALU.add)\
                      .then_inc(h_ready, 1)
                    if j == 2 and not (isinstance(g, int) and g == 0):
                        take_y(g - 1)
                    if last and s == 1:
                        continue
                    unit = g * 2 + s + 1
                    if n == 4:
                        clamp_a(g + s, 1 - s, unit)
                    if n == 6:
                        softplus_1(unit)
                    if n == 7:
                        softplus_2(unit, 1 - s)
                    if n == 9:
                        softplus_3(unit, 1 - s)

            clamp_a(0, 0, 0)
            softplus_1(0)
            softplus_2(0, 0)
            softplus_3(0, 0)
            groups(dve, body)
            take_y(GROUPS - 1)

        @block.gpsimd
        def _(pool):
            def add_e(unit):
                pool.wait_ge(s_ready, unit + 1)
                nc.gpsimd.tensor_tensor(qz[:], qz[:], ez[:], ALU.add).then_inc(s2_ready, 1)

            def times_u(unit, s):
                pool.wait_ge(dt_ready, unit + 1)
                nc.gpsimd.tensor_tensor(dtu[:, s], dt_[:, s], u[:, s], ALU.mult).then_inc(dtu_ready, 1)

            def body(g, last):
                for j in range(GROUP):
                    s, n = j // UNIT, j % UNIT
                    step = g * GROUP + j
                    pool.wait_ge(h_ready, step + 1)
                    pool.wait_ge(crow_ready, step + 1)
                    need(pool, y_added, step - 1)
                    nc.gpsimd.tensor_tensor(hc[:, j % 2], h[:, j % 2], crow[:, j % 2], ALU.mult).then_inc(hc_ready, 1)
                    if last and s == 1:
                        continue
                    if n == 7:
                        add_e(g * 2 + s + 1)
                    if n == 9:
                        times_u(g * 2 + s + 1, 1 - s)

            add_e(0)
            times_u(0, 0)
            groups(pool, body)


def tail(nc, d):
    with ExitStack() as ctx:
        def sb(name, shape, dt=F32):
            return ctx.enter_context(nc.sbuf_tensor("t_" + name, shape, dt))

        def sem(name):
            return ctx.enter_context(nc.semaphore("t_" + name))

        eye = sb("eye", [P, P])
        gavg = sb("gavg", [P, NC * NC, P])
        wout = sb("wout", [P, 2, C])
        gam = sb("gam", [P, DI])
        bet = sb("bet", [P, DI])
        wr = sb("wr", [P, NC, EXPERTS])
        rb = sb("rb", [P, EXPERTS])
        w1 = sb("w1", [P, NC, C])
        b1 = sb("b1", [P, NC])
        w2 = sb("w2", [P, NC, C])
        b2 = sb("b2", [EXPERTS, C])
        spread = sb("spread", [EXPERTS, C])
        y0 = sb("y0", [P, KIND, L])
        y1 = sb("y1", [P, KIND, L])
        yt = sb("yt", [P, TT, 2, DI])
        sz = sb("sz", [P, TT, 2, DI])
        gated = sb("gated", [P, TT, KIND, P])
        yg = sb("yg", [P, KIND, L])
        st = sb("st", [P, NC, 2, 6])
        ln_mv = sb("ln_mv", [P, TT, 2, 2])
        ln_st = sb("ln_st", [P, TT, 2, 6])
        ln_r = sb("ln_r", [P, TT, 2])
        mv = sb("mv", [P, NC, 2])
        gmean = sb("gmean", [P, NC])
        dev = sb("dev", [P, NC])
        chan_var = sb("chan_var", [P, NC])
        std = sb("std", [P, NC])
        rstd = sb("rstd", [P, NC])
        eps = sb("eps", [P, 1])
        xt = sb("xt", [P, NC, L])
        x1 = sb("x1", [P, NC, L])
        xn = sb("xn", [P, NC, L])
        pr = sb("pr", [P, TT, EXPERTS])
        pe_ = sb("pe", [P, TT, EXPERTS])
        ge = sb("ge", [P, TT, EXPERTS])
        rank = sb("rank", [P, TT, EXPERTS])
        comb = sb("comb", [P, TT, EXPERTS])
        red = sb("red", [P, TT])
        combt = sb("combt", [EXPERTS, L])
        hid = sb("hid", [P, NC, L])
        out = sb("out", [P, 4, C])
        big = [ctx.enter_context(nc.psum_tensor(f"t_big{i}", [P, L], F32)) for i in range(3)]
        small = [ctx.enter_context(nc.psum_tensor(f"t_small{i}", [P, BANK], F32)) for i in range(2)]

        weights_in = sem("weights_in")
        NW = 12
        y_in = sem("y_in")
        sz_in = sem("sz_in")
        xt_in = sem("xt_in")
        sum_ready = sem("sum_ready")
        yt_done = sem("yt_done")
        yt_ready = sem("yt_ready")
        ln_stat = sem("ln_stat")
        ln_std = sem("ln_std")
        yln = sem("yln")
        back_done = sem("back_done")
        yg_ready = sem("yg_ready")
        op_done = sem("op_done")
        x1_ready = sem("x1_ready")
        stats = sem("stats")
        sums = sem("sums")
        std_ready = sem("std_ready")
        xn_ready = sem("xn_ready")
        lg_done = sem("lg_done")
        lg_ready = sem("lg_ready")
        ex_ready = sem("ex_ready")
        comb_ready = sem("comb_ready")
        ct_done = sem("ct_done")
        ct_ready = sem("ct_ready")
        f1_done = sem("f1_done")
        gelu_ready = sem("gelu_ready")
        sp_done = sem("sp_done")
        hw_ready = sem("hw_ready")
        f2_done = sem("f2_done")
        out_ready = sem("out_ready")
        out_stored = [sem(f"out_stored{i}") for i in range(4)]
        block = ctx.enter_context(nc.Block())

        @block.sync
        def _(sp):
            sp.dma_start(eye[:], d["eye"]).then_inc(weights_in, 16)
            for pair in range(PAIRS):
                need(sp, sum_ready, KIND * pair)
                sp.dma_start(y0[:], d["y_flat"][(pair * 2) * KIND:(pair * 2 + 1) * KIND].rearrange("t p l -> p t l")).then_inc(y_in, 16)
                sp.dma_start(y1[:], d["y_flat"][(pair * 2 + 1) * KIND:(pair * 2 + 2) * KIND].rearrange("t p l -> p t l")).then_inc(y_in, 16)
                need(sp, yln, 4 * pair)
                sp.dma_start(sz[:].rearrange("p t b c -> p t (b c)"), d["sz"][pair]).then_inc(sz_in, 16)
                if pair == 0:
                    for t, src in ((gavg, d["gavg"]), (wout, d["wout"]), (wr, d["wr"]), (w1, d["w1"]), (b1, d["b1"]),
                                   (w2, d["w2"]), (b2, d["b2"]), (spread, d["spread"]),
                                   (gam, d["ln_g"].partition_broadcast(P)), (bet, d["ln_b"].partition_broadcast(P)),
                                   (rb, d["rb"].partition_broadcast(P))):
                        sp.dma_start(t[:], src).then_inc(weights_in, 16)
                for b in (2 * pair, 2 * pair + 1):
                    need(sp, x1_ready, NC * b)
                    sp.dma_start(xt[:], d["xt"][b].rearrange("c p l -> p c l")).then_inc(xt_in, 16)
                    for t in range(TT):
                        i = b * TT + t
                        sp.wait_ge(out_ready, i + 1)
                        sp.dma_start(d["out"][b, t * P:(t + 1) * P, :], out[:, i % 4]).then_inc(out_stored[i % 4], 16)
            for i in range(4):
                sp.wait_ge(out_stored[i], 16 * BATCH * TT // 4)

        @block.tensor
        def _(pe):
            pe.wait_ge(weights_in, 16 * NW)
            for pair in range(PAIRS):
                for t in range(TT):
                    i = pair * TT + t
                    if t == 0:
                        pe.wait_ge(sum_ready, KIND * (pair + 1))
                    need(pe, yt_ready, i - 1)
                    need(pe, out_ready, 2 * TT * pair)
                    for kind in range(KIND):
                        mm = pe.transpose(small[i % 2][:, kind * P:(kind + 1) * P], yg[:, kind, t * P:(t + 1) * P], eye[:])
                    mm.then_inc(yt_done, 1)
                for kind in range(KIND):
                    i = pair * KIND + kind
                    pe.wait_ge(yln, 4 * (pair + 1))
                    need(pe, hw_ready, NC * 2 * pair)
                    for t in range(TT):
                        mm = pe.transpose(big[kind][:, t * P:(t + 1) * P], gated[:, t, kind], eye[:])
                    mm.then_inc(back_done, 1)
                for b in (2 * pair, 2 * pair + 1):
                    o = b % 2
                    r = slice(o * HALF, (o + 1) * HALF)
                    pe.wait_ge(yg_ready, KIND * (pair + 1))
                    need(pe, hw_ready, NC * b)
                    for c in range(NC):
                        for q in halves():
                            pe.matmul(big[c][:, q], wout[:, 0, c * P:(c + 1) * P], yg[:, o, q], start=True, stop=False)
                            mm = pe.matmul(big[c][:, q], wout[r, 1, c * P:(c + 1) * P], yg[r, 2, q], start=False, stop=True)
                        mm.then_inc(op_done, 1)
                    for step in range(2):
                        pe.wait_ge(stats, 2 * b + step + 1)
                        if step == 0:
                            need(pe, out_ready, TT * b)
                        for co in range(NC):
                            for ci in range(NC):
                                rhs = mv[:, ci, 0:1] if step == 0 else chan_var[:, ci:ci + 1]
                                col = step * NC + co
                                mm = pe.matmul(small[0][:, col:col + 1], gavg[:, ci * NC + co], rhs,
                                               start=(ci == 0), stop=(ci == NC - 1))
                        mm.then_inc(sums, 1)
                    pe.wait_ge(xn_ready, b + 1)
                    for t in range(TT):
                        for c in range(NC):
                            mm = pe.matmul(small[1][:, t * EXPERTS:(t + 1) * EXPERTS], xn[:, c, t * P:(t + 1) * P], wr[:, c],
                                           start=(c == 0), stop=(c == NC - 1))
                    mm.then_inc(lg_done, 1)
                    for j in range(2):
                        for q in halves():
                            for c in range(NC):
                                mm = pe.matmul(big[j][:, q], w1[:, c, j * P:(j + 1) * P], xn[:, c, q], start=(c == 0), stop=(c == NC - 1))
                        mm.then_inc(f1_done, 1)
                    pe.wait_ge(comb_ready, b + 1)
                    for t in range(TT):
                        mm = pe.transpose(big[2][0:EXPERTS, t * P:(t + 1) * P], comb[:, t], eye[:])
                    mm.then_inc(ct_done, 1)
                    for j in range(NC):
                        if j == 2:
                            pe.wait_ge(hw_ready, NC * b + 1)
                            for q in halves():
                                for c in range(NC):
                                    mm = pe.matmul(big[1][:, q], w1[:, c, j * P:(j + 1) * P], xn[:, c, q], start=(c == 0), stop=(c == NC - 1))
                            mm.then_inc(f1_done, 1)
                        pe.wait_ge(ct_ready, b + 1)
                        pe.wait_ge(gelu_ready, NC * b + j + 1 if j < 2 else NC * b + 2)
                        dst = big[2] if j != 1 else big[0]
                        if j:
                            pe.wait_ge(hw_ready, NC * b + j - 1 + (1 if j == 2 else 0))
                        for q in halves():
                            mm = pe.matmul(dst[:, q], spread[:, j * P:(j + 1) * P], combt[:, q], start=True, stop=True)
                        mm.then_inc(sp_done, 1)
                    pe.wait_ge(hw_ready, NC * (b + 1))
                    for t in range(TT):
                        i = b * TT + t
                        tok = slice(t * P, (t + 1) * P)
                        ps = small[t % 2][:, 0:C]
                        if t >= 2:
                            pe.wait_ge(out_ready, i - 1)
                        pe.matmul(ps, combt[:, tok], b2[:], start=True, stop=False, skip_group_check=True)
                        for j in range(NC):
                            pe.matmul(ps, hid[:, j, tok], w2[:, j], start=False, stop=False, skip_group_check=True)
                        for c in range(NC):
                            mm = pe.matmul(ps[:, c * P:(c + 1) * P], x1[:, c, tok], eye[:], start=False, stop=(c == NC - 1),
                                           skip_group_check=True)
                        mm.then_inc(f2_done, 1)

        @block.scalar
        def _(act):
            act.wait_ge(weights_in, 16 * NW)
            for pair in range(PAIRS):
                for t in range(TT):
                    i = pair * TT + t
                    act.wait_ge(yt_done, i + 1)
                    need(act, back_done, KIND * pair)
                    src = small[i % 2]
                    nc.scalar.copy(yt[:, t, :, 0:P], src[:, 0:2 * P].rearrange("p (b c) -> p b c", b=2))
                    nc.scalar.copy(yt[:, t, :, P:DI], src[:, 2 * P:3 * P].rearrange("p (b c) -> p b c", b=2)).then_inc(yt_ready, 1)
                act.wait_ge(ln_stat, pair + 1)
                nc.scalar.activation(ln_r[:], ln_mv[:, :, :, 1], ACT.Sqrt, bias=eps[:]).then_inc(ln_std, 1)
                for kind in range(KIND):
                    act.wait_ge(back_done, pair * KIND + kind + 1)
                    nc.scalar.copy(yg[:, kind], big[kind][:]).then_inc(yg_ready, 1)
                for b in (2 * pair, 2 * pair + 1):
                    act.wait_ge(sums, 2 * b + 2)
                    nc.scalar.activation(std[:], small[0][:, NC:2 * NC], ACT.Sqrt, bias=eps[:]).then_inc(std_ready, 1)
                    act.wait_ge(lg_ready, b + 1)
                    nc.scalar.activation(pe_[:], pr[:], ACT.Exp).then_inc(ex_ready, 1)
                    for j in range(NC):
                        if j == 2:
                            act.wait_ge(f1_done, NC * b + 3)
                        else:
                            act.wait_ge(f1_done, NC * b + j + 1)
                        if j == 0:
                            need(act, f2_done, TT * b)
                        nc.scalar.activation(hid[:, j], big[j if j < 2 else 1][:], ACT.Gelu, bias=b1[:, j:j + 1]).then_inc(gelu_ready, 1)
                        if j == 1:
                            act.wait_ge(ct_done, b + 1)
                            nc.scalar.copy(combt[:], big[2][0:EXPERTS, :]).then_inc(ct_ready, 1)
                    for t in range(TT):
                        i = b * TT + t
                        act.wait_ge(f2_done, i + 1)
                        need(act, out_stored[i % 4], 16 * (i // 4))
                        nc.scalar.copy(out[:, i % 4], small[t % 2][:, 0:C]).then_inc(out_ready, 1)

        @block.vector
        def _(dve):
            chain = ctx.enter_context(nc.semaphore("t_chain"))
            links = [0]

            def link(ins):
                links[0] += 1
                ins.then_inc(chain, 1)
                dve.wait_ge(chain, links[0])

            V = nc.vector
            link(V.memset(eps[:], 1e-5))
            for pair in range(PAIRS):
                for kind in range(KIND):
                    dve.wait_ge(y_in, 32 * (pair + 1))
                    need(dve, op_done, 2 * NC * pair)
                    V.tensor_tensor(yg[:, kind].rearrange("p (h w) -> p h w", h=HW), y0[:, kind].rearrange("p (h w) -> p h w", h=HW),
                                    y1[:, kind].rearrange("p (w h) -> p h w", w=HW), ALU.add).then_inc(sum_ready, 1)
                if pair == 0:
                    dve.wait_ge(weights_in, 16 * NW)
                for t in range(TT):
                    dve.wait_ge(yt_ready, pair * TT + t + 1)
                    for b in range(2):
                        last = V.bn_stats(ln_st[:, t, b], yt[:, t, b])
                    link(last)
                    for b in range(2):
                        last = V.bn_aggr(ln_mv[:, t, b], ln_st[:, t, b])
                last.then_inc(ln_stat, 1)
                dve.wait_ge(ln_std, pair + 1)
                dve.wait_ge(ln_stat, pair + 1)
                link(V.reciprocal(ln_r[:], ln_r[:]))
                for t in range(TT):
                    for b in range(2):
                        last = V.tensor_scalar(yt[:, t, b], yt[:, t, b], ln_mv[:, t, b, 0:1], ln_r[:, t, b:b + 1], ALU.subtract, ALU.mult)
                last.then_inc(yln, 1)
                dve.wait_ge(yln, 4 * pair + 1)
                flat = yt[:].rearrange("p t b c -> p (t b) c")
                V.tensor_tensor(flat, flat, gam[:].unsqueeze(1).broadcast_to([P, 2 * TT, DI]), ALU.mult).then_inc(yln, 1)
                dve.wait_ge(yln, 4 * pair + 2)
                V.tensor_tensor(flat, flat, bet[:].unsqueeze(1).broadcast_to([P, 2 * TT, DI]), ALU.add).then_inc(yln, 1)
                dve.wait_ge(yln, 4 * pair + 3)
                dve.wait_ge(sz_in, 16 * (pair + 1))
                need(dve, back_done, KIND * pair)
                V.tensor_tensor(gated[:, :, 0:2], yt[:, :, :, 0:P], sz[:, :, :, 0:P], ALU.mult)
                V.tensor_tensor(gated[:, :, 2].rearrange("p t (b c) -> p t b c", b=2), yt[:, :, :, P:DI], sz[:, :, :, P:DI],
                                ALU.mult).then_inc(yln, 1)
                for b in (2 * pair, 2 * pair + 1):
                    dve.wait_ge(xt_in, 16 * (b + 1))
                    need(dve, f2_done, TT * b)
                    for c in range(NC):
                        dve.wait_ge(op_done, NC * b + c + 1)
                        V.tensor_tensor(x1[:, c], xt[:, c], big[c][:], ALU.add).then_inc(x1_ready, 1)
                        dve.wait_ge(x1_ready, NC * b + c + 1)
                        for h, q in enumerate(halves()):
                            last = V.bn_stats(st[:, c, h], x1[:, c, q])
                        link(last)
                        last = V.bn_aggr(mv[:, c], st[:, c].rearrange("p a s -> p (a s)"))
                    last.then_inc(stats, 1)
                    dve.wait_ge(stats, 2 * b + 1)
                    dve.wait_ge(sums, 2 * b + 1)
                    link(V.tensor_copy(gmean[:], small[0][:, 0:NC]))
                    link(V.tensor_tensor(dev[:], mv[:, :, 0], gmean[:], ALU.subtract))
                    link(V.tensor_tensor(dev[:], dev[:], dev[:], ALU.mult))
                    V.tensor_tensor(chan_var[:], mv[:, :, 1], dev[:], ALU.add).then_inc(stats, 1)
                    dve.wait_ge(std_ready, b + 1)
                    link(V.reciprocal(rstd[:], std[:]))
                    for c in range(NC):
                        last = V.tensor_scalar(xn[:, c], x1[:, c], gmean[:, c:c + 1], rstd[:, c:c + 1], ALU.subtract, ALU.mult)
                    last.then_inc(xn_ready, 1)

                    dve.wait_ge(lg_done, b + 1)
                    def wide(x, n=EXPERTS):
                        return x.unsqueeze(2).broadcast_to([P, TT, n])
                    lg = small[1][:, 0:TT * EXPERTS].rearrange("p (t e) -> p t e", e=EXPERTS)
                    link(V.tensor_tensor(pr[:], lg, rb[:].unsqueeze(1).broadcast_to([P, TT, EXPERTS]), ALU.add))
                    link(V.tensor_reduce(red[:], pr[:], AX_X, ALU.max))
                    V.tensor_tensor(pr[:], pr[:], wide(red[:]), ALU.subtract).then_inc(lg_ready, 1)
                    dve.wait_ge(ex_ready, b + 1)
                    link(V.tensor_reduce(red[:], pe_[:], AX_X, ALU.add))
                    link(V.reciprocal(red[:], red[:]))
                    link(V.tensor_tensor(pr[:], pe_[:], wide(red[:]), ALU.mult))
                    link(V.memset(rank[:], 0.0))
                    for gap in range(1, EXPERTS):
                        m = EXPERTS - gap
                        link(V.tensor_tensor(ge[:, :, 0:m], pr[:, :, 0:m], pr[:, :, gap:EXPERTS], ALU.is_ge))
                        link(V.tensor_tensor(rank[:, :, gap:EXPERTS], rank[:, :, gap:EXPERTS], ge[:, :, 0:m], ALU.add))
                        link(V.tensor_tensor(rank[:, :, 0:m], rank[:, :, 0:m], ge[:, :, 0:m], ALU.subtract))
                        link(V.tensor_scalar(rank[:, :, 0:m], rank[:, :, 0:m], 1.0, None, ALU.add))
                    link(V.tensor_scalar(rank[:], rank[:], 1.5, None, ALU.is_lt))
                    link(V.tensor_tensor(pr[:], pr[:], rank[:], ALU.mult))
                    link(V.tensor_reduce(red[:], pr[:], AX_X, ALU.add))
                    link(V.tensor_scalar(red[:], red[:], 1e-8, None, ALU.add))
                    link(V.reciprocal(red[:], red[:]))
                    V.tensor_tensor(comb[:], pr[:], wide(red[:]), ALU.mult).then_inc(comb_ready, 1)
                    for j in range(NC):
                        dve.wait_ge(gelu_ready, NC * b + j + 1)
                        dve.wait_ge(sp_done, NC * b + j + 1)
                        V.tensor_tensor(hid[:, j], hid[:, j], (big[2] if j != 1 else big[0])[:], ALU.mult).then_inc(hw_ready, 1)


def bass_vision_mamba_moe(nc, x, eye, win, wx, gavg, conv_p, pick, wdt, par, wout, ln_g, ln_b, wr, rb, w1, b1, w2, b2, spread, out):
    def scratch(name, shape, dt=F32):
        return nc.dram_tensor("scratch_" + name, shape, dt, kind="Internal").ap()

    bc = scratch("bc", (PAIRS, DIRS, 2, PIECES * PR, L), BF16)
    dts = scratch("dts", (PAIRS, DIRS, 2 * PR, L))
    u = scratch("u", (PAIRS, 2, KIND, P, L))
    d = dict(
        x=x.rearrange("b h w c -> b (h w) c"), eye=eye, win=win, wx=wx, gavg=gavg, conv_p=conv_p, pick=pick, wdt=wdt,
        par=par, wout=wout, ln_g=ln_g, ln_b=ln_b, wr=wr, rb=rb, w1=w1, b1=b1, w2=w2, b2=b2, spread=spread,
        out=out.rearrange("b h w c -> b (h w) c"),
        xt=scratch("xt", (BATCH, NC, P, L)), sz=scratch("sz", (PAIRS, P, TT, 2 * DI)),
        bc=bc, dts=dts, u=u, y_flat=scratch("y", (GROUPS, P, L)),
        bc_flat=bc.rearrange("a k m r l -> (a k m) r l"), dts_flat=dts.rearrange("a k r l -> (a k) r l"),
        u_flat=u.rearrange("a o t p l -> (a o t) p l"),
    )
    head(nc, d)
    scan(nc, d)
    tail(nc, d)


def lay_out(np, a):
    f = np.float32
    kinds = [(0, 0, P), (1, 0, P), (2, 0, 0)]
    o = {}
    o["eye"] = np.eye(P, dtype=f)
    chunk = lambda w: np.ascontiguousarray(w.reshape(NC, P, -1).transpose(1, 0, 2))
    o["win"] = chunk(a["L0_conv_in_proj_w"].T)

    def by_kind(w):
        w = np.moveaxis(w, -1, 0)
        return np.stack([w[0:P], w[0:P], np.concatenate([w[P:], w[P:]])])

    wx = np.zeros((DIRS, KIND, P, P), f)
    xw = a["L0_conv_x_proj_w"]
    for kind in range(KIND):
        for b in range(2):
            if kind != 2 and kind != b:
                continue
            rows = slice(0, P) if kind < 2 else slice(b * HALF, (b + 1) * HALF)
            ch = slice(0, P) if kind < 2 else slice(P, DI)
            w = xw[:, :, ch].transpose(0, 2, 1)
            wx[:, kind, rows, b * N:(b + 1) * N] = w[:, :, R:R + N]
            wx[:, kind, rows, PR + b * N:PR + (b + 1) * N] = w[:, :, R + N:]
            wx[:, kind, rows, (2 + b) * PR:(2 + b) * PR + R] = w[:, :, 0:R]
    o["wx"] = np.ascontiguousarray(wx.reshape(DIRS * KIND, P, P).transpose(1, 0, 2))
    ch = np.arange(C) // (C // 32)
    g = (ch[:, None] == ch[None, :]).astype(f) / f(C // 32)
    o["gavg"] = np.ascontiguousarray(g.reshape(NC, P, NC, P).transpose(1, 0, 2, 3).reshape(P, NC * NC, P))
    cp = np.concatenate([by_kind(a["L0_conv_conv_w"].reshape(DI, 9).T), by_kind(a["L0_conv_conv_b"][None])], -1)
    o["conv_p"] = np.ascontiguousarray(cp.transpose(1, 0, 2))
    pick = np.zeros((KIND, PIECES, 2, N, N, P), f)
    for kind in range(KIND):
        for b in range(2):
            cols = slice(0, P) if kind == b else slice(b * HALF, (b + 1) * HALF) if kind == 2 else slice(0, 0)
            for n in range(N):
                pick[kind, :, b, n, n, cols] = 1
    o["pick"] = pick.reshape(KIND, PIECES * PR, N * P).astype(np.dtype("bfloat16"))
    wdt = np.zeros((DIRS, KIND, 2 * PR, P), f)
    dw = a["L0_conv_dt_projs_w"].transpose(0, 2, 1)
    wdt[:, 0, 0:R] = dw[:, :, 0:P]
    wdt[:, 1, PR:PR + R] = dw[:, :, 0:P]
    wdt[:, 2, 0:R, 0:HALF] = dw[:, :, P:]
    wdt[:, 2, PR:PR + R, HALF:] = dw[:, :, P:]
    o["wdt"] = wdt.reshape(DIRS * KIND, 2 * PR, P)
    par = np.zeros((DIRS, KIND, P, N + 3), f)
    logs = a["L0_conv_A_logs"].reshape(DIRS, DI, N)
    skips = a["L0_conv_Ds"].reshape(DIRS, DI)
    for k in range(DIRS):
        par[k, :, :, 0:N] = by_kind(logs[k].T)
        par[k, :, :, N] = by_kind(a["L0_conv_dt_projs_b"][k])
        par[k, :, :, N + 1] = by_kind(skips[k % 2])
        par[k, :, :, N + 2] = by_kind(skips[k % 2 + 2])
    o["par"] = par.reshape(DIRS * KIND, P, N + 3)
    wo = a["L0_conv_out_proj_w"].T
    o["wout"] = np.ascontiguousarray(np.stack([wo[0:P], np.concatenate([wo[P:], wo[P:]])], 1))
    o["ln_g"], o["ln_b"] = a["L0_conv_out_norm_g"], a["L0_conv_out_norm_b"]
    o["wr"] = chunk(a["L1_conv_router_w"].T)
    o["rb"] = a["L1_conv_router_b"]
    o["w1"] = chunk(a["L1_conv_fc1_w"].reshape(C, C).T)
    o["b1"] = np.ascontiguousarray(a["L1_conv_fc1_b"].reshape(NC, P).T)
    o["w2"] = chunk(a["L1_conv_fc2_w"].transpose(0, 2, 1).reshape(C, C))
    o["b2"] = a["L1_conv_fc2_b"]
    e = np.arange(C) // HID
    o["spread"] = (np.arange(EXPERTS)[:, None] == e[None, :]).astype(f)
    return o


_INS = ["x", "eye", "win", "wx", "gavg", "conv_p", "pick", "wdt", "par", "wout", "ln_g", "ln_b", "wr", "rb", "w1", "b1", "w2",
        "b2", "spread"]


def kernel(**inputs):
    import numpy as _np
    import concourse.bacc as _bacc
    from concourse import mybir as _mybir
    from concourse.bass_utils import run_bass_kernel_spmd as _run

    nc = _bacc.Bacc("TRN2", target_bir_lowering=False, num_devices=1)
    given = {k: _np.asarray(v) for k, v in inputs.items()}
    laid = lay_out(_np, given)
    laid["x"] = given["x"]
    arrays, args = {}, []
    for name in _INS:
        a = _np.ascontiguousarray(laid[name])
        arrays[f"in_{name}_dram"] = a
        args.append(nc.dram_tensor(f"in_{name}_dram", a.shape, _mybir.dt.from_np(a.dtype), kind="ExternalInput").ap())
    args.append(nc.dram_tensor("out_0_dram", (BATCH, HW, HW, C), F32, kind="ExternalOutput").ap())
    bass_vision_mamba_moe(nc, *args)
    r = _run(nc, [arrays], core_ids=[0])
    return r.results[0]["out_0_dram"]
```

```python
from contextlib import ExitStack

import concourse.bass as bass
from concourse import mybir

F32 = mybir.dt.float32
BF16 = mybir.dt.bfloat16
ALU = mybir.AluOpType
ACT = mybir.ActivationFunctionType
AX_X = mybir.AxisListType.X

P = 128
BATCH = 4
HW = 32
L = HW * HW
C = 384
NC = C // P
DI = 192
HALF = DI - P
N = 16
R = 24
DIRS = 4
KIND = 3
PAIRS = BATCH // 2
TT = L // P
PAD = HW + 2
EXPERTS = 4
HID = 96
BANK = 512
PIECES = 3
PR = 32
UNIT = N
GROUP = 2 * UNIT
GROUPS = PAIRS * 2 * KIND
RING = 4
HC_RING = 8
LAG = 5
AHEAD = 2
PREP = 4
LN2 = 0.693147
LOG_MAX = 80.0


def need(eng, semaphore, value):
    if isinstance(value, int) and value <= 0:
        return
    eng.wait_ge(semaphore, value)


def halves():
    return [slice(q * BANK, (q + 1) * BANK) for q in range(L // BANK)]


def head(nc, d, keep, keep_from):
    with ExitStack() as ctx:
        def sb(name, shape, dt=F32):
            return ctx.enter_context(nc.sbuf_tensor("h_" + name, shape, dt))

        def sem(name):
            return ctx.enter_context(nc.semaphore("h_" + name))

        eye, gavg = keep["eye"], keep["gavg"]
        win = sb("win", [P, NC, C])
        wx = sb("wx", [P, DIRS * KIND, P])
        conv_p = sb("conv_p", [P, KIND, 10])
        xin = sb("xin", [P, 2, TT, C])
        xt = sb("xt", [P, 2, NC, L])
        xn = sb("xn", [P, 2, NC, L])
        xpad = sb("xpad", [P, KIND, PAD, PAD])
        acc = sb("acc", [P, KIND, L])
        xc = sb("xc", [P, KIND, L])
        xct = sb("xct", [P, KIND, L])
        zt = sb("zt", [P, TT, 2 * DI])
        hi = sb("hi", [2 * PR, 2, L], BF16)
        mid = sb("mid", [2 * PR, 2, L], BF16)
        lo = sb("lo", [2 * PR, 2, L], BF16)
        rest = sb("rest", [2 * PR, L])
        dts = sb("dts", [P, 2, L])
        st = sb("st", [P, NC, 2, 6])
        mv = sb("mv", [P, BATCH, NC, 2])
        gmean = sb("gmean", [P, BATCH, NC])
        dev = sb("dev", [P, BATCH, NC])
        chan_var = sb("chan_var", [P, BATCH, NC])
        rstd = sb("rstd", [P, BATCH, NC])
        std = sb("std", [P, BATCH, NC])
        eps = sb("eps", [P, 1])
        big = [ctx.enter_context(nc.psum_tensor(f"h_big{i}", [P, L], F32)) for i in range(2)]
        pz = [ctx.enter_context(nc.psum_tensor(f"h_pz{i}", [P, BANK], F32)) for i in range(2)]
        pst = ctx.enter_context(nc.psum_tensor("h_pst", [P, BANK], F32))

        weights_in = sem("weights_in")
        kept_in = sem("kept_in")
        x_in = [sem(f"x_in{b}") for b in range(BATCH)]
        xt_out = [sem(f"xt_out{b}") for b in range(BATCH)]
        borders = sem("borders")
        turned = sem("turned")
        xt_ready = sem("xt_ready")
        stats = sem("stats")
        sums = sem("sums")
        std_ready = sem("std_ready")
        xn_ready = sem("xn_ready")
        xh_done = sem("xh_done")
        xpad_ready = sem("xpad_ready")
        z_done = sem("z_done")
        z_ready = sem("z_ready")
        z_out = sem("z_out")
        conv_step = sem("conv_step")
        xc_ready = sem("xc_ready")
        xct_ready = sem("xct_ready")
        u_out = sem("u_out")
        xd_done = sem("xd_done")
        hi_ready = sem("hi_ready")
        rest_ready = sem("rest_ready")
        mid_ready = sem("mid_ready")
        lo_ready = sem("lo_ready")
        bc_out = [sem(f"bc_out{i}") for i in range(2)]
        block = ctx.enter_context(nc.Block())

        def xd(pair, k):
            return pair * DIRS + k

        @block.sync
        def _(sp):
            for t, src in ((eye, d["eye"]), (win, d["win"]), (gavg, d["gavg"]), (wx, d["wx"]), (conv_p, d["conv_p"])):
                sp.dma_start(t[:], src).then_inc(weights_in, 16)
            for b in range(BATCH):
                if b >= 2:
                    sp.wait_ge(turned, NC * (b - 1))
                sp.dma_start(xin[:, b % 2], d["x"][b].rearrange("(t p) c -> p t c", p=P)).then_inc(x_in[b], 16)
            for pair in range(PAIRS):
                for b in (2 * pair, 2 * pair + 1):
                    sp.wait_ge(xt_ready, NC * (b + 1))
                    sp.dma_start(d["xt"][b].rearrange("c p l -> p c l"), xt[:, b % 2]).then_inc(xt_out[b], 16)
                sp.wait_ge(z_ready, TT * (pair + 1))
                sp.dma_start(d["sz"][pair], zt[:]).then_inc(z_out, 16)
                sp.wait_ge(xc_ready, KIND * (pair + 1))
                sp.dma_start(d["u"][pair, 0].rearrange("t p l -> p t l"), xc[:]).then_inc(u_out, 16)
                sp.wait_ge(xct_ready, KIND * (pair + 1))
                sp.dma_start(d["u"][pair, 1].rearrange("t p l -> p t l"), xct[:]).then_inc(u_out, 16)
                for k in range(DIRS):
                    i = xd(pair, k)
                    sp.wait_ge(lo_ready, i + 1)
                    for piece, t in enumerate((hi, mid, lo)):
                        for m in range(2):
                            sp.dma_start(d["bc"][pair, k, m, piece * PR:(piece + 1) * PR], t[m * PR:(m + 1) * PR, i % 2])\
                              .then_inc(bc_out[i % 2], 16)
                    sp.dma_start(d["dts"][pair, k], dts[2 * PR:P, i % 2]).then_inc(bc_out[i % 2], 16)
            for name, src in keep_from.items():
                sp.dma_start(keep[name][:], src).then_inc(kept_in, 16)
            sp.wait_ge(kept_in, 16 * len(keep_from))
            for b in range(BATCH):
                sp.wait_ge(xt_out[b], 16)
            sp.wait_ge(z_out, 16 * PAIRS)
            sp.wait_ge(u_out, 32 * PAIRS)
            for i in range(2):
                sp.wait_ge(bc_out[i], 16 * 7 * PAIRS * DIRS // 2)

        @block.tensor
        def _(pe):
            pe.wait_ge(weights_in, 16 * 5)

            def transposes(pair):
                for b in (2 * pair, 2 * pair + 1):
                    pe.wait_ge(x_in[b], 16)
                    for c in range(NC):
                        i = b * NC + c
                        if b % 2 == 0 and c < 2:
                            if pair:
                                pe.wait_ge(xpad_ready, KIND * pair)
                        else:
                            pe.wait_ge(xt_ready, i - 1)
                        for t in range(TT):
                            mm = pe.transpose(big[i % 2][:, t * P:(t + 1) * P], xin[:, b % 2, t, c * P:(c + 1) * P], eye[:])
                        mm.then_inc(turned, 1)

            def group_stats(pair):
                for b in (2 * pair, 2 * pair + 1):
                    for step, src in ((0, mv), (1, chan_var)):
                        pe.wait_ge(stats, 2 * b + step + 1)
                        for co in range(NC):
                            for ci in range(NC):
                                rhs = mv[:, b, ci, 0:1] if step == 0 else chan_var[:, b, ci:ci + 1]
                                col = (b * 2 + step) * NC + co
                                mm = pe.matmul(pst[:, col:col + 1], gavg[:, ci * NC + co], rhs,
                                               start=(ci == 0), stop=(ci == NC - 1))
                        mm.then_inc(sums, 1)

            def in_proj(pair):
                pe.wait_ge(xn_ready, 2 * (pair + 1))
                pe.wait_ge(xt_ready, NC * 2 * (pair + 1))
                if pair:
                    pe.wait_ge(rest_ready, DIRS * pair)
                for kind in range(KIND):
                    i = pair * KIND + kind
                    buf = big[kind % 2]
                    if kind == 2:
                        pe.wait_ge(xpad_ready, i - 1)
                    for q in halves():
                        if kind < 2:
                            for c in range(NC):
                                mm = pe.matmul(buf[:, q], win[:, c, 0:P], xn[:, kind, c, q], start=(c == 0), stop=(c == NC - 1))
                        else:
                            for b in range(2):
                                for c in range(NC):
                                    mm = pe.matmul(buf[b * HALF:(b + 1) * HALF, q], win[:, c, P:DI], xn[:, b, c, q],
                                                   start=(c == 0), stop=(c == NC - 1))
                    mm.then_inc(xh_done, 1)
                for t in range(TT):
                    i = pair * TT + t
                    need(pe, z_ready, i - 1)
                    for b in range(2):
                        for c in range(NC):
                            mm = pe.matmul(pz[i % 2][:, b * DI:(b + 1) * DI], xn[:, b, c, t * P:(t + 1) * P], win[:, c, DI:C],
                                           start=(c == 0), stop=(c == NC - 1))
                    mm.then_inc(z_done, 1)

            def x_proj(pair):
                for k in range(DIRS):
                    i = xd(pair, k)
                    src = xct if k % 2 else xc
                    need(pe, xct_ready if k % 2 else xc_ready, KIND * (pair + 1))
                    if k < 2:
                        pe.wait_ge(xt_ready, NC * 2 * min(pair + 2, PAIRS))
                        pe.wait_ge(xpad_ready, KIND * (pair + 1))
                    else:
                        pe.wait_ge(rest_ready, i - 1)
                    for q in halves():
                        for t in range(KIND):
                            mm = pe.matmul(big[k % 2][:, q], wx[:, k * KIND + t], src[:, t, q], start=(t == 0), stop=(t == KIND - 1))
                    mm.then_inc(xd_done, 1)

            transposes(0)
            group_stats(0)
            in_proj(0)
            transposes(1)
            group_stats(1)
            x_proj(0)
            in_proj(1)
            x_proj(1)

        @block.scalar
        def _(act):
            def copy_xt(pair):
                for b in (2 * pair, 2 * pair + 1):
                    for c in range(NC):
                        i = b * NC + c
                        act.wait_ge(turned, i + 1)
                        if b >= 2:
                            act.wait_ge(xt_out[b - 2], 16)
                            act.wait_ge(xn_ready, b - 1)
                        nc.scalar.copy(xt[:, b % 2, c], big[i % 2][:]).then_inc(xt_ready, 1)

            def root(pair):
                for b in (2 * pair, 2 * pair + 1):
                    act.wait_ge(sums, 2 * b + 2)
                    nc.scalar.activation(std[:, b], pst[:, (b * 2 + 1) * NC:(b * 2 + 2) * NC], ACT.Sqrt,
                                         bias=eps[:]).then_inc(std_ready, 1)

            def fill_xpad(pair):
                act.wait_ge(borders, 1)
                for kind in range(KIND):
                    act.wait_ge(xh_done, pair * KIND + kind + 1)
                    need(act, conv_step, pair * KIND * 9)
                    nc.scalar.copy(xpad[:, kind, 1:HW + 1, 1:HW + 1], big[kind % 2][:].rearrange("p (h w) -> p h w", h=HW))\
                      .then_inc(xpad_ready, 1)

            def silu_z(pair):
                for t in range(TT):
                    i = pair * TT + t
                    act.wait_ge(z_done, i + 1)
                    need(act, z_out, 16 * pair)
                    nc.scalar.activation(zt[:, t], pz[i % 2][:, 0:2 * DI], ACT.Silu).then_inc(z_ready, 1)

            def silu_conv(pair):
                for kind in range(KIND):
                    act.wait_ge(conv_step, (pair * KIND + kind + 1) * 9)
                    need(act, u_out, 32 * pair)
                    need(act, xct_ready, KIND * pair)
                    need(act, xd_done, DIRS * pair)
                    nc.scalar.activation(xc[:, kind], acc[:, kind], ACT.Silu, bias=conv_p[:, kind, 9:10]).then_inc(xc_ready, 1)

            def split(pair):
                for k in range(DIRS):
                    i = xd(pair, k)
                    src = big[k % 2]
                    act.wait_ge(xd_done, i + 1)
                    need(act, bc_out[i % 2], 16 * 7 * (i // 2))
                    nc.scalar.copy(dts[2 * PR:P, i % 2], src[2 * PR:P, :])
                    nc.scalar.copy(hi[:, i % 2], src[0:2 * PR, :]).then_inc(hi_ready, 1)
                    act.wait_ge(rest_ready, i + 1)
                    nc.scalar.copy(mid[:, i % 2], rest[:]).then_inc(mid_ready, 1)

            act.wait_ge(weights_in, 16 * 5)
            copy_xt(0)
            root(0)
            fill_xpad(0)
            silu_z(0)
            copy_xt(1)
            silu_conv(0)
            root(1)
            split(0)
            fill_xpad(1)
            silu_z(1)
            silu_conv(1)
            split(1)

        @block.vector
        def _(dve):
            chain = ctx.enter_context(nc.semaphore("h_chain"))
            links = [0]

            def link(ins):
                links[0] += 1
                ins.then_inc(chain, 1)
                dve.wait_ge(chain, links[0])

            link(nc.vector.memset(eps[:], 1e-5))

            def normalise(pair):
                for b in (2 * pair, 2 * pair + 1):
                    for c in range(NC):
                        dve.wait_ge(xt_ready, b * NC + c + 1)
                        for h, q in enumerate(halves()):
                            last = nc.vector.bn_stats(st[:, c, h], xt[:, b % 2, c, q])
                        link(last)
                        last = nc.vector.bn_aggr(mv[:, b, c], st[:, c].rearrange("p a s -> p (a s)"))
                    last.then_inc(stats, 1)
                    dve.wait_ge(stats, 2 * b + 1)
                    dve.wait_ge(sums, 2 * b + 1)
                    link(nc.vector.tensor_copy(gmean[:, b], pst[:, b * 2 * NC:(b * 2 + 1) * NC]))
                    link(nc.vector.tensor_tensor(dev[:, b], mv[:, b, :, 0], gmean[:, b], ALU.subtract))
                    link(nc.vector.tensor_tensor(dev[:, b], dev[:, b], dev[:, b], ALU.mult))
                    nc.vector.tensor_tensor(chan_var[:, b], mv[:, b, :, 1], dev[:, b], ALU.add).then_inc(stats, 1)
                    dve.wait_ge(std_ready, b + 1)
                    link(nc.vector.reciprocal(rstd[:, b], std[:, b]))
                    need(dve, z_done, TT * pair)
                    for c in range(NC):
                        last = nc.vector.tensor_scalar(xn[:, b % 2, c], xt[:, b % 2, c], gmean[:, b, c:c + 1],
                                                       rstd[:, b, c:c + 1], ALU.subtract, ALU.mult)
                    last.then_inc(xn_ready, 1)

            def convolve(pair):
                for kind in range(KIND):
                    dve.wait_ge(xpad_ready, pair * KIND + kind + 1)
                    need(dve, xc_ready, KIND * pair)
                    out = acc[:, kind].rearrange("p (h w) -> p h w", h=HW)
                    for tap in range(9):
                        view = xpad[:, kind, tap // 3:tap // 3 + HW, tap % 3:tap % 3 + HW]
                        w = conv_p[:, kind, tap:tap + 1]
                        at = (pair * KIND + kind) * 9 + tap
                        if tap == 0:
                            nc.vector.tensor_scalar(out, view, w, None, ALU.mult).then_inc(conv_step, 1)
                        else:
                            dve.wait_ge(conv_step, at)
                            nc.vector.scalar_tensor_tensor(out, view, w, out, ALU.mult, ALU.add).then_inc(conv_step, 1)

            def split(pair):
                for k in range(DIRS):
                    i = xd(pair, k)
                    dve.wait_ge(hi_ready, i + 1)
                    need(dve, lo_ready, i)
                    nc.vector.tensor_tensor(rest[:], big[k % 2][0:2 * PR, :], hi[:, i % 2], ALU.subtract).then_inc(rest_ready, 1)
                    dve.wait_ge(mid_ready, i + 1)
                    nc.vector.tensor_tensor(lo[:, i % 2], rest[:], mid[:, i % 2], ALU.subtract).then_inc(lo_ready, 1)

            dve.wait_ge(weights_in, 16 * 5)
            normalise(0)
            convolve(0)
            normalise(1)
            split(0)
            convolve(1)
            split(1)

        @block.gpsimd
        def _(pool):
            nc.gpsimd.memset(xpad[:], 0.0).then_inc(borders, 1)
            for pair in range(PAIRS):
                for kind in range(KIND):
                    pool.wait_ge(xc_ready, pair * KIND + kind + 1)
                    need(pool, u_out, 32 * pair)
                    need(pool, xd_done, DIRS * pair)
                    nc.gpsimd.tensor_copy(xct[:, kind].rearrange("p (w h) -> p h w", w=HW),
                                          xc[:, kind].rearrange("p (h w) -> p h w", h=HW)).then_inc(xct_ready, 1)


def scan(nc, d, keep):
    with ExitStack() as ctx:
        def sb(name, shape, dt=F32):
            return ctx.enter_context(nc.sbuf_tensor("s_" + name, shape, dt))

        def sem(name):
            return ctx.enter_context(nc.semaphore("s_" + name))

        eye = keep["eye"]
        bc = sb("bc", [PIECES * PR, 2, 2, L], BF16)
        pick = sb("pick", [PIECES * PR, 2, N * P], BF16)
        dtr = sb("dtr", [2 * PR, 2, L])
        wdt = sb("wdt", [2 * PR, 2, P])
        par = sb("par", [P, 2, N + 3])
        u = sb("u", [P, 2, L])
        amin = sb("amin", [P, 2, N])
        aexp = sb("aexp", [P, 2, N])
        aneg = sb("aneg", [P, 2, N])
        dt_ = sb("dt", [P, 2, L])
        dtu = sb("dtu", [P, 2, L])
        ez = sb("ez", [P, L])
        rz = sb("rz", [P, L])
        lz = sb("lz", [P, L])
        qz = sb("qz", [P, L])
        a = sb("a", [P, RING, L])
        h = sb("h", [P, RING, L])
        hc = sb("hc", [P, HC_RING, L])
        du = sb("du", [P, L])
        crow = sb("crow", [P, RING, L])
        dsum = sb("dsum", [P, 1])
        yout = sb("yout", [P, L])
        pb = ctx.enter_context(nc.psum_tensor("s_pb", [P, 2, L], F32))
        pc = ctx.enter_context(nc.psum_tensor("s_pc", [P, L], F32))
        py = ctx.enter_context(nc.psum_tensor("s_py", [P, L], F32))

        dt_loads = [sem(f"dt_loads{i}") for i in range(2)]
        loads = [sem(f"loads{i}") for i in range(2)]
        b_row = sem("b_row")
        c_row = sem("c_row")
        crow_ready = sem("crow_ready")
        a_ready = sem("a_ready")
        b_ready = sem("b_ready")
        h_ready = sem("h_ready")
        hc_ready = sem("hc_ready")
        y_added = sem("y_added")
        y_taken = sem("y_taken")
        y_stored = sem("y_stored")
        z_done = sem("z_done")
        z_taken = sem("z_taken")
        e_ready = sem("e_ready")
        l_ready = sem("l_ready")
        q_ready = sem("q_ready")
        s_ready = sem("s_ready")
        s2_ready = sem("s2_ready")
        s3_ready = sem("s3_ready")
        dt_ready = sem("dt_ready")
        dtu_ready = sem("dtu_ready")
        amin_ready = sem("amin_ready")
        aexp_ready = sem("aexp_ready")
        a_neg_ready = sem("a_neg_ready")
        dsum_ready = sem("dsum_ready")
        skip_ready = sem("skip_ready")
        block = ctx.enter_context(nc.Block())

        def groups(eng, body):
            body(0, False)
            with eng.Fori(1, GROUPS - 1) as g:
                body(g, False)
            body(GROUPS - 1, True)

        def flow(s):
            return slice(None, None, -1) if s else slice(None)

        @block.sync
        def _(sp):
            def load(s, rows):
                bc_row, kind, dts_row, par_row, u_row = rows
                for dst, src, arrived in (
                    (dtr[:, s], d["dts_flat"][bass.ds(dts_row, 1)], dt_loads),
                    (wdt[:, s], d["wdt"][bass.ds(par_row, 1)], dt_loads),
                    (par[:, s], d["par"][bass.ds(par_row, 1)], dt_loads),
                    (u[:, s], d["u_flat"][bass.ds(u_row, 1)], loads),
                    (bc[:, s, 0], d["bc_flat"][bass.ds(bc_row, 1)], loads),
                    (bc[:, s, 1], d["bc_flat"][bass.ds(bc_row + 1, 1)], loads),
                    (pick[:, s], d["pick"][bass.ds(kind, 1)], loads),
                ):
                    sp.dma_start(dst, src.rearrange("a p l -> p (a l)")).then_inc(arrived[s], 16)

            def rows_of(g, s):
                po, kind = g // KIND, g % KIND
                pair, k = po // 2, po % 2 + 2 * s
                return (pair * DIRS + k) * 2, kind, pair * DIRS + k, k * KIND + kind, g

            for s in range(2):
                load(s, rows_of(0, s))
            with sp.Fori(1, GROUPS) as g:
                rows = [[sp.snap(v) for v in rows_of(g, s)] for s in range(2)]
                last_y = sp.snap(g - 1)
                steps = [sp.snap(g * GROUP - GROUP + (s + 1) * UNIT) for s in range(2)]
                for s in range(2):
                    sp.wait_ge(h_ready, steps[s])
                    sp.wait_ge(c_row, steps[s])
                    if s == 1:
                        sp.wait_ge(skip_ready, g)
                    load(s, rows[s])
                sp.wait_ge(y_taken, g)
                sp.dma_start(d["y_flat"][bass.ds(last_y, 1)].rearrange("a p l -> p (a l)"), yout[:]).then_inc(y_stored, 16)
            sp.wait_ge(y_taken, GROUPS)
            sp.dma_start(d["y_flat"][bass.ds(GROUPS - 1, 1)].rearrange("a p l -> p (a l)"), yout[:]).then_inc(y_stored, 16)
            sp.wait_ge(y_stored, 16 * GROUPS)

        DT_LOADED, LOADED = 16 * 3, 16 * 4

        @block.tensor
        def _(pe):
            def dt_product(g, s):
                pe.wait_ge(dt_loads[s], (g + 1) * DT_LOADED)
                for q in halves():
                    mm = pe.matmul(pc[:, q], wdt[:, s], dtr[:, s, q], start=True, stop=True)
                mm.then_inc(z_done, 1)

            def add_y(g, j):
                step = g * GROUP + j
                n = j % GROUP
                pe.wait_ge(hc_ready, step + 1)
                if n == 0:
                    need(pe, y_taken, g)
                for q in halves():
                    mm = pe.matmul(py[:, q], eye[:], hc[:, n % HC_RING, q], start=(n == 0), stop=(n == GROUP - 1))
                mm.then_inc(y_added, 1)

            def spread_c(g, j, last=False):
                step = g * GROUP + j
                s, n = j // UNIT % 2, j % UNIT
                if n == 0:
                    pe.wait_ge(loads[s], (g + 1 + j // GROUP) * LOADED)
                need(pe, crow_ready, step)
                if n == PREP + AHEAD + 1 and not (last and s == 1):
                    pe.wait_ge(z_taken, g * 2 + j // UNIT + 2)
                for q in halves():
                    mm = pe.matmul(pc[:, q], pick[:, s, n * P:(n + 1) * P], bc[:, s, 1, q], start=True, stop=True)
                mm.then_inc(c_row, 1)

            def body(g, last):
                first = isinstance(g, int) and g == 0
                for j in range(GROUP):
                    s, n = j // UNIT, j % UNIT
                    step = g * GROUP + j
                    need(pe, h_ready, step - 1)
                    for q in halves():
                        mm = pe.matmul(pb[:, j % 2, q], pick[:, s, n * P:(n + 1) * P], bc[:, s, 0, q], start=True, stop=True)
                    mm.then_inc(b_row, 1)
                    prepare = n == PREP and not (last and s == 1)
                    if prepare:
                        spread_c(g, j + AHEAD, last)
                    if j >= LAG:
                        add_y(g, j - LAG)
                    elif not first:
                        if j < LAG - 1:
                            add_y(g, j - LAG)
                        if j == LAG - 2:
                            add_y(g, -1)
                    if not prepare and not (last and j + AHEAD >= GROUP):
                        spread_c(g, j + AHEAD, last)
                    if prepare:
                        pe.wait_ge(crow_ready, step + AHEAD + 1)
                        dt_product(g + s, 1 - s)

            dt_product(0, 0)
            pe.wait_ge(z_taken, 1)
            for j in range(AHEAD):
                spread_c(0, j)
            groups(pe, body)
            for j in range(GROUP - LAG, GROUP):
                add_y(GROUPS - 1, j)

        @block.scalar
        def _(act):
            def take_z(g, s, unit):
                act.wait_ge(z_done, unit + 1)
                act.wait_ge(dt_loads[s], (g + 1) * DT_LOADED)
                need(act, dt_ready, unit)
                nc.scalar.activation(ez[:], pc[:], ACT.Abs, bias=par[:, s, N:N + 1]).then_inc(e_ready, 1)
                nc.scalar.activation(rz[:], pc[:], ACT.Relu, bias=par[:, s, N:N + 1]).then_inc(z_taken, 1)

            def exp_z(unit, s):
                act.wait_ge(e_ready, 2 * unit + 1)
                nc.scalar.activation(ez[:], ez[:], ACT.Exp, scale=-1.0).then_inc(e_ready, 1)
                act.wait_ge(amin_ready, unit + 1)
                nc.scalar.activation(aexp[:, s], amin[:, s], ACT.Exp).then_inc(aexp_ready, 1)

            def ln_z(unit):
                act.wait_ge(e_ready, 2 * unit + 2)
                nc.scalar.activation(lz[:], ez[:], ACT.Ln, bias=1.0).then_inc(l_ready, 1)

            def decay(g, j):
                step = g * GROUP + j
                s, n = j // UNIT % 2, j % UNIT
                if n == 0:
                    act.wait_ge(dt_ready, g * 2 + j // UNIT + 1)
                    act.wait_ge(a_neg_ready, g * 2 + j // UNIT + 1)
                need(act, h_ready, step - RING + 1)
                nc.scalar.activation(a[:, j % RING], dt_[:, s], ACT.Exp, scale=aneg[:, s, n:n + 1]).then_inc(a_ready, 1)

            def take_c(g, j):
                step = g * GROUP + j
                need(act, hc_ready, step - RING + 1)
                act.wait_ge(c_row, step + 1)
                nc.scalar.copy(crow[:, j % RING], pc[:]).then_inc(crow_ready, 1)

            def body(g, last):
                for j in range(GROUP):
                    s, n = j // UNIT, j % UNIT
                    if not (last and j + AHEAD >= GROUP):
                        decay(g, j + AHEAD)
                        take_c(g, j + AHEAD)
                    if last and s == 1:
                        continue
                    if n == PREP:
                        take_z(g + s, 1 - s, g * 2 + s + 1)
                    if n == PREP + 1:
                        exp_z(g * 2 + s + 1, 1 - s)
                    if n == PREP + 2:
                        ln_z(g * 2 + s + 1)

            act.preload_act_table_set("natural_log_exp_and_others")
            take_z(0, 0, 0)
            exp_z(0, 0)
            for j in range(AHEAD):
                take_c(0, j)
            ln_z(0)
            for j in range(AHEAD):
                decay(0, j)
            groups(act, body)

        @block.vector
        def _(dve):
            def clamp_a(g, s, unit):
                dve.wait_ge(dt_loads[s], (g + 1) * DT_LOADED)
                nc.vector.tensor_scalar(amin[:, s], par[:, s, 0:N], LOG_MAX, None, ALU.min).then_inc(amin_ready, 1)

            def softplus_1(unit):
                dve.wait_ge(e_ready, 2 * unit + 2)
                nc.vector.tensor_scalar(qz[:], ez[:], 1.0, -1.0, ALU.add, ALU.add).then_inc(q_ready, 1)

            def softplus_2(unit, s):
                dve.wait_ge(q_ready, unit + 1)
                dve.wait_ge(l_ready, unit + 1)
                nc.vector.tensor_tensor(qz[:], lz[:], qz[:], ALU.subtract).then_inc(s_ready, 1)
                dve.wait_ge(aexp_ready, unit + 1)
                nc.vector.tensor_scalar(aneg[:, s], aexp[:, s], -1.0, None, ALU.mult).then_inc(a_neg_ready, 1)

            def softplus_3(unit):
                dve.wait_ge(s2_ready, unit + 1)
                nc.vector.scalar_tensor_tensor(lz[:], ez[:], LN2, qz[:], ALU.mult, ALU.max).then_inc(s3_ready, 1)

            def softplus_4(unit, s):
                dve.wait_ge(s3_ready, unit + 1)
                nc.vector.tensor_tensor(dt_[:, s], lz[:], rz[:], ALU.add).then_inc(dt_ready, 1)

            def take_y(g):
                dve.wait_ge(y_added, g * GROUP + GROUP)
                dve.wait_ge(skip_ready, g + 1)
                need(dve, y_stored, g * 16)
                nc.vector.tensor_tensor(yout[:], du[:], py[:], ALU.add).then_inc(y_taken, 1)

            def skip_part(g):
                dve.wait_ge(loads[1], (g + 1) * LOADED)
                nc.vector.tensor_tensor(dsum[:], par[:, 1, N + 1:N + 2], par[:, 1, N + 2:N + 3], ALU.add).then_inc(dsum_ready, 1)
                dve.wait_ge(dsum_ready, g + 1)
                need(dve, y_taken, g)
                nc.vector.tensor_scalar(du[:], u[:, 1], dsum[:], None, ALU.mult).then_inc(skip_ready, 1)

            def body(g, last):
                for j in range(GROUP):
                    s, n = j // UNIT, j % UNIT
                    step = g * GROUP + j
                    if n == 0:
                        dve.wait_ge(dtu_ready, g * 2 + s + 1)
                    if j == LAG - 1 and not (isinstance(g, int) and g == 0):
                        take_y(g - 1)
                    if j == GROUP - 1:
                        skip_part(g)
                    dve.wait_ge(b_row, step + 1)
                    nc.vector.tensor_tensor(pb[:, j % 2], dtu[:, s], pb[:, j % 2], ALU.mult).then_inc(b_ready, 1)
                    dve.wait_ge(b_ready, step + 1)
                    dve.wait_ge(a_ready, step + 1)
                    need(dve, hc_ready, step - RING + 1)
                    f = flow(s)
                    nc.vector.tensor_tensor_scan(h[:, j % RING, f], a[:, j % RING, f], pb[:, j % 2, f], 0.0, ALU.mult, ALU.add)\
                      .then_inc(h_ready, 1)
                    if last and s == 1:
                        continue
                    unit = g * 2 + s + 1
                    if n == PREP:
                        clamp_a(g + s, 1 - s, unit)
                    if n == PREP + 2:
                        softplus_1(unit)
                    if n == PREP + 4:
                        softplus_2(unit, 1 - s)
                    if n == PREP + 6:
                        softplus_3(unit)
                    if n == PREP + 8:
                        softplus_4(unit, 1 - s)

            clamp_a(0, 0, 0)
            softplus_1(0)
            softplus_2(0, 0)
            softplus_3(0)
            softplus_4(0, 0)
            groups(dve, body)
            take_y(GROUPS - 1)

        @block.gpsimd
        def _(pool):
            def add_e(unit):
                pool.wait_ge(s_ready, unit + 1)
                nc.gpsimd.tensor_tensor(qz[:], qz[:], ez[:], ALU.add).then_inc(s2_ready, 1)

            def times_u(g, unit, s):
                pool.wait_ge(loads[s], (g + 1) * LOADED)
                pool.wait_ge(dt_ready, unit + 1)
                nc.gpsimd.tensor_tensor(dtu[:, s], dt_[:, s], u[:, s], ALU.mult).then_inc(dtu_ready, 1)

            def body(g, last):
                for j in range(GROUP):
                    s, n = j // UNIT, j % UNIT
                    step = g * GROUP + j
                    pool.wait_ge(h_ready, step + 1)
                    pool.wait_ge(crow_ready, step + 1)
                    need(pool, y_added, step - HC_RING + 1)
                    nc.gpsimd.tensor_tensor(hc[:, j % HC_RING], h[:, j % RING], crow[:, j % RING], ALU.mult).then_inc(hc_ready, 1)
                    if last and s == 1:
                        continue
                    if n == PREP + 4:
                        add_e(g * 2 + s + 1)
                    if n == PREP + 8:
                        times_u(g + s, g * 2 + s + 1, 1 - s)

            add_e(0)
            times_u(0, 0, 0)
            groups(pool, body)


def tail(nc, d, keep):
    with ExitStack() as ctx:
        def sb(name, shape, dt=F32):
            return ctx.enter_context(nc.sbuf_tensor("t_" + name, shape, dt))

        def sem(name):
            return ctx.enter_context(nc.semaphore("t_" + name))

        eye, gavg, wout, gam, bet, wr, rb, w1, b1, w2, b2, spread, eyeb = (
            keep[k] for k in ("eye", "gavg", "wout", "gam", "bet", "wr", "rb", "w1", "b1", "w2", "b2", "spread", "eyeb"))
        y0 = sb("y0", [P, KIND, L])
        y1 = sb("y1", [P, KIND, L])
        yt = sb("yt", [P, TT, 2, DI])
        sz = sb("sz", [P, TT, 2, DI])
        gated = sb("gated", [P, TT, KIND, P])
        yg = sb("yg", [P, KIND, L])
        st = sb("st", [P, NC, 2, 6])
        ln_mv = sb("ln_mv", [P, TT, 2, 2])
        ln_st = sb("ln_st", [P, TT, 2, 6])
        ln_r = sb("ln_r", [P, TT, 2])
        mv = sb("mv", [P, NC, 2])
        gmean = sb("gmean", [P, NC])
        dev = sb("dev", [P, NC])
        chan_var = sb("chan_var", [P, NC])
        std = sb("std", [P, NC])
        rstd = sb("rstd", [P, NC])
        eps = sb("eps", [P, 1])
        xt = sb("xt", [P, NC, L])
        x1 = sb("x1", [P, 2, NC, L])
        xn = sb("xn", [P, 2, NC, L])
        pr = sb("pr", [P, TT, EXPERTS])
        ex = sb("ex", [P, TT, EXPERTS])
        ge = sb("ge", [P, TT, EXPERTS])
        rank = sb("rank", [P, TT, EXPERTS])
        comb = sb("comb", [P, TT, EXPERTS])
        left = sb("left", [P, TT, EXPERTS])
        red = sb("red", [P, TT])
        parts = sb("parts", [P, TT, PIECES, PR], BF16)
        combt = sb("combt", [PIECES * PR, L], BF16)
        b2_hi = sb("b2_hi", [PIECES * PR, C], BF16)
        b2_mid = sb("b2_mid", [PIECES * PR, C], BF16)
        b2_rest = sb("b2_rest", [PIECES * PR, C])
        b2_parts = sb("b2_parts", [PIECES * PR, C], BF16)
        hid = sb("hid", [P, NC, L])
        out = sb("out", [P, 4, C])
        big = [ctx.enter_context(nc.psum_tensor(f"t_big{i}", [P, L], F32)) for i in range(2)]
        small = [ctx.enter_context(nc.psum_tensor(f"t_small{i}", [P, BANK], F32)) for i in range(3)]
        stat = ctx.enter_context(nc.psum_tensor("t_stat", [P, BANK], F32))

        y0_in = sem("y0_in")
        y1_in = sem("y1_in")
        sz_in = sem("sz_in")
        xt_in = sem("xt_in")
        sum_ready = sem("sum_ready")
        yt_done = sem("yt_done")
        small_taken = sem("small_taken")
        ln_stat = sem("ln_stat")
        ln_std = sem("ln_std")
        yln = sem("yln")
        gate_ready = sem("gate_ready")
        back_done = sem("back_done")
        yg_ready = sem("yg_ready")
        op_done = sem("op_done")
        x1_ready = sem("x1_ready")
        stats = sem("stats")
        sums = sem("sums")
        std_ready = sem("std_ready")
        xn_ready = sem("xn_ready")
        lg_done = sem("lg_done")
        lg_ready = sem("lg_ready")
        ex_ready = sem("ex_ready")
        comb_ready = sem("comb_ready")
        ct_done = sem("ct_done")
        f1_done = sem("f1_done")
        gelu_ready = sem("gelu_ready")
        sp_done = sem("sp_done")
        hw_ready = sem("hw_ready")
        f2_done = sem("f2_done")
        b2_ready = sem("b2_ready")
        out_stored = [sem(f"out_stored{i}") for i in range(4)]
        block = ctx.enter_context(nc.Block())

        def stage(b):
            nxt = b + 1 < BATCH
            steps = [("LG", b), ("F1", b, 0)]
            steps += [("STA", b + 1)] if nxt else []
            steps += [("F1", b, 1)]
            steps += [("STB", b + 1)] if nxt else []
            steps += [("CT", b), ("SP", b, 0), ("F1", b, 2), ("SP", b, 1), ("SP", b, 2)]
            steps += [("F2", b, t) for t in range(TT)]
            steps += [("BK", 1, k) for k in range(KIND)] if b == 0 else []
            steps += [("OP", b + 2, c) for c in range(NC)] if b + 2 < BATCH else []
            return steps

        order = [("YT", 0, t) for t in range(TT)] + [("BK", 0, k) for k in range(KIND)]
        order += [("OP", 0, c) for c in range(NC)]
        order += [("OP", 1, 0), ("STA", 0), ("OP", 1, 1), ("STB", 0), ("OP", 1, 2)]
        order += [("YT", 1, t) for t in range(TT)]
        for b in range(BATCH):
            order += stage(b)
        large = [s for s in order if s[0] in ("BK", "OP", "F1", "SP")]
        little = [s for s in order if s[0] in ("YT", "CT", "F2")]

        def big_of(*step):
            return big[large.index(step) % 2]

        def small_of(*step):
            return small[little.index(step) % 3]

        def emptied(step):
            kind, b, i = step
            return {"BK": (yg_ready, b * KIND + i + 1), "OP": (x1_ready, b * NC + i + 1),
                    "F1": (gelu_ready, b * NC + i + 1), "SP": (hw_ready, b * NC + i + 1)}[kind]

        @block.sync
        def _(sp):
            for pair in range(PAIRS):
                at = pair * 2 * KIND
                need(sp, yt_done, TT * pair)
                sp.dma_start(y0[:], d["y_flat"][at:at + KIND].rearrange("t p l -> p t l")).then_inc(y0_in, 16)
                need(sp, sum_ready, KIND * pair)
                sp.dma_start(y1[:], d["y_flat"][at + KIND:at + 2 * KIND].rearrange("t p l -> p t l")).then_inc(y1_in, 16)
                need(sp, gate_ready, pair)
                sp.dma_start(sz[:].rearrange("p t b c -> p t (b c)"), d["sz"][pair]).then_inc(sz_in, 16)
                if pair == 0:
                    for b in range(2):
                        need(sp, x1_ready, NC * b)
                        sp.dma_start(xt[:], d["xt"][b].rearrange("c p l -> p c l")).then_inc(xt_in, 16)
            for b in range(BATCH):
                for t in range(TT):
                    i = b * TT + t
                    sp.wait_ge(small_taken, little.index(("F2", b, t)) + 1)
                    sp.dma_start(d["out"][b, t * P:(t + 1) * P, :], out[:, i % 4]).then_inc(out_stored[i % 4], 16)
                    if t == 0 and b + 2 < BATCH:
                        sp.wait_ge(x1_ready, NC * (b + 2))
                        sp.dma_start(xt[:], d["xt"][b + 2].rearrange("c p l -> p c l")).then_inc(xt_in, 16)
            for i in range(4):
                sp.wait_ge(out_stored[i], 16 * BATCH * TT // 4)

        @block.tensor
        def _(pe):
            def y_to_tokens(pair, t):
                if t == 0:
                    pe.wait_ge(sum_ready, KIND * (pair + 1))
                for kind in range(KIND):
                    mm = pe.transpose(small_of("YT", pair, t)[:, kind * P:(kind + 1) * P], y0[:, kind, t * P:(t + 1) * P], eye[:])
                mm.then_inc(yt_done, 1)

            def gated_back(pair, kind):
                pe.wait_ge(gate_ready, pair + 1)
                for t in range(TT):
                    mm = pe.transpose(big_of("BK", pair, kind)[:, t * P:(t + 1) * P], gated[:, t, kind], eye[:])
                mm.then_inc(back_done, 1)

            def out_proj(b, c):
                pair, o = b // 2, b % 2
                r = slice(o * HALF, (o + 1) * HALF)
                pe.wait_ge(yg_ready, KIND * (pair + 1))
                for q in halves():
                    buf = big_of("OP", b, c)[:, q]
                    pe.matmul(buf, wout[:, 0, c * P:(c + 1) * P], yg[:, o, q], start=True, stop=False)
                    mm = pe.matmul(buf, wout[r, 1, c * P:(c + 1) * P], yg[r, 2, q], start=False, stop=True)
                mm.then_inc(op_done, 1)

            def average(b, step):
                pe.wait_ge(stats, 2 * b + step + 1)
                need(pe, lg_ready, b)
                for co in range(NC):
                    for ci in range(NC):
                        rhs = mv[:, ci, 0:1] if step == 0 else chan_var[:, ci:ci + 1]
                        col = step * NC + co
                        mm = pe.matmul(stat[:, col:col + 1], gavg[:, ci * NC + co], rhs, start=(ci == 0), stop=(ci == NC - 1))
                mm.then_inc(sums, 1)

            def logits(b):
                pe.wait_ge(xn_ready, b + 1)
                for t in range(TT):
                    for c in range(NC):
                        mm = pe.matmul(stat[:, 64 + t * EXPERTS:64 + (t + 1) * EXPERTS], xn[:, b % 2, c, t * P:(t + 1) * P], wr[:, c],
                                       start=(c == 0), stop=(c == NC - 1))
                mm.then_inc(lg_done, 1)

            def first_layer(b, j):
                for q in halves():
                    for c in range(NC):
                        mm = pe.matmul(big_of("F1", b, j)[:, q], w1[:, c, j * P:(j + 1) * P], xn[:, b % 2, c, q],
                                       start=(c == 0), stop=(c == NC - 1))
                mm.then_inc(f1_done, 1)

            def turn_weights(b):
                pe.wait_ge(comb_ready, b + 1)
                buf = small_of("CT", b)[:].bitcast(BF16)
                for t in range(TT):
                    mm = pe.transpose(buf[0:PIECES * PR, t * P:(t + 1) * P], parts[:, t].rearrange("p a r -> p (a r)"), eyeb[:])
                mm.then_inc(ct_done, 1)

            def spread_weights(b, j):
                pe.wait_ge(small_taken, little.index(("CT", b)) + 1)
                for q in halves():
                    mm = pe.matmul(big_of("SP", b, j)[:, q], spread[:, j * P:(j + 1) * P], combt[0:PR, q], start=True, stop=True)
                mm.then_inc(sp_done, 1)

            def second_layer(b, t):
                if t == 0:
                    pe.wait_ge(hw_ready, NC * (b + 1))
                    pe.wait_ge(b2_ready, 5)
                tok = slice(t * P, (t + 1) * P)
                ps = small_of("F2", b, t)[:, 0:C]
                pe.matmul(ps, combt[:, tok], b2_parts[:], start=True, stop=False, skip_group_check=True)
                for j in range(NC):
                    pe.matmul(ps, hid[:, j, tok], w2[:, j], start=False, stop=False, skip_group_check=True)
                for c in range(NC):
                    mm = pe.matmul(ps[:, c * P:(c + 1) * P], x1[:, b % 2, c, tok], eye[:], start=False, stop=(c == NC - 1),
                                   skip_group_check=True)
                mm.then_inc(f2_done, 1)

            work = {"YT": y_to_tokens, "BK": gated_back, "OP": out_proj, "STA": lambda b: average(b, 0),
                    "STB": lambda b: average(b, 1), "LG": logits, "F1": first_layer, "CT": turn_weights,
                    "SP": spread_weights, "F2": second_layer}
            for step in order:
                if step in large and large.index(step) >= 2:
                    pe.wait_ge(*emptied(large[large.index(step) - 2]))
                if step in little and little.index(step) >= 3:
                    pe.wait_ge(small_taken, little.index(step) - 2)
                work[step[0]](*step[1:])

        @block.scalar
        def _(act):
            def take_yt(pair):
                for t in range(TT):
                    act.wait_ge(yt_done, pair * TT + t + 1)
                    need(act, gate_ready, pair)
                    src = small_of("YT", pair, t)
                    nc.scalar.copy(yt[:, t, :, 0:P], src[:, 0:2 * P].rearrange("p (b c) -> p b c", b=2))
                    nc.scalar.copy(yt[:, t, :, P:DI], src[:, 2 * P:3 * P].rearrange("p (b c) -> p b c", b=2)).then_inc(small_taken, 1)

            def root_ln(pair):
                act.wait_ge(ln_stat, pair + 1)
                nc.scalar.activation(ln_r[:], ln_mv[:, :, :, 1], ACT.Sqrt, bias=eps[:]).then_inc(ln_std, 1)

            def take_back(pair):
                need(act, op_done, 2 * NC * pair)
                for kind in range(KIND):
                    act.wait_ge(back_done, pair * KIND + kind + 1)
                    nc.scalar.copy(yg[:, kind], big_of("BK", pair, kind)[:]).then_inc(yg_ready, 1)

            def root(b):
                act.wait_ge(sums, 2 * b + 2)
                nc.scalar.activation(std[:], stat[:, NC:2 * NC], ACT.Sqrt, bias=eps[:]).then_inc(std_ready, 1)

            def exp_logits(b):
                act.wait_ge(lg_ready, b + 1)
                nc.scalar.activation(ex[:], pr[:], ACT.Exp).then_inc(ex_ready, 1)

            def gelu(b, j):
                act.wait_ge(f1_done, NC * b + j + 1)
                if j == 0:
                    need(act, f2_done, TT * b)
                nc.scalar.activation(hid[:, j], big_of("F1", b, j)[:], ACT.Gelu, bias=b1[:, j:j + 1]).then_inc(gelu_ready, 1)

            def take_weights(b):
                act.wait_ge(ct_done, b + 1)
                nc.scalar.copy(combt[:], small_of("CT", b)[0:PIECES * PR].bitcast(BF16)).then_inc(small_taken, 1)

            def take_out(b):
                for t in range(TT):
                    i = b * TT + t
                    act.wait_ge(f2_done, i + 1)
                    need(act, out_stored[i % 4], 16 * (i // 4))
                    nc.scalar.copy(out[:, i % 4], small_of("F2", b, t)[:, 0:C]).then_inc(small_taken, 1)

            take_yt(0)
            root_ln(0)
            take_back(0)
            root(0)
            take_yt(1)
            for b in range(BATCH):
                exp_logits(b)
                gelu(b, 0)
                gelu(b, 1)
                if b + 1 < BATCH:
                    root(b + 1)
                if b == 0:
                    root_ln(1)
                take_weights(b)
                gelu(b, 2)
                take_out(b)
                if b == 0:
                    take_back(1)

        def add_orientations(eng, tt, pair):
            for kind in range(KIND):
                eng.wait_ge(y0_in, 16 * (pair + 1))
                eng.wait_ge(y1_in, 16 * (pair + 1))
                whole = y0[:, kind].rearrange("p (h w) -> p h w", h=HW)
                tt(whole, whole, y1[:, kind].rearrange("p (w h) -> p h w", w=HW), ALU.add).then_inc(sum_ready, 1)

        def scale_and_gate(eng, tt, pair):
            flat = yt[:].rearrange("p t b c -> p (t b) c")
            eng.wait_ge(yln, 3 * pair + 1)
            tt(flat, flat, gam[:].unsqueeze(1).broadcast_to([P, 2 * TT, DI]), ALU.mult).then_inc(yln, 1)
            eng.wait_ge(yln, 3 * pair + 2)
            tt(flat, flat, bet[:].unsqueeze(1).broadcast_to([P, 2 * TT, DI]), ALU.add).then_inc(yln, 1)
            eng.wait_ge(yln, 3 * pair + 3)
            eng.wait_ge(sz_in, 16 * (pair + 1))
            need(eng, back_done, KIND * pair)
            tt(gated[:, :, 0:2], yt[:, :, :, 0:P], sz[:, :, :, 0:P], ALU.mult)
            tt(gated[:, :, 2].rearrange("p t (b c) -> p t b c", b=2), yt[:, :, :, P:DI], sz[:, :, :, P:DI],
               ALU.mult).then_inc(gate_ready, 1)

        @block.gpsimd
        def _(pool):
            add_orientations(pool, nc.gpsimd.tensor_tensor, 1)
            scale_and_gate(pool, nc.gpsimd.tensor_tensor, 1)

        @block.vector
        def _(dve):
            chain = ctx.enter_context(nc.semaphore("t_chain"))
            links = [0]

            def link(ins):
                links[0] += 1
                ins.then_inc(chain, 1)
                dve.wait_ge(chain, links[0])

            V = nc.vector

            def ln_stats(pair):
                for t in range(TT):
                    dve.wait_ge(small_taken, little.index(("YT", pair, t)) + 1)
                    for b in range(2):
                        last = V.bn_stats(ln_st[:, t, b], yt[:, t, b])
                link(last)
                for t in range(TT):
                    for b in range(2):
                        last = V.bn_aggr(ln_mv[:, t, b], ln_st[:, t, b])
                last.then_inc(ln_stat, 1)

            def ln_apply(pair):
                dve.wait_ge(ln_std, pair + 1)
                dve.wait_ge(ln_stat, pair + 1)
                link(V.reciprocal(ln_r[:], ln_r[:]))
                for t in range(TT):
                    for b in range(2):
                        last = V.tensor_scalar(yt[:, t, b], yt[:, t, b], ln_mv[:, t, b, 0:1], ln_r[:, t, b:b + 1], ALU.subtract, ALU.mult)
                last.then_inc(yln, 1)

            def residual(b, c):
                dve.wait_ge(xt_in, 16 * (b + 1))
                need(dve, f2_done, TT * (b - 1))
                dve.wait_ge(op_done, NC * b + c + 1)
                V.tensor_tensor(x1[:, b % 2, c], xt[:, c], big_of("OP", b, c)[:], ALU.add).then_inc(x1_ready, 1)
                dve.wait_ge(x1_ready, NC * b + c + 1)
                for h, q in enumerate(halves()):
                    last = V.bn_stats(st[:, c, h], x1[:, b % 2, c, q])
                link(last)
                last = V.bn_aggr(mv[:, c], st[:, c].rearrange("p a s -> p (a s)"))
                if c == NC - 1:
                    last.then_inc(stats, 1)

            def group_means(b):
                dve.wait_ge(stats, 2 * b + 1)
                dve.wait_ge(sums, 2 * b + 1)
                link(V.tensor_copy(gmean[:], stat[:, 0:NC]))
                link(V.tensor_tensor(dev[:], mv[:, :, 0], gmean[:], ALU.subtract))
                link(V.tensor_tensor(dev[:], dev[:], dev[:], ALU.mult))
                V.tensor_tensor(chan_var[:], mv[:, :, 1], dev[:], ALU.add).then_inc(stats, 1)

            def normalise(b):
                dve.wait_ge(std_ready, b + 1)
                link(V.reciprocal(rstd[:], std[:]))
                need(dve, f1_done, NC * (b - 1))
                for c in range(NC):
                    last = V.tensor_scalar(xn[:, b % 2, c], x1[:, b % 2, c], gmean[:, c:c + 1], rstd[:, c:c + 1], ALU.subtract, ALU.mult)
                last.then_inc(xn_ready, 1)

            def route(b):
                def wide(x):
                    return x.unsqueeze(2).broadcast_to([P, TT, EXPERTS])

                dve.wait_ge(lg_done, b + 1)
                lg = stat[:, 64:64 + TT * EXPERTS].rearrange("p (t e) -> p t e", e=EXPERTS)
                link(V.tensor_tensor(pr[:], lg, rb[:].unsqueeze(1).broadcast_to([P, TT, EXPERTS]), ALU.add))
                link(V.tensor_reduce(red[:], pr[:], AX_X, ALU.max))
                V.tensor_tensor(pr[:], pr[:], wide(red[:]), ALU.subtract).then_inc(lg_ready, 1)
                dve.wait_ge(ex_ready, b + 1)
                link(V.tensor_reduce(red[:], ex[:], AX_X, ALU.add))
                link(V.reciprocal(red[:], red[:]))
                link(V.tensor_tensor(pr[:], ex[:], wide(red[:]), ALU.mult))
                link(V.memset(rank[:], 0.0))
                for gap in range(1, EXPERTS):
                    m = EXPERTS - gap
                    link(V.tensor_tensor(ge[:, :, 0:m], pr[:, :, 0:m], pr[:, :, gap:EXPERTS], ALU.is_ge))
                    link(V.tensor_tensor(rank[:, :, gap:EXPERTS], rank[:, :, gap:EXPERTS], ge[:, :, 0:m], ALU.add))
                    link(V.tensor_tensor(rank[:, :, 0:m], rank[:, :, 0:m], ge[:, :, 0:m], ALU.subtract))
                    link(V.tensor_scalar(rank[:, :, 0:m], rank[:, :, 0:m], 1.0, None, ALU.add))
                link(V.tensor_scalar(rank[:], rank[:], 1.5, None, ALU.is_lt))
                link(V.tensor_tensor(pr[:], pr[:], rank[:], ALU.mult))
                link(V.tensor_reduce(red[:], pr[:], AX_X, ALU.add))
                link(V.tensor_scalar(red[:], red[:], 1e-8, None, ALU.add))
                link(V.reciprocal(red[:], red[:]))
                link(V.tensor_tensor(comb[:], pr[:], wide(red[:]), ALU.mult))
                need(dve, ct_done, b)
                E4 = EXPERTS
                link(V.tensor_copy(parts[:, :, 0, 0:E4], comb[:]))
                link(V.tensor_tensor(left[:], comb[:], parts[:, :, 0, 0:E4], ALU.subtract))
                link(V.tensor_copy(parts[:, :, 0, E4:2 * E4], left[:]))
                link(V.tensor_tensor(parts[:, :, 0, 2 * E4:3 * E4], left[:], parts[:, :, 0, E4:2 * E4], ALU.subtract))
                V.tensor_copy(parts[:, :, 1, 0:3 * E4], parts[:, :, 0, 0:3 * E4])
                V.tensor_copy(parts[:, :, 2, 0:3 * E4], parts[:, :, 0, 0:3 * E4]).then_inc(comb_ready, 1)

            def weigh(b, j):
                dve.wait_ge(gelu_ready, NC * b + j + 1)
                dve.wait_ge(sp_done, NC * b + j + 1)
                V.tensor_tensor(hid[:, j], hid[:, j], big_of("SP", b, j)[:], ALU.mult).then_inc(hw_ready, 1)

            def split_b2():
                V.tensor_copy(b2_hi[:], b2[:]).then_inc(b2_ready, 1)
                dve.wait_ge(b2_ready, 1)
                V.tensor_tensor(b2_rest[:], b2[:], b2_hi[:], ALU.subtract).then_inc(b2_ready, 1)
                dve.wait_ge(b2_ready, 2)
                V.tensor_copy(b2_mid[:], b2_rest[:]).then_inc(b2_ready, 1)
                dve.wait_ge(b2_ready, 3)
                V.tensor_tensor(b2_parts[:], b2_rest[:], b2_mid[:], ALU.subtract).then_inc(b2_ready, 1)
                dve.wait_ge(b2_ready, 4)
                V.tensor_copy(b2_parts[0:PR], b2_hi[0:PR])
                V.tensor_copy(b2_parts[PR:2 * PR], b2_mid[PR:2 * PR]).then_inc(b2_ready, 1)

            V.memset(parts[:], 0.0)
            link(V.memset(eps[:], 1e-5))
            split_b2()
            add_orientations(dve, V.tensor_tensor, 0)
            ln_stats(0)
            ln_apply(0)
            scale_and_gate(dve, V.tensor_tensor, 0)
            for c in range(NC):
                residual(0, c)
            group_means(0)
            residual(1, 0)
            normalise(0)
            residual(1, 1)
            residual(1, 2)
            for b in range(BATCH):
                route(b)
                if b == 0:
                    ln_stats(1)
                if b + 1 < BATCH:
                    group_means(b + 1)
                    normalise(b + 1)
                for j in range(NC):
                    weigh(b, j)
                if b == 0:
                    ln_apply(1)
                if b + 2 < BATCH:
                    for c in range(NC):
                        residual(b + 2, c)


def kept(nc, ctx, d):
    def sb(name, shape, dt=F32):
        return ctx.enter_context(nc.sbuf_tensor("k_" + name, shape, dt))

    keep = dict(
        eye=sb("eye", [P, P]), eyeb=sb("eyeb", [P, P], BF16), gavg=sb("gavg", [P, NC * NC, P]),
        wout=sb("wout", [P, 2, C]),
        gam=sb("gam", [P, DI]), bet=sb("bet", [P, DI]), wr=sb("wr", [P, NC, EXPERTS]), rb=sb("rb", [P, EXPERTS]),
        w1=sb("w1", [P, NC, C]), b1=sb("b1", [P, NC]), w2=sb("w2", [P, NC, C]), b2=sb("b2", [PIECES * PR, C]),
        spread=sb("spread", [PR, C], BF16),
    )
    from_dram = dict(wout=d["wout"], gam=d["ln_g"].partition_broadcast(P), bet=d["ln_b"].partition_broadcast(P), wr=d["wr"],
                     rb=d["rb"].partition_broadcast(P), w1=d["w1"], b1=d["b1"], w2=d["w2"], b2=d["b2"], spread=d["spread"],
                     eyeb=d["eyeb"])
    return keep, from_dram


def bass_vision_mamba_moe(nc, x, eye, win, wx, gavg, conv_p, pick, wdt, par, wout, ln_g, ln_b, wr, rb, w1, b1, w2, b2, spread, eyeb, out):
    def scratch(name, shape, dt=F32):
        return nc.dram_tensor("scratch_" + name, shape, dt, kind="Internal").ap()

    bc = scratch("bc", (PAIRS, DIRS, 2, PIECES * PR, L), BF16)
    dts = scratch("dts", (PAIRS, DIRS, 2 * PR, L))
    u = scratch("u", (PAIRS, 2, KIND, P, L))
    d = dict(
        x=x.rearrange("b h w c -> b (h w) c"), eye=eye, win=win, wx=wx, gavg=gavg, conv_p=conv_p, pick=pick, wdt=wdt,
        par=par, wout=wout, ln_g=ln_g, ln_b=ln_b, wr=wr, rb=rb, w1=w1, b1=b1, w2=w2, b2=b2, spread=spread, eyeb=eyeb,
        out=out.rearrange("b h w c -> b (h w) c"),
        xt=scratch("xt", (BATCH, NC, P, L)), sz=scratch("sz", (PAIRS, P, TT, 2 * DI)),
        bc=bc, dts=dts, u=u, y_flat=scratch("y", (GROUPS, P, L)),
        bc_flat=bc.rearrange("a k m r l -> (a k m) r l"), dts_flat=dts.rearrange("a k r l -> (a k) r l"),
        u_flat=u.rearrange("a o t p l -> (a o t) p l"),
    )
    with ExitStack() as ctx:
        keep, keep_from = kept(nc, ctx, d)
        head(nc, d, keep, keep_from)
        scan(nc, d, keep)
        tail(nc, d, keep)


def lay_out(np, a):
    f = np.float32
    kinds = [(0, 0, P), (1, 0, P), (2, 0, 0)]
    o = {}
    o["eye"] = np.eye(P, dtype=f)
    chunk = lambda w: np.ascontiguousarray(w.reshape(NC, P, -1).transpose(1, 0, 2))
    o["win"] = chunk(a["L0_conv_in_proj_w"].T)

    def by_kind(w):
        w = np.moveaxis(w, -1, 0)
        return np.stack([w[0:P], w[0:P], np.concatenate([w[P:], w[P:]])])

    wx = np.zeros((DIRS, KIND, P, P), f)
    xw = a["L0_conv_x_proj_w"]
    for kind in range(KIND):
        for b in range(2):
            if kind != 2 and kind != b:
                continue
            rows = slice(0, P) if kind < 2 else slice(b * HALF, (b + 1) * HALF)
            ch = slice(0, P) if kind < 2 else slice(P, DI)
            w = xw[:, :, ch].transpose(0, 2, 1)
            wx[:, kind, rows, b * N:(b + 1) * N] = w[:, :, R:R + N]
            wx[:, kind, rows, PR + b * N:PR + (b + 1) * N] = w[:, :, R + N:]
            wx[:, kind, rows, (2 + b) * PR:(2 + b) * PR + R] = w[:, :, 0:R]
    o["wx"] = np.ascontiguousarray(wx.reshape(DIRS * KIND, P, P).transpose(1, 0, 2))
    ch = np.arange(C) // (C // 32)
    g = (ch[:, None] == ch[None, :]).astype(f) / f(C // 32)
    o["gavg"] = np.ascontiguousarray(g.reshape(NC, P, NC, P).transpose(1, 0, 2, 3).reshape(P, NC * NC, P))
    cp = np.concatenate([by_kind(a["L0_conv_conv_w"].reshape(DI, 9).T), by_kind(a["L0_conv_conv_b"][None])], -1)
    o["conv_p"] = np.ascontiguousarray(cp.transpose(1, 0, 2))
    pick = np.zeros((KIND, PIECES, 2, N, N, P), f)
    for kind in range(KIND):
        for b in range(2):
            cols = slice(0, P) if kind == b else slice(b * HALF, (b + 1) * HALF) if kind == 2 else slice(0, 0)
            for n in range(N):
                pick[kind, :, b, n, n, cols] = 1
    o["pick"] = pick.reshape(KIND, PIECES * PR, N * P).astype(np.dtype("bfloat16"))
    wdt = np.zeros((DIRS, KIND, 2 * PR, P), f)
    dw = a["L0_conv_dt_projs_w"].transpose(0, 2, 1)
    wdt[:, 0, 0:R] = dw[:, :, 0:P]
    wdt[:, 1, PR:PR + R] = dw[:, :, 0:P]
    wdt[:, 2, 0:R, 0:HALF] = dw[:, :, P:]
    wdt[:, 2, PR:PR + R, HALF:] = dw[:, :, P:]
    o["wdt"] = wdt.reshape(DIRS * KIND, 2 * PR, P)
    par = np.zeros((DIRS, KIND, P, N + 3), f)
    logs = a["L0_conv_A_logs"].reshape(DIRS, DI, N)
    skips = a["L0_conv_Ds"].reshape(DIRS, DI)
    for k in range(DIRS):
        par[k, :, :, 0:N] = by_kind(logs[k].T)
        par[k, :, :, N] = by_kind(a["L0_conv_dt_projs_b"][k])
        par[k, :, :, N + 1] = by_kind(skips[k % 2])
        par[k, :, :, N + 2] = by_kind(skips[k % 2 + 2])
    o["par"] = par.reshape(DIRS * KIND, P, N + 3)
    wo = a["L0_conv_out_proj_w"].T
    o["wout"] = np.ascontiguousarray(np.stack([wo[0:P], np.concatenate([wo[P:], wo[P:]])], 1))
    o["ln_g"], o["ln_b"] = a["L0_conv_out_norm_g"], a["L0_conv_out_norm_b"]
    o["wr"] = chunk(a["L1_conv_router_w"].T)
    o["rb"] = a["L1_conv_router_b"]
    o["w1"] = chunk(a["L1_conv_fc1_w"].reshape(C, C).T)
    o["b1"] = np.ascontiguousarray(a["L1_conv_fc1_b"].reshape(NC, P).T)
    o["w2"] = chunk(a["L1_conv_fc2_w"].transpose(0, 2, 1).reshape(C, C))
    b2 = np.zeros((PIECES, PR, C), f)
    b2[:, 0:PIECES * EXPERTS] = np.tile(a["L1_conv_fc2_b"], (PIECES, 1))
    o["b2"] = b2.reshape(PIECES * PR, C)
    e = np.arange(C) // HID
    spread = np.zeros((PR, C), f)
    spread[0:PIECES * EXPERTS] = np.tile(np.arange(EXPERTS)[:, None] == e[None, :], (PIECES, 1))
    o["spread"] = spread.astype(np.dtype("bfloat16"))
    o["eyeb"] = o["eye"].astype(np.dtype("bfloat16"))
    return o


_INS = ["x", "eye", "win", "wx", "gavg", "conv_p", "pick", "wdt", "par", "wout", "ln_g", "ln_b", "wr", "rb", "w1", "b1", "w2",
        "b2", "spread", "eyeb"]


def kernel(**inputs):
    import numpy as _np
    import concourse.bacc as _bacc
    from concourse import mybir as _mybir
    from concourse.bass_utils import run_bass_kernel_spmd as _run

    nc = _bacc.Bacc("TRN2", target_bir_lowering=False, num_devices=1)
    given = {k: _np.asarray(v) for k, v in inputs.items()}
    laid = lay_out(_np, given)
    laid["x"] = given["x"]
    arrays, args = {}, []
    for name in _INS:
        a = _np.ascontiguousarray(laid[name])
        arrays[f"in_{name}_dram"] = a
        args.append(nc.dram_tensor(f"in_{name}_dram", a.shape, _mybir.dt.from_np(a.dtype), kind="ExternalInput").ap())
    args.append(nc.dram_tensor("out_0_dram", (BATCH, HW, HW, C), F32, kind="ExternalOutput").ap())
    bass_vision_mamba_moe(nc, *args)
    r = _run(nc, [arrays], core_ids=[0])
    return r.results[0]["out_0_dram"]
```

```python
from contextlib import ExitStack

import concourse.bass as bass
from concourse import mybir

F32 = mybir.dt.float32
BF16 = mybir.dt.bfloat16
ALU = mybir.AluOpType
ACT = mybir.ActivationFunctionType
AX_X = mybir.AxisListType.X

P = 128
BATCH = 4
HW = 32
L = HW * HW
C = 384
NC = C // P
GN_GROUPS = 32
DI = 192
HALF = DI - P
N = 16
R = 24
DIRS = 4
KIND = 3
PAIRS = BATCH // 2
TT = L // P
PAD = HW + 2
EXPERTS = 4
HID = 96
BANK = 512
PIECES = 3
PR = 32
KEPT = ("wout", "gam", "bet", "wr", "rb", "w1", "b1", "w2", "b2", "spread", "eyeb")
UNIT = N
GROUP = 2 * UNIT
PROJ = 4
GROUPS = PAIRS * 2 * KIND
RING = 4
CROW_RING = 8
HC_RING = 8
LAG = 5
AHEAD = 2
C_AHEAD = 3
PREP = 3
LN2 = 0.693147
LOG_MAX = 80.0


def need(eng, semaphore, value):
    if isinstance(value, int) and value <= 0:
        return
    eng.wait_ge(semaphore, value)


def neighbours(chunk):
    assert C // GN_GROUPS <= P
    return [c for c in range(NC) if abs(c - chunk) <= 1]


def halves():
    return [slice(q * BANK, (q + 1) * BANK) for q in range(L // BANK)]


def load_unit(sp, d, unit, shared, s, rows):
    bc_row, kind, dts_row, par_row, u_row = rows
    for dst, src, arrived in (
        (unit["dtr"][:, s], d["dts_flat"][bass.ds(dts_row, 1)], "dt_loads"),
        (unit["wdt"][:, s], d["wdt"][bass.ds(par_row, 1)], "dt_loads"),
        (unit["par"][:, s], d["par"][bass.ds(par_row, 1)], "dt_loads"),
        (unit["u"][:, s], d["u_flat"][bass.ds(u_row, 1)], "loads"),
        (unit["bc"][:, s, 0], d["bc_flat"][bass.ds(bc_row, 1)], "loads"),
        (unit["bc"][:, s, 1], d["bc_flat"][bass.ds(bc_row + 1, 1)], "loads"),
        (unit["pick"][:, s], d["pick"][bass.ds(kind, 1)], "loads"),
    ):
        sp.dma_start(dst, src.rearrange("a p l -> p (a l)")).then_inc(shared[arrived][s], 16)


def rows_of(g, s):
    po, kind = g // KIND, g % KIND
    k = po % 2 + 2 * s
    return (po * 2 + s) * 2, kind, po * 2 + s, k * KIND + kind, g


def unit_buffers(keep):
    area = keep["area"]
    return dict(
        u=area[:, 0:2],
        dtr=area[0:2 * PR, 2:4],
        bc=area[0:PIECES * PR, 4:6].bitcast(BF16).rearrange("p s (m l) -> p s m l", m=2),
        pick=area[0:PIECES * PR, 6:8].bitcast(BF16),
        wdt=keep["wdt"], par=keep["par"],
    )


def head(nc, d, keep, keep_from, shared):
    with ExitStack() as ctx:
        def sb(name, shape, dt=F32):
            return ctx.enter_context(nc.sbuf_tensor("h_" + name, shape, dt))

        def sem(name):
            return ctx.enter_context(nc.semaphore("h_" + name))

        eye, gavg = keep["eye"], keep["gavg"]
        win = sb("win", [P, NC, C])
        wx = sb("wx", [P, 4, P])
        conv_p = sb("conv_p", [P, KIND, 10])
        xin = [keep["area"][:, KIND * i:KIND * (i + 1)].rearrange("p a l -> p (a l)").rearrange("p (t c) -> p t c", c=C)
               for i in range(2)]
        xt = sb("xt", [P, 2, NC, L])
        xn = sb("xn", [P, 2, NC, L])
        xpad = sb("xpad", [P, KIND, PAD, PAD])
        acc = sb("acc", [P, KIND, L])
        xc = sb("xc", [P, KIND, L])
        xct = sb("xct", [P, KIND, L])
        zt = sb("zt", [P, TT, 2 * DI])
        hi = sb("hi", [2 * PR, 2, L], BF16)
        mid = sb("mid", [2 * PR, 2, L], BF16)
        lo = sb("lo", [2 * PR, 2, L], BF16)
        rest = sb("rest", [2 * PR, 2, L])
        dts = sb("dts", [P, 2, L])
        st = sb("st", [P, NC, 2, 6])
        mv = sb("mv", [P, BATCH, NC, 2])
        gmean = sb("gmean", [P, BATCH, NC])
        dev = sb("dev", [P, BATCH, NC])
        chan_var = sb("chan_var", [P, BATCH, NC])
        rstd = sb("rstd", [P, BATCH, NC])
        std = sb("std", [P, BATCH, NC])
        eps = sb("eps", [P, 1])
        big = [ctx.enter_context(nc.psum_tensor(f"h_big{i}", [P, L], F32)) for i in range(2)]
        pz = [ctx.enter_context(nc.psum_tensor(f"h_pz{i}", [P, BANK], F32)) for i in range(2)]
        pst = ctx.enter_context(nc.psum_tensor("h_pst", [P, BANK], F32))

        weights_in = {name: sem(f"{name}_in") for name in ("eye", "gavg", "win", "conv_p", "wx")}
        x_in = [sem(f"x_in{b}") for b in range(BATCH)]
        xt_out = [sem(f"xt_out{b}") for b in range(BATCH)]
        borders = sem("borders")
        turned = sem("turned")
        xt_ready = sem("xt_ready")
        chan_stats = sem("chan_stats")
        mean_sums = sem("mean_sums")
        var_stats = sem("var_stats")
        var_sums = sem("var_sums")
        std_ready = sem("std_ready")
        xn_ready = sem("xn_ready")
        xh_done = sem("xh_done")
        xpad_ready = sem("xpad_ready")
        z_done = sem("z_done")
        z_ready = sem("z_ready")
        z_out = sem("z_out")
        convolved = [sem(f"convolved{kind}") for kind in range(KIND)]
        xc_ready = sem("xc_ready")
        xct_ready = sem("xct_ready")
        u_out = sem("u_out")
        xd_done = sem("xd_done")
        hi_ready = sem("hi_ready")
        rest_ready = sem("rest_ready")
        mid_ready = sem("mid_ready")
        lo_ready = sem("lo_ready")
        bc_out = [sem(f"bc_out{i}") for i in range(2)]
        U_STORED = 16 * 2 * KIND
        block = ctx.enter_context(nc.Block())

        def xd(pair, k):
            return pair * PROJ + k

        def use_t(b, c):
            return b * NC + c if b < 3 else b * NC + c + KIND

        def use_x(pair, kind):
            return 3 * NC + kind if pair == 0 else BATCH * NC + KIND + kind

        def use_p(pair, k):
            return BATCH * NC + PAIRS * KIND + xd(pair, k)

        emptied = {}
        for b in range(BATCH):
            for c in range(NC):
                emptied[use_t(b, c)] = (xt_ready, b * NC + c + 1)
        for pair in range(PAIRS):
            for kind in range(KIND):
                emptied[use_x(pair, kind)] = (xpad_ready, pair * KIND + kind + 1)
            for k in range(PROJ):
                emptied[use_p(pair, k)] = (mid_ready, xd(pair, k) + 1)

        @block.sync
        def _(sp):
            def store_z(pair):
                sp.wait_ge(z_ready, TT * (pair + 1))
                sp.dma_start(d["sz"][pair], zt[:]).then_inc(z_out, 16)

            def weights(**tiles):
                for name, t in tiles.items():
                    sp.dma_start(t[:], d[name]).then_inc(weights_in[name], 16)

            weights(eye=eye)
            for b in range(BATCH):
                if b >= 2:
                    sp.wait_ge(turned, NC * (b - 1))
                sp.dma_start(xin[b % 2], d["x"][b].rearrange("(t p) c -> p t c", p=P)).then_inc(x_in[b], 16)
                if b == 0:
                    weights(gavg=gavg)
                if b == 1:
                    weights(win=win, conv_p=conv_p, wx=wx)
            for b in range(BATCH):
                sp.wait_ge(xt_ready, NC * (b + 1))
                sp.dma_start(d["xt"][b].rearrange("c p l -> p c l"), xt[:, b % 2]).then_inc(xt_out[b], 16)
                if b == 1:
                    for name, src in keep_from.items():
                        sp.dma_start(keep[name][:], src).then_inc(shared["kept_in"], 16)
            for pair in range(PAIRS):
                if pair:
                    sp.wait_ge(turned, NC * BATCH)
                    sp.wait_ge(u_out, U_STORED)
                    for i in range(2):
                        sp.wait_ge(bc_out[i], 16 * 4 * PROJ // 2)
                    load_unit(sp, d, unit_buffers(keep), shared, 0, rows_of(0, 0))
                store_z(pair)
                for o, (t, ready) in enumerate(((xc, xc_ready), (xct, xct_ready))):
                    for kind in range(KIND):
                        sp.wait_ge(ready, pair * KIND + kind + 1)
                        sp.dma_start(d["u"][pair, o, kind], t[:, kind]).then_inc(u_out, 16)
                for k in range(PROJ):
                    i, o, m = xd(pair, k), k // 2, k % 2
                    sp.wait_ge(lo_ready, i + 1)
                    for piece, t in enumerate((hi, mid, lo)):
                        at = piece * PR + m * N
                        sp.dma_start(d["bc"][pair, o, :, at:at + N], t[:, i % 2]).then_inc(bc_out[i % 2], 16)
                    sp.dma_start(d["dts"][pair, o, :, m * PR:(m + 1) * PR], dts[2 * PR:P, i % 2]).then_inc(bc_out[i % 2], 16)
            for b in range(BATCH):
                sp.wait_ge(xt_out[b], 16)
            sp.wait_ge(z_out, 16 * PAIRS)
            sp.wait_ge(u_out, U_STORED * PAIRS)
            for i in range(2):
                sp.wait_ge(bc_out[i], 16 * 4 * PAIRS * PROJ // 2)

        @block.tensor
        def _(pe):
            pe.wait_ge(weights_in["eye"], 16)

            def big_for(use):
                if use >= 2:
                    pe.wait_ge(*emptied[use - 2])
                return big[use % 2]

            def transposes(b):
                pe.wait_ge(x_in[b], 16)
                for c in range(NC):
                    buf = big_for(use_t(b, c))
                    for t in range(TT):
                        mm = pe.transpose(buf[:, t * P:(t + 1) * P], xin[b % 2][:, t, c * P:(c + 1) * P], eye[:])
                    mm.then_inc(turned, 1)

            def averages(b, step):
                if b == 0:
                    pe.wait_ge(weights_in["gavg"], 16)
                if step == 0:
                    pe.wait_ge(chan_stats, b + 1)
                    if b == 3:
                        pe.wait_ge(var_stats, b)
                    else:
                        need(pe, std_ready, b)
                else:
                    pe.wait_ge(var_stats, b + 1 if b < 2 else BATCH)
                for co in range(NC):
                    near = neighbours(co)
                    for ci in near:
                        rhs = mv[:, b, ci, 0:1] if step == 0 else chan_var[:, b, ci:ci + 1]
                        col = (b * 2 + step) * NC + co
                        mm = pe.matmul(pst[:, col:col + 1], gavg[:, ci * NC + co], rhs,
                                       start=(ci == near[0]), stop=(ci == near[-1]))
                mm.then_inc((mean_sums, var_sums)[step], 1)

            def in_proj_x(pair):
                pe.wait_ge(xn_ready, 2 * (pair + 1))
                pe.wait_ge(weights_in["win"], 16)
                for kind in range(KIND):
                    buf = big_for(use_x(pair, kind))
                    for q in halves():
                        if kind < 2:
                            for c in range(NC):
                                mm = pe.matmul(buf[:, q], win[:, c, 0:P], xn[:, kind, c, q], start=(c == 0), stop=(c == NC - 1))
                        else:
                            for b in range(2):
                                for c in range(NC):
                                    mm = pe.matmul(buf[b * HALF:(b + 1) * HALF, q], win[:, c, P:DI], xn[:, b, c, q],
                                                   start=(c == 0), stop=(c == NC - 1))
                    mm.then_inc(xh_done, 1)

            def in_proj_z(pair, tiles):
                for t in tiles:
                    i = pair * TT + t
                    need(pe, z_ready, i - 1)
                    for b in range(2):
                        for c in range(NC):
                            mm = pe.matmul(pz[i % 2][:, b * DI:(b + 1) * DI], xn[:, b, c, t * P:(t + 1) * P], win[:, c, DI:C],
                                           start=(c == 0), stop=(c == NC - 1))
                    mm.then_inc(z_done, 1)

            def x_proj(pair, tiles):
                for k in tiles:
                    o, b = k // 2, k % 2
                    src = xct if o else xc
                    pe.wait_ge(xct_ready if o else xc_ready, KIND * (pair + 1))
                    pe.wait_ge(weights_in["wx"], 16)
                    buf = big_for(use_p(pair, k))
                    rest_rows = slice(b * HALF, (b + 1) * HALF)
                    for q in halves():
                        pe.matmul(buf[:, q], wx[:, 2 * o], src[:, b, q], start=True, stop=False)
                        mm = pe.matmul(buf[:, q], wx[rest_rows, 2 * o + 1], src[rest_rows, 2, q], start=False, stop=True)
                    mm.then_inc(xd_done, 1)

            transposes(0)
            transposes(1)
            for b in range(2):
                averages(b, 0)
                averages(b, 1)
            transposes(2)
            in_proj_x(0)
            transposes(3)
            in_proj_z(0, range(0, 1))
            averages(2, 0)
            in_proj_z(0, range(1, 2))
            averages(3, 0)
            in_proj_z(0, range(2, 4))
            averages(2, 1)
            averages(3, 1)
            in_proj_z(0, range(4, TT))
            in_proj_x(1)
            x_proj(0, range(0, 2))
            in_proj_z(1, range(0, 4))
            x_proj(0, range(2, PROJ))
            in_proj_z(1, range(4, TT))
            x_proj(1, range(PROJ))

        @block.scalar
        def _(act):
            def copy_xt(b):
                for c in range(NC):
                    act.wait_ge(turned, b * NC + c + 1)
                    if b >= 2:
                        act.wait_ge(xt_out[b - 2], 16)
                        act.wait_ge(xn_ready, b - 1)
                    nc.scalar.copy(xt[:, b % 2, c], big[use_t(b, c) % 2][:]).then_inc(xt_ready, 1)

            def root(b):
                act.wait_ge(var_sums, b + 1 if b < 2 else BATCH)
                nc.scalar.activation(std[:, b], pst[:, (b * 2 + 1) * NC:(b * 2 + 2) * NC], ACT.Sqrt,
                                     bias=eps[:]).then_inc(std_ready, 1)

            def fill_xpad(pair, kinds):
                act.wait_ge(borders, 1)
                for kind in kinds:
                    act.wait_ge(xh_done, pair * KIND + kind + 1)
                    need(act, convolved[kind], pair * 9)
                    nc.scalar.copy(xpad[:, kind, 1:HW + 1, 1:HW + 1],
                                   big[use_x(pair, kind) % 2][:].rearrange("p (h w) -> p h w", h=HW)).then_inc(xpad_ready, 1)

            def silu_z(pair, tiles):
                for t in tiles:
                    i = pair * TT + t
                    act.wait_ge(z_done, i + 1)
                    need(act, z_out, 16 * pair)
                    nc.scalar.activation(zt[:, t], pz[i % 2][:, 0:2 * DI], ACT.Silu).then_inc(z_ready, 1)

            def silu_conv(pair, kind):
                act.wait_ge(weights_in["conv_p"], 16)
                act.wait_ge(convolved[kind], (pair + 1) * 9)
                need(act, u_out, U_STORED * pair)
                need(act, xct_ready, KIND * pair)
                need(act, xd_done, PROJ * pair)
                nc.scalar.activation(xc[:, kind], acc[:, kind], ACT.Silu, bias=conv_p[:, kind, 9:10]).then_inc(xc_ready, 1)

            def split(pair, k):
                i = xd(pair, k)
                src = big[use_p(pair, k) % 2]
                act.wait_ge(xd_done, i + 1)
                need(act, bc_out[i % 2], 16 * 4 * (i // 2))
                nc.scalar.copy(hi[:, i % 2], src[0:2 * PR, :]).then_inc(hi_ready, 1)
                nc.scalar.copy(dts[2 * PR:P, i % 2], src[2 * PR:P, :])
                act.wait_ge(rest_ready, i + 1)
                nc.scalar.copy(mid[:, i % 2], rest[:, i % 2]).then_inc(mid_ready, 1)

            copy_xt(0)
            copy_xt(1)
            root(0)
            root(1)
            copy_xt(2)
            fill_xpad(0, range(KIND))
            copy_xt(3)
            silu_z(0, range(0, 4))
            silu_conv(0, 0)
            silu_z(0, range(4, 6))
            root(2)
            root(3)
            silu_z(0, range(6, TT))
            silu_conv(0, 1)
            fill_xpad(1, range(2))
            silu_conv(0, 2)
            fill_xpad(1, range(2, KIND))
            split(0, 0)
            split(0, 1)
            silu_z(1, range(0, 4))
            split(0, 2)
            split(0, 3)
            silu_conv(1, 0)
            silu_z(1, range(4, 6))
            silu_conv(1, 1)
            silu_conv(1, 2)
            silu_z(1, range(6, TT))
            for k in range(PROJ):
                split(1, k)

        def lowest(eng, tt, i):
            eng.wait_ge(mid_ready, i + 1)
            tt(lo[:, i % 2], rest[:, i % 2], mid[:, i % 2], ALU.subtract).then_inc(lo_ready, 1)

        def convolve(eng, pair, kind, taps=range(9)):
            eng.wait_ge(weights_in["conv_p"], 16)
            eng.wait_ge(xpad_ready, pair * KIND + kind + 1)
            need(eng, xc_ready, (KIND * (pair - 1) + kind + 1) if pair else 0)
            out = acc[:, kind].rearrange("p (h w) -> p h w", h=HW)
            for tap in taps:
                view = xpad[:, kind, tap // 3:tap // 3 + HW, tap % 3:tap % 3 + HW]
                w = conv_p[:, kind, tap:tap + 1]
                if tap == 0:
                    eng.tensor_scalar(out, view, w, None, ALU.mult).then_inc(convolved[kind], 1)
                else:
                    eng.wait_ge(convolved[kind], pair * 9 + tap)
                    eng.scalar_tensor_tensor(out, view, w, out, ALU.mult, ALU.add).then_inc(convolved[kind], 1)

        @block.vector
        def _(dve):
            chain = ctx.enter_context(nc.semaphore("h_chain"))
            links = [0]

            def link(ins):
                links[0] += 1
                ins.then_inc(chain, 1)
                dve.wait_ge(chain, links[0])

            link(nc.vector.memset(eps[:], 1e-5))

            def channel_stats(b):
                for c in range(NC):
                    dve.wait_ge(xt_ready, b * NC + c + 1)
                    for h, q in enumerate(halves()):
                        last = nc.vector.bn_stats(st[:, c, h], xt[:, b % 2, c, q])
                    link(last)
                    last = nc.vector.bn_aggr(mv[:, b, c], st[:, c].rearrange("p a s -> p (a s)"))
                last.then_inc(chan_stats, 1)

            def about_group(b):
                dve.wait_ge(chan_stats, b + 1)
                dve.wait_ge(mean_sums, b + 1)
                link(nc.vector.tensor_copy(gmean[:, b], pst[:, b * 2 * NC:(b * 2 + 1) * NC]))
                link(nc.vector.tensor_tensor(dev[:, b], mv[:, b, :, 0], gmean[:, b], ALU.subtract))
                link(nc.vector.tensor_tensor(dev[:, b], dev[:, b], dev[:, b], ALU.mult))
                nc.vector.tensor_tensor(chan_var[:, b], mv[:, b, :, 1], dev[:, b], ALU.add).then_inc(var_stats, 1)

            def normalise(b):
                dve.wait_ge(std_ready, b + 1)
                link(nc.vector.reciprocal(rstd[:, b], std[:, b]))
                need(dve, z_done, TT * (b // 2))
                for c in range(NC):
                    last = nc.vector.tensor_scalar(xn[:, b % 2, c], xt[:, b % 2, c], gmean[:, b, c:c + 1],
                                                   rstd[:, b, c:c + 1], ALU.subtract, ALU.mult)
                last.then_inc(xn_ready, 1)

            def split(pair, k):
                i = xd(pair, k)
                dve.wait_ge(hi_ready, i + 1)
                need(dve, lo_ready, max(i - 1, PROJ * pair))
                nc.vector.tensor_tensor(rest[:, i % 2], big[use_p(pair, k) % 2][0:2 * PR, :], hi[:, i % 2], ALU.subtract)\
                  .then_inc(rest_ready, 1)
                if pair:
                    lowest(dve, nc.vector.tensor_tensor, i)

            channel_stats(0)
            about_group(0)
            channel_stats(1)
            about_group(1)
            normalise(0)
            normalise(1)
            channel_stats(2)
            convolve(dve, 0, 0)
            channel_stats(3)
            about_group(2)
            about_group(3)
            convolve(dve, 0, 1)
            convolve(dve, 0, 2, range(4))
            normalise(2)
            normalise(3)
            convolve(dve, 0, 2, range(4, 9))
            convolve(dve, 1, 0)
            split(0, 0)
            split(0, 1)
            convolve(dve, 1, 1)
            split(0, 2)
            split(0, 3)
            convolve(dve, 1, 2)
            for k in range(PROJ):
                split(1, k)

        @block.gpsimd
        def _(pool):
            nc.gpsimd.memset(xpad[:], 0.0).then_inc(borders, 1)
            for pair in range(PAIRS):
                for kind in range(KIND):
                    pool.wait_ge(xc_ready, pair * KIND + kind + 1)
                    need(pool, u_out, U_STORED * pair)
                    need(pool, xd_done, PROJ * pair)
                    nc.gpsimd.tensor_copy(xct[:, kind].rearrange("p (w h) -> p h w", w=HW),
                                          xc[:, kind].rearrange("p (h w) -> p h w", h=HW)).then_inc(xct_ready, 1)
                if pair == 0:
                    for k in range(PROJ):
                        lowest(pool, nc.gpsimd.tensor_tensor, k)


def scan(nc, d, keep, ys, shared):
    with ExitStack() as ctx:
        def sb(name, shape, dt=F32):
            return ctx.enter_context(nc.sbuf_tensor("s_" + name, shape, dt))

        def sem(name):
            return ctx.enter_context(nc.semaphore("s_" + name))

        eye = keep["eye"]
        unit_in = unit_buffers(keep)
        bc, pick = unit_in["bc"], unit_in["pick"]
        dtr, wdt, u = unit_in["dtr"], unit_in["wdt"], unit_in["u"]
        par = unit_in["par"]
        amin = sb("amin", [P, 2, N])
        aexp = sb("aexp", [P, 2, N])
        aneg = sb("aneg", [P, 2, N])
        dt_ = sb("dt", [P, 2, L])
        dtu = sb("dtu", [P, 2, L])
        ez, rz, qz = (ys["y1"][:, i] for i in range(3))
        lz = sb("lz", [P, L])
        a = sb("a", [P, RING, L])
        h = sb("h", [P, RING, L])
        hc = sb("hc", [P, HC_RING, L])
        du = sb("du", [P, L])
        crow = sb("crow", [P, CROW_RING, L])
        dsum = sb("dsum", [P, 1])
        yout = ys["yout"]
        pb = ctx.enter_context(nc.psum_tensor("s_pb", [P, 2, L], F32))
        pc = ctx.enter_context(nc.psum_tensor("s_pc", [P, L], F32))
        py = ctx.enter_context(nc.psum_tensor("s_py", [P, L], F32))

        dt_loads, loads, y_stored = shared["dt_loads"], shared["loads"], shared["y_stored"]
        b_row = sem("b_row")
        c_row = sem("c_row")
        crow_ready = sem("crow_ready")
        a_ready = sem("a_ready")
        b_ready = sem("b_ready")
        h_ready = sem("h_ready")
        hc_ready = sem("hc_ready")
        y_added = sem("y_added")
        y_taken = sem("y_taken")
        z_done = sem("z_done")
        z_taken = sem("z_taken")
        e_ready = sem("e_ready")
        l_ready = sem("l_ready")
        q_ready = sem("q_ready")
        s_ready = sem("s_ready")
        s2_ready = sem("s2_ready")
        s3_ready = sem("s3_ready")
        dt_ready = sem("dt_ready")
        dtu_ready = sem("dtu_ready")
        amin_ready = sem("amin_ready")
        aexp_ready = sem("aexp_ready")
        a_neg_ready = sem("a_neg_ready")
        dsum_ready = sem("dsum_ready")
        skip_ready = sem("skip_ready")
        block = ctx.enter_context(nc.Block())

        def groups(eng, body):
            body(0, False)
            with eng.Fori(1, GROUPS - 1) as g:
                body(g, False)
            body(GROUPS - 1, True)

        def prepares(n, s, last):
            return n == PREP and not (last and s == 1)

        def c_steps(j, last):
            s, n = j // UNIT, j % UNIT
            steps = [j + C_AHEAD]
            if not (last and s == 1):
                if n == PREP:
                    steps = []
                elif n in (PREP + 1, PREP + 2):
                    steps = [j + C_AHEAD - 1]
                elif n == PREP + 3:
                    steps = [j + C_AHEAD - 1, j + C_AHEAD]
            return [i for i in steps if not (last and i >= GROUP)]

        def flow(s):
            return slice(None, None, -1) if s else slice(None)

        def add_e(eng, tt, unit):
            eng.wait_ge(s_ready, unit + 1)
            tt(qz, qz, ez, ALU.add).then_inc(s2_ready, 1)

        def times_u(eng, tt, g, unit, s):
            eng.wait_ge(loads[s], (g + 1) * LOADED)
            eng.wait_ge(dt_ready, unit + 1)
            tt(dtu[:, s], dt_[:, s], u[:, s], ALU.mult).then_inc(dtu_ready, 1)

        @block.sync
        def _(sp):
            load_unit(sp, d, unit_in, shared, 1, rows_of(0, 1))
            sp.wait_ge(shared["kept_in"], 16 * len(KEPT))
            with sp.Fori(1, GROUPS) as g:
                rows = [[sp.snap(v) for v in rows_of(g, s)] for s in range(2)]
                last_y = sp.snap(g - 1)
                steps = [sp.snap(g * GROUP - GROUP + (s + 1) * UNIT) for s in range(2)]
                for s in range(2):
                    sp.wait_ge(h_ready, steps[s])
                    sp.wait_ge(c_row, steps[s])
                    if s == 1:
                        sp.wait_ge(skip_ready, g)
                    load_unit(sp, d, unit_in, shared, s, rows[s])
                sp.wait_ge(y_taken, g)
                sp.dma_start(d["y_flat"][bass.ds(last_y, 1)].rearrange("a p l -> p (a l)"), yout[:]).then_inc(y_stored, 16)
            sp.wait_ge(y_stored, 16 * (GROUPS - 1))
            sp.dma_start(ys["y0"][:], d["y_flat"][0:KIND].rearrange("t p l -> p t l")).then_inc(shared["y0_in"], 16)
            sp.wait_ge(dt_ready, 2 * GROUPS)
            sp.dma_start(ys["y1"][:], d["y_flat"][KIND:2 * KIND].rearrange("t p l -> p t l")).then_inc(shared["y1_in"], 16)
            sp.wait_ge(y_taken, GROUPS)
            sp.dma_start(d["y_flat"][bass.ds(GROUPS - 1, 1)].rearrange("a p l -> p (a l)"), yout[:]).then_inc(y_stored, 16)

        DT_LOADED, LOADED = 16 * 3, 16 * 4

        @block.tensor
        def _(pe):
            def dt_product(g, s):
                pe.wait_ge(dt_loads[s], (g + 1) * DT_LOADED)
                for q in halves():
                    mm = pe.matmul(pc[:, q], wdt[:, s], dtr[:, s, q], start=True, stop=True)
                mm.then_inc(z_done, 1)

            def add_y(g, j, between=None):
                step = g * GROUP + j
                n = j % GROUP
                pe.wait_ge(hc_ready, step + 1)
                if n == 0:
                    need(pe, y_taken, g)
                for i, q in enumerate(halves()):
                    if i and between is not None:
                        spread_c(g, between)
                    mm = pe.matmul(py[:, q], eye[:], hc[:, n % HC_RING, q], start=(n == 0), stop=(n == GROUP - 1))
                mm.then_inc(y_added, 1)

            def spread_c(g, j, last=False):
                step = g * GROUP + j
                s, n = j // UNIT % 2, j % UNIT
                if n == 0:
                    pe.wait_ge(loads[s], (g + 1 + j // GROUP) * LOADED)
                need(pe, crow_ready, step)
                if n == PREP + C_AHEAD and not (last and s == 1):
                    pe.wait_ge(z_taken, g * 2 + j // UNIT + 2)
                for q in halves():
                    mm = pe.matmul(pc[:, q], pick[:, s, n * P:(n + 1) * P], bc[:, s, 1, q], start=True, stop=True)
                mm.then_inc(c_row, 1)

            def body(g, last):
                first = isinstance(g, int) and g == 0
                for j in range(GROUP):
                    s, n = j // UNIT, j % UNIT
                    step = g * GROUP + j
                    need(pe, h_ready, step - 1)
                    for q in halves():
                        mm = pe.matmul(pb[:, j % 2, q], pick[:, s, n * P:(n + 1) * P], bc[:, s, 0, q], start=True, stop=True)
                    mm.then_inc(b_row, 1)
                    rows = c_steps(j, last)
                    if j >= LAG:
                        add_y(g, j - LAG, rows[0] if len(rows) == 2 else None)
                    elif not first:
                        if j < LAG - 1:
                            add_y(g, j - LAG)
                    if prepares(n, s, last):
                        pe.wait_ge(crow_ready, step + C_AHEAD)
                        dt_product(g + s, 1 - s)
                    if j == LAG - 2 and not first:
                        add_y(g, -1)
                    for c in rows[-1:]:
                        spread_c(g, c, last)

            dt_product(0, 0)
            pe.wait_ge(z_taken, 1)
            for j in range(C_AHEAD):
                spread_c(0, j)
            groups(pe, body)
            for j in range(GROUP - LAG, GROUP):
                add_y(GROUPS - 1, j)

        @block.scalar
        def _(act):
            def take_z(g, s, unit):
                act.wait_ge(z_done, unit + 1)
                act.wait_ge(dt_loads[s], (g + 1) * DT_LOADED)
                need(act, dt_ready, unit)
                nc.scalar.activation(rz, pc[:], ACT.Identity, bias=par[:, s, N:N + 1]).then_inc(z_taken, 1)

            def abs_z(unit):
                act.wait_ge(z_taken, unit + 1)
                nc.scalar.activation(ez, rz, ACT.Abs).then_inc(e_ready, 1)

            def exp_z(unit, s):
                act.wait_ge(e_ready, 2 * unit + 1)
                nc.scalar.activation(ez, ez, ACT.Exp, scale=-1.0).then_inc(e_ready, 1)
                act.wait_ge(amin_ready, unit + 1)
                nc.scalar.activation(aexp[:, s], amin[:, s], ACT.Exp).then_inc(aexp_ready, 1)

            def ln_z(unit):
                act.wait_ge(e_ready, 2 * unit + 2)
                nc.scalar.activation(lz[:], ez, ACT.Ln, bias=1.0).then_inc(l_ready, 1)

            def decay(g, j):
                step = g * GROUP + j
                s, n = j // UNIT % 2, j % UNIT
                if n == 0:
                    act.wait_ge(dt_ready, g * 2 + j // UNIT + 1)
                    act.wait_ge(a_neg_ready, g * 2 + j // UNIT + 1)
                need(act, h_ready, step - RING + 1)
                nc.scalar.activation(a[:, j % RING], dt_[:, s], ACT.Exp, scale=aneg[:, s, n:n + 1]).then_inc(a_ready, 1)

            def take_c(g, j):
                step = g * GROUP + j
                need(act, hc_ready, step - CROW_RING + 1)
                act.wait_ge(c_row, step + 1)
                nc.scalar.copy(crow[:, j % CROW_RING], pc[:]).then_inc(crow_ready, 1)

            def body(g, last):
                for j in range(GROUP):
                    s, n = j // UNIT, j % UNIT
                    rows = c_steps(j, last)
                    for c in rows[:-1]:
                        take_c(g, c)
                    if not (last and j + AHEAD >= GROUP):
                        decay(g, j + AHEAD)
                    for c in rows[-1:]:
                        take_c(g, c)
                    if last and s == 1:
                        continue
                    if n == PREP:
                        take_z(g + s, 1 - s, g * 2 + s + 1)
                    if n == PREP + 1:
                        abs_z(g * 2 + s + 1)
                    if n == PREP + 2:
                        exp_z(g * 2 + s + 1, 1 - s)
                    if n == PREP + 3:
                        ln_z(g * 2 + s + 1)

            act.preload_act_table_set("natural_log_exp_and_others")
            take_z(0, 0, 0)
            abs_z(0)
            exp_z(0, 0)
            ln_z(0)
            for j in range(C_AHEAD):
                take_c(0, j)
            for j in range(AHEAD):
                decay(0, j)
            groups(act, body)

        @block.vector
        def _(dve):
            def clamp_a(g, s, unit):
                dve.wait_ge(dt_loads[s], (g + 1) * DT_LOADED)
                nc.vector.tensor_scalar(amin[:, s], par[:, s, 0:N], LOG_MAX, None, ALU.min).then_inc(amin_ready, 1)

            def softplus_1(unit):
                dve.wait_ge(e_ready, 2 * unit + 2)
                nc.vector.tensor_scalar(qz, ez, 1.0, -1.0, ALU.add, ALU.add).then_inc(q_ready, 1)

            def softplus_2(unit, s):
                dve.wait_ge(q_ready, unit + 1)
                dve.wait_ge(l_ready, unit + 1)
                nc.vector.tensor_tensor(qz, lz[:], qz, ALU.subtract).then_inc(s_ready, 1)
                dve.wait_ge(aexp_ready, unit + 1)
                nc.vector.tensor_scalar(aneg[:, s], aexp[:, s], -1.0, None, ALU.mult).then_inc(a_neg_ready, 1)

            def softplus_3(unit):
                dve.wait_ge(s2_ready, unit + 1)
                nc.vector.scalar_tensor_tensor(lz[:], ez, LN2, qz, ALU.mult, ALU.max).then_inc(s3_ready, 1)

            def softplus_4(unit, s):
                dve.wait_ge(s3_ready, unit + 1)
                nc.vector.scalar_tensor_tensor(dt_[:, s], rz, 0.0, lz[:], ALU.max, ALU.add).then_inc(dt_ready, 1)

            def take_y(g):
                dve.wait_ge(y_added, g * GROUP + GROUP)
                dve.wait_ge(skip_ready, g + 1)
                need(dve, y_stored, g * 16)
                nc.vector.tensor_tensor(yout[:], du[:], py[:], ALU.add).then_inc(y_taken, 1)

            def skip_part(g):
                dve.wait_ge(loads[1], (g + 1) * LOADED)
                nc.vector.tensor_tensor(dsum[:], par[:, 1, N + 1:N + 2], par[:, 1, N + 2:N + 3], ALU.add).then_inc(dsum_ready, 1)
                dve.wait_ge(dsum_ready, g + 1)
                need(dve, y_taken, g)
                nc.vector.tensor_scalar(du[:], u[:, 1], dsum[:], None, ALU.mult).then_inc(skip_ready, 1)

            def body(g, last):
                for j in range(GROUP):
                    s, n = j // UNIT, j % UNIT
                    step = g * GROUP + j
                    if n == 0:
                        dve.wait_ge(dtu_ready, g * 2 + s + 1)
                    if j == LAG - 1 and not (isinstance(g, int) and g == 0):
                        take_y(g - 1)
                    if j == GROUP - 1:
                        skip_part(g)
                    dve.wait_ge(b_row, step + 1)
                    nc.vector.tensor_tensor(pb[:, j % 2], dtu[:, s], pb[:, j % 2], ALU.mult).then_inc(b_ready, 1)
                    dve.wait_ge(b_ready, step + 1)
                    dve.wait_ge(a_ready, step + 1)
                    need(dve, hc_ready, step - RING + 1)
                    f = flow(s)
                    nc.vector.tensor_tensor_scan(h[:, j % RING, f], a[:, j % RING, f], pb[:, j % 2, f], 0.0, ALU.mult, ALU.add)\
                      .then_inc(h_ready, 1)
                    if last and s == 1:
                        continue
                    unit = g * 2 + s + 1
                    if n == PREP:
                        clamp_a(g + s, 1 - s, unit)
                    if n == PREP + 3:
                        softplus_1(unit)
                    if n == PREP + 5:
                        softplus_2(unit, 1 - s)
                    if n == PREP + 7:
                        softplus_3(unit)
                    if n == PREP + 9:
                        softplus_4(unit, 1 - s)

            clamp_a(0, 0, 0)
            softplus_1(0)
            softplus_2(0, 0)
            add_e(dve, nc.vector.tensor_tensor, 0)
            softplus_3(0)
            softplus_4(0, 0)
            times_u(dve, nc.vector.tensor_tensor, 0, 0, 0)
            groups(dve, body)
            add_orientations(dve, nc.vector.tensor_tensor, ys, shared, 0)
            take_y(GROUPS - 1)

        @block.gpsimd
        def _(pool):
            def body(g, last):
                for j in range(GROUP):
                    s, n = j // UNIT, j % UNIT
                    step = g * GROUP + j
                    pool.wait_ge(h_ready, step + 1)
                    pool.wait_ge(crow_ready, step + 1)
                    need(pool, y_added, step - HC_RING + 1)
                    nc.gpsimd.tensor_tensor(hc[:, j % HC_RING], h[:, j % RING], crow[:, j % CROW_RING], ALU.mult).then_inc(hc_ready, 1)
                    if last and s == 1:
                        continue
                    if n == PREP + 5:
                        add_e(pool, nc.gpsimd.tensor_tensor, g * 2 + s + 1)
                    if n == PREP + 9:
                        times_u(pool, nc.gpsimd.tensor_tensor, g + s, g * 2 + s + 1, 1 - s)

            groups(pool, body)


def add_orientations(eng, tt, ys, shared, pair):
    for kind in range(KIND):
        eng.wait_ge(shared["y0_in"], 16 * (pair + 1))
        eng.wait_ge(shared["y1_in"], 16 * (pair + 1))
        whole = ys["y0"][:, kind].rearrange("p (h w) -> p h w", h=HW)
        tt(whole, whole, ys["y1"][:, kind].rearrange("p (w h) -> p h w", w=HW), ALU.add).then_inc(shared["sum_ready"], 1)


def tail(nc, d, keep, ys, shared):
    with ExitStack() as ctx:
        def sb(name, shape, dt=F32):
            return ctx.enter_context(nc.sbuf_tensor("t_" + name, shape, dt))

        def sem(name):
            return ctx.enter_context(nc.semaphore("t_" + name))

        eye, gavg, wout, gam, bet, wr, rb, w1, b1, w2, b2, spread, eyeb = (
            keep[k] for k in ("eye", "gavg", "wout", "gam", "bet", "wr", "rb", "w1", "b1", "w2", "b2", "spread", "eyeb"))
        y0, y1 = ys["y0"], ys["y1"]
        yt = sb("yt", [P, TT, 2, DI])
        sz = sb("sz", [P, TT, 2, DI])
        gated = sb("gated", [P, TT, KIND, P])
        yg = sb("yg", [P, KIND, L])
        st = sb("st", [P, NC, 2, 6])
        ln_mv = sb("ln_mv", [P, TT, 2, 2])
        ln_st = sb("ln_st", [P, TT, 2, 6])
        ln_r = sb("ln_r", [P, TT, 2])
        mv = sb("mv", [P, NC, 2])
        gmean = sb("gmean", [P, NC])
        dev = sb("dev", [P, NC])
        chan_var = sb("chan_var", [P, NC])
        std = sb("std", [P, NC])
        rstd = sb("rstd", [P, NC])
        eps = sb("eps", [P, 1])
        xt = [keep["area"][:, NC * i:NC * (i + 1)] for i in range(2)]
        hid = keep["area"][:, NC:2 * NC]
        x1 = sb("x1", [P, 2, NC, L])
        xn = sb("xn", [P, 2, NC, L])
        pr = sb("pr", [P, TT, EXPERTS])
        ex = sb("ex", [P, TT, EXPERTS])
        ge = sb("ge", [P, TT, EXPERTS])
        rank = sb("rank", [P, TT, EXPERTS])
        comb = sb("comb", [P, TT, EXPERTS])
        left = sb("left", [P, TT, EXPERTS])
        red = sb("red", [P, TT])
        parts = sb("parts", [P, TT, PIECES, PR], BF16)
        combt = sb("combt", [PIECES * PR, L], BF16)
        b2_hi = sb("b2_hi", [PIECES * PR, C], BF16)
        b2_mid = sb("b2_mid", [PIECES * PR, C], BF16)
        b2_rest = sb("b2_rest", [PIECES * PR, C])
        b2_parts = sb("b2_parts", [PIECES * PR, C], BF16)
        out = sb("out", [P, 4, C])
        big = [ctx.enter_context(nc.psum_tensor(f"t_big{i}", [P, L], F32)) for i in range(2)]
        small = [ctx.enter_context(nc.psum_tensor(f"t_small{i}", [P, BANK], F32)) for i in range(3)]
        stat = ctx.enter_context(nc.psum_tensor("t_stat", [P, BANK], F32))

        y0_in, y1_in, sum_ready = shared["y0_in"], shared["y1_in"], shared["sum_ready"]
        sz_in = sem("sz_in")
        xt_in = [sem(f"xt_in{b}") for b in range(BATCH)]
        yt_done = sem("yt_done")
        small_taken = sem("small_taken")
        ln_stat = sem("ln_stat")
        ln_std = sem("ln_std")
        yln = sem("yln")
        gate_ready = sem("gate_ready")
        back_done = sem("back_done")
        yg_ready = sem("yg_ready")
        op_done = sem("op_done")
        x1_ready = sem("x1_ready")
        stats = sem("stats")
        sums = sem("sums")
        std_ready = sem("std_ready")
        xn_ready = sem("xn_ready")
        lg_done = sem("lg_done")
        lg_ready = sem("lg_ready")
        ex_ready = sem("ex_ready")
        comb_ready = sem("comb_ready")
        ct_done = sem("ct_done")
        f1_done = sem("f1_done")
        gelu_ready = sem("gelu_ready")
        sp_done = sem("sp_done")
        hw_ready = sem("hw_ready")
        f2_done = sem("f2_done")
        b2_ready = sem("b2_ready")
        out_stored = [sem(f"out_stored{i}") for i in range(4)]
        block = ctx.enter_context(nc.Block())

        def stage(b):
            nxt = b + 1 < BATCH
            steps = [("F1", b, 1)]
            steps += [("STA", b + 1)] if nxt else []
            steps += [("CT", b)]
            steps += [("STB", b + 1)] if nxt else []
            steps += [("F1", b, 2), ("SP", b, 0), ("SP", b, 1), ("SP", b, 2)]
            steps += [("LG", b + 1), ("F1", b + 1, 0)] if nxt else []
            steps += [("F2", b, t) for t in range(TT)]
            steps += [("BK", 1, k) for k in range(KIND)] if b == 0 else []
            steps += [("OP", b + 2, c) for c in range(NC)] if b + 2 < BATCH else []
            return steps

        order = [("YT", 0, t) for t in range(TT)] + [("BK", 0, k) for k in range(KIND)]
        order += [("OP", 0, c) for c in range(NC)]
        order += [("OP", 1, 0), ("STA", 0), ("OP", 1, 1), ("STB", 0), ("OP", 1, 2)]
        order += [("YT", 1, t) for t in range(TT)]
        order += [("LG", 0), ("F1", 0, 0)]
        for b in range(BATCH):
            order += stage(b)
        large = [s for s in order if s[0] in ("BK", "OP", "F1", "SP")]
        little = [s for s in order if s[0] in ("YT", "CT", "F2")]

        def big_of(*step):
            return big[large.index(step) % 2]

        def small_of(*step):
            return small[little.index(step) % 3]

        def emptied(step):
            kind, b, i = step
            return {"BK": (yg_ready, b * KIND + i + 1), "OP": (x1_ready, b * NC + i + 1),
                    "F1": (gelu_ready, b * NC + i + 1), "SP": (hw_ready, b * NC + i + 1)}[kind]

        @block.sync
        def _(sp):
            sp.dma_start(sz[:].rearrange("p t b c -> p t (b c)"), d["sz"][0]).then_inc(sz_in, 16)
            sp.dma_start(xt[0], d["xt"][0].rearrange("c p l -> p c l")).then_inc(xt_in[0], 16)
            sp.wait_ge(shared["y_stored"], 16 * GROUPS)
            sp.wait_ge(yt_done, TT)
            at = 2 * KIND
            sp.dma_start(y0[:], d["y_flat"][at:at + KIND].rearrange("t p l -> p t l")).then_inc(y0_in, 16)
            sp.dma_start(y1[:], d["y_flat"][at + KIND:at + 2 * KIND].rearrange("t p l -> p t l")).then_inc(y1_in, 16)
            sp.dma_start(xt[1], d["xt"][1].rearrange("c p l -> p c l")).then_inc(xt_in[1], 16)
            sp.wait_ge(gate_ready, TT)
            sp.dma_start(sz[:].rearrange("p t b c -> p t (b c)"), d["sz"][1]).then_inc(sz_in, 16)
            for b in range(BATCH):
                for t in range(TT):
                    i = b * TT + t
                    sp.wait_ge(small_taken, little.index(("F2", b, t)) + 1)
                    sp.dma_start(d["out"][b, t * P:(t + 1) * P, :], out[:, i % 4]).then_inc(out_stored[i % 4], 16)
                    if t == 0 and b + 2 < BATCH:
                        sp.wait_ge(x1_ready, NC * (b + 2))
                        sp.dma_start(xt[0], d["xt"][b + 2].rearrange("c p l -> p c l")).then_inc(xt_in[b + 2], 16)
            for i in range(4):
                sp.wait_ge(out_stored[i], 16 * BATCH * TT // 4)

        @block.tensor
        def _(pe):
            def y_to_tokens(pair, t):
                if t == 0:
                    pe.wait_ge(sum_ready, KIND * (pair + 1))
                for kind in range(KIND):
                    mm = pe.transpose(small_of("YT", pair, t)[:, kind * P:(kind + 1) * P], y0[:, kind, t * P:(t + 1) * P], eye[:])
                mm.then_inc(yt_done, 1)

            def gated_back(pair, kind):
                for t in range(TT):
                    if kind == 0:
                        pe.wait_ge(gate_ready, pair * TT + t + 1)
                    mm = pe.transpose(big_of("BK", pair, kind)[:, t * P:(t + 1) * P], gated[:, t, kind], eye[:])
                mm.then_inc(back_done, 1)

            def out_proj(b, c):
                pair, o = b // 2, b % 2
                r = slice(o * HALF, (o + 1) * HALF)
                pe.wait_ge(yg_ready, KIND * (pair + 1))
                for q in halves():
                    buf = big_of("OP", b, c)[:, q]
                    pe.matmul(buf, wout[:, 0, c * P:(c + 1) * P], yg[:, o, q], start=True, stop=False)
                    mm = pe.matmul(buf, wout[r, 1, c * P:(c + 1) * P], yg[r, 2, q], start=False, stop=True)
                mm.then_inc(op_done, 1)

            def average(b, step):
                pe.wait_ge(stats, 2 * b + step + 1)
                need(pe, lg_ready, b)
                for co in range(NC):
                    near = neighbours(co)
                    for ci in near:
                        rhs = mv[:, ci, 0:1] if step == 0 else chan_var[:, ci:ci + 1]
                        col = step * NC + co
                        mm = pe.matmul(stat[:, col:col + 1], gavg[:, ci * NC + co], rhs,
                                       start=(ci == near[0]), stop=(ci == near[-1]))
                mm.then_inc(sums, 1)

            def logits(b):
                pe.wait_ge(xn_ready, b + 1)
                for t in range(TT):
                    for c in range(NC):
                        mm = pe.matmul(stat[:, 64 + t * EXPERTS:64 + (t + 1) * EXPERTS], xn[:, b % 2, c, t * P:(t + 1) * P], wr[:, c],
                                       start=(c == 0), stop=(c == NC - 1))
                mm.then_inc(lg_done, 1)

            def first_layer(b, j):
                for q in halves():
                    for c in range(NC):
                        mm = pe.matmul(big_of("F1", b, j)[:, q], w1[:, c, j * P:(j + 1) * P], xn[:, b % 2, c, q],
                                       start=(c == 0), stop=(c == NC - 1))
                mm.then_inc(f1_done, 1)

            def turn_weights(b):
                pe.wait_ge(comb_ready, b + 1)
                buf = small_of("CT", b)[:].bitcast(BF16)
                for t in range(TT):
                    mm = pe.transpose(buf[0:PIECES * PR, t * P:(t + 1) * P], parts[:, t].rearrange("p a r -> p (a r)"), eyeb[:])
                mm.then_inc(ct_done, 1)

            def spread_weights(b, j):
                pe.wait_ge(small_taken, little.index(("CT", b)) + 1)
                for q in halves():
                    mm = pe.matmul(big_of("SP", b, j)[:, q], spread[:, j * P:(j + 1) * P], combt[0:PR, q], start=True, stop=True)
                mm.then_inc(sp_done, 1)

            def second_layer(b, t):
                if t == 0:
                    pe.wait_ge(hw_ready, NC * (b + 1))
                    pe.wait_ge(b2_ready, 5)
                tok = slice(t * P, (t + 1) * P)
                ps = small_of("F2", b, t)[:, 0:C]
                pe.matmul(ps, combt[:, tok], b2_parts[:], start=True, stop=False, skip_group_check=True)
                for j in range(NC):
                    pe.matmul(ps, hid[:, j, tok], w2[:, j], start=False, stop=False, skip_group_check=True)
                for c in range(NC):
                    mm = pe.matmul(ps[:, c * P:(c + 1) * P], x1[:, b % 2, c, tok], eye[:], start=False, stop=(c == NC - 1),
                                   skip_group_check=True)
                mm.then_inc(f2_done, 1)

            work = {"YT": y_to_tokens, "BK": gated_back, "OP": out_proj, "STA": lambda b: average(b, 0),
                    "STB": lambda b: average(b, 1), "LG": logits, "F1": first_layer, "CT": turn_weights,
                    "SP": spread_weights, "F2": second_layer}
            for step in order:
                if step in large and large.index(step) >= 2:
                    pe.wait_ge(*emptied(large[large.index(step) - 2]))
                if step in little and little.index(step) >= 3:
                    pe.wait_ge(small_taken, little.index(step) - 2)
                work[step[0]](*step[1:])

        @block.scalar
        def _(act):
            def take_yt(pair):
                for t in range(TT):
                    act.wait_ge(yt_done, pair * TT + t + 1)
                    need(act, gate_ready, TT * pair)
                    src = small_of("YT", pair, t)
                    nc.scalar.copy(yt[:, t, :, 0:P], src[:, 0:2 * P].rearrange("p (b c) -> p b c", b=2))
                    nc.scalar.copy(yt[:, t, :, P:DI], src[:, 2 * P:3 * P].rearrange("p (b c) -> p b c", b=2)).then_inc(small_taken, 1)

            def root_ln(pair):
                act.wait_ge(ln_stat, pair + 1)
                nc.scalar.activation(ln_r[:], ln_mv[:, :, :, 1], ACT.Sqrt, bias=eps[:]).then_inc(ln_std, 1)

            def take_back(pair):
                need(act, op_done, 2 * NC * pair)
                for kind in range(KIND):
                    act.wait_ge(back_done, pair * KIND + kind + 1)
                    nc.scalar.copy(yg[:, kind], big_of("BK", pair, kind)[:]).then_inc(yg_ready, 1)

            def root(b):
                act.wait_ge(sums, 2 * b + 2)
                nc.scalar.activation(std[:], stat[:, NC:2 * NC], ACT.Sqrt, bias=eps[:]).then_inc(std_ready, 1)

            def exp_logits(b):
                act.wait_ge(lg_ready, b + 1)
                nc.scalar.activation(ex[:], pr[:], ACT.Exp).then_inc(ex_ready, 1)

            def gelu(b, j):
                act.wait_ge(f1_done, NC * b + j + 1)
                if j == 0:
                    need(act, f2_done, TT * b)
                    act.wait_ge(x1_ready, 2 * NC)
                nc.scalar.activation(hid[:, j], big_of("F1", b, j)[:], ACT.Gelu, bias=b1[:, j:j + 1]).then_inc(gelu_ready, 1)

            def take_weights(b):
                act.wait_ge(ct_done, b + 1)
                nc.scalar.copy(combt[:], small_of("CT", b)[0:PIECES * PR].bitcast(BF16)).then_inc(small_taken, 1)

            def take_out(b, tiles):
                for t in tiles:
                    i = b * TT + t
                    act.wait_ge(f2_done, i + 1)
                    need(act, out_stored[i % 4], 16 * (i // 4))
                    nc.scalar.copy(out[:, i % 4], small_of("F2", b, t)[:, 0:C]).then_inc(small_taken, 1)

            take_yt(0)
            root_ln(0)
            take_back(0)
            root(0)
            take_yt(1)
            exp_logits(0)
            gelu(0, 0)
            for b in range(BATCH):
                nxt = b + 1 < BATCH
                gelu(b, 1)
                take_weights(b)
                if nxt:
                    root(b + 1)
                gelu(b, 2)
                take_out(b, range(3))
                if b == 0:
                    root_ln(1)
                take_out(b, range(3, 6))
                if nxt:
                    exp_logits(b + 1)
                take_out(b, range(6, TT))
                if nxt:
                    gelu(b + 1, 0)
                if b == 0:
                    take_back(1)

        @block.gpsimd
        def _(pool):
            def gate(pair):
                pool.wait_ge(sz_in, 16 * (pair + 1))
                need(pool, back_done, KIND * pair)
                for t in range(TT):
                    pool.wait_ge(yln, pair * TT + t + 1)
                    nc.gpsimd.tensor_tensor(gated[:, t, 0:2], yt[:, t, :, 0:P], sz[:, t, :, 0:P], ALU.mult)
                    nc.gpsimd.tensor_tensor(gated[:, t, 2].rearrange("p (b c) -> p b c", b=2), yt[:, t, :, P:DI], sz[:, t, :, P:DI],
                                            ALU.mult).then_inc(gate_ready, 1)

            gate(0)
            add_orientations(pool, nc.gpsimd.tensor_tensor, ys, shared, 1)
            gate(1)

        @block.vector
        def _(dve):
            chain = ctx.enter_context(nc.semaphore("t_chain"))
            links = [0]

            def link(ins):
                links[0] += 1
                ins.then_inc(chain, 1)
                dve.wait_ge(chain, links[0])

            V = nc.vector

            def ln_stats(pair):
                for t in range(TT):
                    dve.wait_ge(small_taken, little.index(("YT", pair, t)) + 1)
                    for b in range(2):
                        last = V.bn_stats(ln_st[:, t, b], yt[:, t, b])
                link(last)
                for t in range(TT):
                    for b in range(2):
                        last = V.bn_aggr(ln_mv[:, t, b], ln_st[:, t, b])
                last.then_inc(ln_stat, 1)

            def ln_apply(pair):
                dve.wait_ge(ln_stat, pair + 1)
                for part in range(2):
                    tiles = range(part * TT // 2, (part + 1) * TT // 2)
                    for t in tiles:
                        for b in range(2):
                            last = V.scalar_tensor_tensor(yt[:, t, b], yt[:, t, b], ln_mv[:, t, b, 0:1], gam[:], ALU.subtract, ALU.mult)
                    link(last)
                    if part == 0:
                        dve.wait_ge(ln_std, pair + 1)
                        link(V.reciprocal(ln_r[:], ln_r[:]))
                    for t in tiles:
                        for b in range(2):
                            last = V.scalar_tensor_tensor(yt[:, t, b], yt[:, t, b], ln_r[:, t, b:b + 1], bet[:], ALU.mult, ALU.add)
                        last.then_inc(yln, 1)

            def residual(b, c):
                dve.wait_ge(xt_in[b], 16)
                need(dve, f2_done, TT * (b - 1))
                dve.wait_ge(op_done, NC * b + c + 1)
                V.tensor_tensor(x1[:, b % 2, c], xt[b == 1][:, c], big_of("OP", b, c)[:], ALU.add).then_inc(x1_ready, 1)
                dve.wait_ge(x1_ready, NC * b + c + 1)
                for h, q in enumerate(halves()):
                    last = V.bn_stats(st[:, c, h], x1[:, b % 2, c, q])
                link(last)
                last = V.bn_aggr(mv[:, c], st[:, c].rearrange("p a s -> p (a s)"))
                if c == NC - 1:
                    last.then_inc(stats, 1)

            def group_means(b):
                dve.wait_ge(stats, 2 * b + 1)
                dve.wait_ge(sums, 2 * b + 1)
                link(V.tensor_copy(gmean[:], stat[:, 0:NC]))
                link(V.tensor_tensor(dev[:], mv[:, :, 0], gmean[:], ALU.subtract))
                link(V.tensor_tensor(dev[:], dev[:], dev[:], ALU.mult))
                V.tensor_tensor(chan_var[:], mv[:, :, 1], dev[:], ALU.add).then_inc(stats, 1)

            def normalise(b):
                dve.wait_ge(std_ready, b + 1)
                link(V.reciprocal(rstd[:], std[:]))
                need(dve, f1_done, NC * (b - 1))
                for c in range(NC):
                    last = V.tensor_scalar(xn[:, b % 2, c], x1[:, b % 2, c], gmean[:, c:c + 1], rstd[:, c:c + 1], ALU.subtract, ALU.mult)
                last.then_inc(xn_ready, 1)

            def route(b):
                def wide(x):
                    return x.unsqueeze(2).broadcast_to([P, TT, EXPERTS])

                dve.wait_ge(lg_done, b + 1)
                lg = stat[:, 64:64 + TT * EXPERTS].rearrange("p (t e) -> p t e", e=EXPERTS)
                link(V.tensor_tensor(pr[:], lg, rb[:].unsqueeze(1).broadcast_to([P, TT, EXPERTS]), ALU.add))
                link(V.tensor_reduce(red[:], pr[:], AX_X, ALU.max))
                V.tensor_tensor(pr[:], pr[:], wide(red[:]), ALU.subtract).then_inc(lg_ready, 1)
                dve.wait_ge(ex_ready, b + 1)
                link(V.tensor_reduce(red[:], ex[:], AX_X, ALU.add))
                link(V.reciprocal(red[:], red[:]))
                link(V.tensor_tensor(pr[:], ex[:], wide(red[:]), ALU.mult))
                link(V.memset(rank[:], 0.0))
                for gap in range(1, EXPERTS):
                    m = EXPERTS - gap
                    link(V.tensor_tensor(ge[:, :, 0:m], pr[:, :, 0:m], pr[:, :, gap:EXPERTS], ALU.is_ge))
                    link(V.tensor_tensor(rank[:, :, gap:EXPERTS], rank[:, :, gap:EXPERTS], ge[:, :, 0:m], ALU.add))
                    link(V.tensor_tensor(rank[:, :, 0:m], rank[:, :, 0:m], ge[:, :, 0:m], ALU.subtract))
                    link(V.tensor_scalar(rank[:, :, 0:m], rank[:, :, 0:m], 1.0, None, ALU.add))
                link(V.tensor_scalar(rank[:], rank[:], 1.5, None, ALU.is_lt))
                link(V.tensor_tensor(pr[:], pr[:], rank[:], ALU.mult))
                link(V.tensor_reduce(red[:], pr[:], AX_X, ALU.add))
                link(V.tensor_scalar(red[:], red[:], 1e-8, None, ALU.add))
                link(V.reciprocal(red[:], red[:]))
                link(V.tensor_tensor(comb[:], pr[:], wide(red[:]), ALU.mult))
                need(dve, ct_done, b)
                E4 = EXPERTS
                link(V.tensor_copy(parts[:, :, 0, 0:E4], comb[:]))
                link(V.tensor_tensor(left[:], comb[:], parts[:, :, 0, 0:E4], ALU.subtract))
                link(V.tensor_copy(parts[:, :, 0, E4:2 * E4], left[:]))
                link(V.tensor_tensor(parts[:, :, 0, 2 * E4:3 * E4], left[:], parts[:, :, 0, E4:2 * E4], ALU.subtract))
                V.tensor_copy(parts[:, :, 1, 0:3 * E4], parts[:, :, 0, 0:3 * E4])
                V.tensor_copy(parts[:, :, 2, 0:3 * E4], parts[:, :, 0, 0:3 * E4]).then_inc(comb_ready, 1)

            def weigh(b, j):
                dve.wait_ge(gelu_ready, NC * b + j + 1)
                dve.wait_ge(sp_done, NC * b + j + 1)
                V.tensor_tensor(hid[:, j], hid[:, j], big_of("SP", b, j)[:], ALU.mult).then_inc(hw_ready, 1)

            def split_b2():
                V.tensor_copy(b2_hi[:], b2[:]).then_inc(b2_ready, 1)
                dve.wait_ge(b2_ready, 1)
                V.tensor_tensor(b2_rest[:], b2[:], b2_hi[:], ALU.subtract).then_inc(b2_ready, 1)
                dve.wait_ge(b2_ready, 2)
                V.tensor_copy(b2_mid[:], b2_rest[:]).then_inc(b2_ready, 1)
                dve.wait_ge(b2_ready, 3)
                V.tensor_tensor(b2_parts[:], b2_rest[:], b2_mid[:], ALU.subtract).then_inc(b2_ready, 1)
                dve.wait_ge(b2_ready, 4)
                V.tensor_copy(b2_parts[0:PR], b2_hi[0:PR])
                V.tensor_copy(b2_parts[PR:2 * PR], b2_mid[PR:2 * PR]).then_inc(b2_ready, 1)

            link(V.memset(eps[:], 1e-5))
            ln_stats(0)
            ln_apply(0)
            V.memset(parts[:], 0.0)
            split_b2()
            for c in range(NC):
                residual(0, c)
            group_means(0)
            residual(1, 0)
            normalise(0)
            residual(1, 1)
            residual(1, 2)
            route(0)
            for b in range(BATCH):
                if b + 1 < BATCH:
                    group_means(b + 1)
                    normalise(b + 1)
                for j in range(NC):
                    weigh(b, j)
                if b == 0:
                    ln_stats(1)
                    ln_apply(1)
                if b + 1 < BATCH:
                    route(b + 1)
                if b + 2 < BATCH:
                    for c in range(NC):
                        residual(b + 2, c)


def kept(nc, ctx, d):
    def sb(name, shape, dt=F32):
        return ctx.enter_context(nc.sbuf_tensor("k_" + name, shape, dt))

    keep = dict(
        eye=sb("eye", [P, P]), eyeb=sb("eyeb", [P, P], BF16), gavg=sb("gavg", [P, NC * NC, P]),
        wout=sb("wout", [P, 2, C]),
        gam=sb("gam", [P, DI]), bet=sb("bet", [P, DI]), wr=sb("wr", [P, NC, EXPERTS]), rb=sb("rb", [P, EXPERTS]),
        w1=sb("w1", [P, NC, C]), b1=sb("b1", [P, NC]), w2=sb("w2", [P, NC, C]), b2=sb("b2", [PIECES * PR, C]),
        spread=sb("spread", [PR, C], BF16),
    )
    keep["area"] = sb("area", [P, 2 * 4, L])
    keep["wdt"] = sb("wdt", [2 * PR, 2, P])
    keep["par"] = sb("par", [P, 2, N + 3])
    from_dram = dict(wout=d["wout"], gam=d["ln_g"].partition_broadcast(P), bet=d["ln_b"].partition_broadcast(P), wr=d["wr"],
                     rb=d["rb"].partition_broadcast(P), w1=d["w1"], b1=d["b1"], w2=d["w2"], b2=d["b2"], spread=d["spread"],
                     eyeb=d["eyeb"])
    return keep, from_dram


def bass_vision_mamba_moe(nc, x, eye, win, wx, gavg, conv_p, pick, wdt, par, wout, ln_g, ln_b, wr, rb, w1, b1, w2, b2, spread, eyeb, out):
    def scratch(name, shape, dt=F32):
        return nc.dram_tensor("scratch_" + name, shape, dt, kind="Internal").ap()

    bc = scratch("bc", (PAIRS, 2, 2 * 2, PIECES * PR, L), BF16)
    dts = scratch("dts", (PAIRS, 2, 2, 2 * PR, L))
    u = scratch("u", (PAIRS, 2, KIND, P, L))
    d = dict(
        x=x.rearrange("b h w c -> b (h w) c"), eye=eye, win=win, wx=wx, gavg=gavg, conv_p=conv_p, pick=pick, wdt=wdt,
        par=par, wout=wout, ln_g=ln_g, ln_b=ln_b, wr=wr, rb=rb, w1=w1, b1=b1, w2=w2, b2=b2, spread=spread, eyeb=eyeb,
        out=out.rearrange("b h w c -> b (h w) c"),
        xt=scratch("xt", (BATCH, NC, P, L)), sz=scratch("sz", (PAIRS, P, TT, 2 * DI)),
        bc=bc, dts=dts, u=u, y_flat=scratch("y", (GROUPS, P, L)),
        bc_flat=bc.rearrange("a o m r l -> (a o m) r l"), dts_flat=dts.rearrange("a o s r l -> (a o s) r l"),
        u_flat=u.rearrange("a o t p l -> (a o t) p l"),
    )
    with ExitStack() as ctx:
        keep, keep_from = kept(nc, ctx, d)

        def sem(name):
            return ctx.enter_context(nc.semaphore(name))

        shared = dict(
            kept_in=sem("kept_in"),
            dt_loads=[sem(f"dt_loads{i}") for i in range(2)],
            loads=[sem(f"loads{i}") for i in range(2)],
            y_stored=sem("y_stored"), y0_in=sem("y0_in"), y1_in=sem("y1_in"),
            sum_ready=sem("sum_ready"),
        )
        head(nc, d, keep, keep_from, shared)

        def sb(name, shape):
            return ctx.enter_context(nc.sbuf_tensor("y_" + name, shape, F32))

        ys = dict(y0=sb("y0", [P, KIND, L]), y1=sb("y1", [P, KIND, L]), yout=sb("yout", [P, L]))
        scan(nc, d, keep, ys, shared)
        tail(nc, d, keep, ys, shared)


def lay_out(np, a):
    f = np.float32
    kinds = [(0, 0, P), (1, 0, P), (2, 0, 0)]
    o = {}
    o["eye"] = np.eye(P, dtype=f)
    chunk = lambda w: np.ascontiguousarray(w.reshape(NC, P, -1).transpose(1, 0, 2))
    o["win"] = chunk(a["L0_conv_in_proj_w"].T)

    def by_kind(w):
        w = np.moveaxis(w, -1, 0)
        return np.stack([w[0:P], w[0:P], np.concatenate([w[P:], w[P:]])])

    wx = np.zeros((2, 2, P, P), f)
    xw = a["L0_conv_x_proj_w"].transpose(0, 2, 1)
    for r in range(2):
        w = xw[2 * r:2 * r + 2]
        wx[:, 0, :, r * PR:(r + 1) * PR] = w[:, 0:P, R:]
        wx[:, 0, :, (2 + r) * PR:(2 + r) * PR + R] = w[:, 0:P, 0:R]
        for rows in (slice(0, HALF), slice(HALF, P)):
            wx[:, 1, rows, r * PR:(r + 1) * PR] = w[:, P:, R:]
            wx[:, 1, rows, (2 + r) * PR:(2 + r) * PR + R] = w[:, P:, 0:R]
    o["wx"] = np.ascontiguousarray(wx.reshape(4, P, P).transpose(1, 0, 2))
    ch = np.arange(C) // (C // 32)
    g = (ch[:, None] == ch[None, :]).astype(f) / f(C // 32)
    o["gavg"] = np.ascontiguousarray(g.reshape(NC, P, NC, P).transpose(1, 0, 2, 3).reshape(P, NC * NC, P))
    cp = np.concatenate([by_kind(a["L0_conv_conv_w"].reshape(DI, 9).T), by_kind(a["L0_conv_conv_b"][None])], -1)
    o["conv_p"] = np.ascontiguousarray(cp.transpose(1, 0, 2))
    pick = np.zeros((KIND, PIECES, 2, N, N, P), f)
    for kind in range(KIND):
        for b in range(2):
            cols = slice(0, P) if kind == b else slice(b * HALF, (b + 1) * HALF) if kind == 2 else slice(0, 0)
            for n in range(N):
                pick[kind, :, b, n, n, cols] = 1
    o["pick"] = pick.reshape(KIND, PIECES * PR, N * P).astype(np.dtype("bfloat16"))
    wdt = np.zeros((DIRS, KIND, 2 * PR, P), f)
    dw = a["L0_conv_dt_projs_w"].transpose(0, 2, 1)
    wdt[:, 0, 0:R] = dw[:, :, 0:P]
    wdt[:, 1, PR:PR + R] = dw[:, :, 0:P]
    wdt[:, 2, 0:R, 0:HALF] = dw[:, :, P:]
    wdt[:, 2, PR:PR + R, HALF:] = dw[:, :, P:]
    o["wdt"] = wdt.reshape(DIRS * KIND, 2 * PR, P)
    par = np.zeros((DIRS, KIND, P, N + 3), f)
    logs = a["L0_conv_A_logs"].reshape(DIRS, DI, N)
    skips = a["L0_conv_Ds"].reshape(DIRS, DI)
    for k in range(DIRS):
        par[k, :, :, 0:N] = by_kind(logs[k].T)
        par[k, :, :, N] = by_kind(a["L0_conv_dt_projs_b"][k])
        par[k, :, :, N + 1] = by_kind(skips[k % 2])
        par[k, :, :, N + 2] = by_kind(skips[k % 2 + 2])
    o["par"] = par.reshape(DIRS * KIND, P, N + 3)
    wo = a["L0_conv_out_proj_w"].T
    o["wout"] = np.ascontiguousarray(np.stack([wo[0:P], np.concatenate([wo[P:], wo[P:]])], 1))
    o["ln_g"], o["ln_b"] = a["L0_conv_out_norm_g"], a["L0_conv_out_norm_b"]
    o["wr"] = chunk(a["L1_conv_router_w"].T)
    o["rb"] = a["L1_conv_router_b"]
    o["w1"] = chunk(a["L1_conv_fc1_w"].reshape(C, C).T)
    o["b1"] = np.ascontiguousarray(a["L1_conv_fc1_b"].reshape(NC, P).T)
    o["w2"] = chunk(a["L1_conv_fc2_w"].transpose(0, 2, 1).reshape(C, C))
    b2 = np.zeros((PIECES, PR, C), f)
    b2[:, 0:PIECES * EXPERTS] = np.tile(a["L1_conv_fc2_b"], (PIECES, 1))
    o["b2"] = b2.reshape(PIECES * PR, C)
    e = np.arange(C) // HID
    spread = np.zeros((PR, C), f)
    spread[0:PIECES * EXPERTS] = np.tile(np.arange(EXPERTS)[:, None] == e[None, :], (PIECES, 1))
    o["spread"] = spread.astype(np.dtype("bfloat16"))
    o["eyeb"] = o["eye"].astype(np.dtype("bfloat16"))
    return o


_INS = ["x", "eye", "win", "wx", "gavg", "conv_p", "pick", "wdt", "par", "wout", "ln_g", "ln_b", "wr", "rb", "w1", "b1", "w2",
        "b2", "spread", "eyeb"]


def kernel(**inputs):
    import numpy as _np
    import concourse.bacc as _bacc
    from concourse import mybir as _mybir
    from concourse.bass_utils import run_bass_kernel_spmd as _run

    nc = _bacc.Bacc("TRN2", target_bir_lowering=False, num_devices=1)
    given = {k: _np.asarray(v) for k, v in inputs.items()}
    laid = lay_out(_np, given)
    laid["x"] = given["x"]
    arrays, args = {}, []
    for name in _INS:
        a = _np.ascontiguousarray(laid[name])
        arrays[f"in_{name}_dram"] = a
        args.append(nc.dram_tensor(f"in_{name}_dram", a.shape, _mybir.dt.from_np(a.dtype), kind="ExternalInput").ap())
    args.append(nc.dram_tensor("out_0_dram", (BATCH, HW, HW, C), F32, kind="ExternalOutput").ap())
    bass_vision_mamba_moe(nc, *args)
    r = _run(nc, [arrays], core_ids=[0])
    return r.results[0]["out_0_dram"]
```
